# Optimizing a Trainium2 kernel written in Bass

```python
import numpy as np
import jax
import jax.numpy as jnp

def _softmax(x, axis=-1):
    return jax.nn.softmax(x, axis=axis)

def _gelu(x):
    return jax.nn.gelu(x, approximate=True)

def _silu(x):
    return jax.nn.silu(x)

def _sigmoid(x):
    return jax.nn.sigmoid(x)

def _layernorm(x, axis=-1, eps=1e-05):
    m = jnp.mean(x, axis=axis, keepdims=True)
    v = jnp.var(x, axis=axis, keepdims=True)
    return (x - m) / jnp.sqrt(v + eps)

def _scatter_add(tgt, idx, src, axis=0):
    return tgt.at[idx].add(src)

def _segment_sum(src, seg, n):
    return jax.ops.segment_sum(src, seg, n)
kernel_name = 'mk_sandwich_d1_jaxref_r4_f94bd4'

def setup_inputs(seed: int=0):
    np.random.seed(seed)
    _w = jnp.asarray

    def _L0_attn_setup():
        import jax, jax.numpy as jnp
        import numpy as np
        from jax.scipy.linalg import solve_triangular
        B, L, D, H = (1, 512, 256, 4)
        DK = DV = D // H
        CONV = 4
        FIR_S, FIR_M, FIR_L = (3, 15, 63)
        CHUNK = 32

        def _l2norm(x):
            return x * jax.lax.rsqrt(jnp.sum(x * x, -1, keepdims=True) + 1e-06)

        def _short_conv(x, w):
            K = w.shape[-1]
            l = x.shape[1]
            xp = jnp.pad(x, ((0, 0), (K - 1, 0), (0, 0)))
            y = sum((xp[:, j:j + l, :] * w[:, j] for j in range(K)))
            return jax.nn.silu(y)

        def _fir(x, filt):
            b, l, h, d = x.shape
            K = filt.shape[-1]
            xf = jnp.transpose(x.reshape(b, l, h * d), (0, 2, 1))
            y = jax.lax.conv_general_dilated(xf, filt.reshape(h * d, 1, K), (1,), [(K - 1, 0)], feature_group_count=h * d)
            return jnp.transpose(y, (0, 2, 1)).reshape(b, l, h, d)

        def _delta_rule_chunkwise(q, k, v, beta):
            b, h, Lq, dk = q.shape
            c = CHUNK
            n = Lq // c
            q = _l2norm(q)
            k = _l2norm(k)
            v = v * beta[..., None]
            kb = k * beta[..., None]
            rs = lambda t: t.reshape(b, h, n, c, t.shape[-1])
            qc, kc, vc, kbc = (rs(q), rs(k), rs(v), rs(kb))
            tri_strict = jnp.tril(jnp.ones((c, c), bool), -1)
            A = jnp.where(tri_strict, -(kbc @ jnp.swapaxes(kc, -1, -2)), 0.0)
            eye = jnp.eye(c, dtype=q.dtype)
            M = eye - A
            T = solve_triangular(M, jnp.broadcast_to(eye, M.shape), lower=True)
            u = T @ vc
            w = T @ kbc
            causal = jnp.tril(jnp.ones((c, c), bool))

            def step(S, inp):
                q_i, k_i, u_i, w_i = inp
                attn = jnp.where(causal, q_i @ jnp.swapaxes(k_i, -1, -2), 0.0)
                u_adj = u_i - w_i @ S
                o_i = q_i @ S + attn @ u_adj
                return (S + jnp.swapaxes(k_i, -1, -2) @ u_adj, o_i)
            S0 = jnp.zeros((b, h, dk, v.shape[-1]), q.dtype)
            mv = lambda t: jnp.moveaxis(t, 2, 0)
            _, o = jax.lax.scan(step, S0, (mv(qc), mv(kc), mv(u), mv(w)))
            return jnp.moveaxis(o, 0, 2).reshape(b, h, Lq, -1)

        def _rmsnorm(x, w, eps=1e-05):
            return x * jax.lax.rsqrt(jnp.mean(x * x, -1, keepdims=True) + eps) * w
        key = jax.random.key(seed)
        ks = jax.random.split(key, 16)
        wn = lambda k, shape, s: jax.random.normal(k, shape, jnp.float32) * s

        def fir_init(k, K):
            f = jnp.zeros((H, DV, K), jnp.float32).at[..., -1].set(1.0)
            return f + wn(k, (H, DV, K), 0.01)
        return {'hidden_states': jax.random.normal(ks[0], (B, L, D), jnp.float32), 'Wq': wn(ks[1], (D, D), 0.02), 'Wk': wn(ks[2], (D, D), 0.02), 'Wv': wn(ks[3], (D, D), 0.02), 'Wb': wn(ks[4], (H, D), 0.02), 'conv_q': wn(ks[5], (D, CONV), 0.1), 'conv_k': wn(ks[6], (D, CONV), 0.1), 'conv_v': wn(ks[7], (D, CONV), 0.1), 'fir_s': fir_init(ks[8], FIR_S), 'fir_m': fir_init(ks[9], FIR_M), 'fir_l': fir_init(ks[10], FIR_L), 'gate_w': wn(ks[11], (H, 5, D), 1.0 / np.sqrt(D)), 'gate_b': jnp.zeros((H, 5), jnp.float32), 'log_temp': jnp.zeros((H, 1), jnp.float32), 'eps_param': jnp.full((H, 1), 0.02, jnp.float32), 'norm_w': jnp.ones((DV,), jnp.float32), 'Wo': wn(ks[12], (D, D), 0.02)}
    _L0_attn_in = _L0_attn_setup()

    def _L0_ffn_setup():
        import jax, jax.numpy as jnp
        import numpy as np
        DIM = 256

        def _reference_tuple_inner(x, W_r, W_k, W_v, mu_r, mu_k):
            B, T, C = x.shape
            x_prev = jnp.concatenate([jnp.zeros((B, 1, C), x.dtype), x[:, :-1, :]], axis=1)
            xr = mu_r * x + (1.0 - mu_r) * x_prev
            xk = mu_k * x + (1.0 - mu_k) * x_prev
            r = jax.nn.sigmoid(jnp.einsum('btc,dc->btd', xr, W_r))
            k = jnp.einsum('btc,dc->btd', xk, W_k)
            k_act = jnp.square(jax.nn.relu(k))
            out = r * jnp.einsum('btc,dc->btd', k_act, W_v)
            new_state = x[:, -1, :]
            return (out, new_state)
        key = jax.random.key(seed)
        ks = jax.random.split(key, 6)
        B, T, C = (8, 512, DIM)
        x = jax.random.normal(ks[0], (B, T, C), dtype=jnp.float32)
        s = 1.0 / np.sqrt(C)
        W_r = jax.random.uniform(ks[1], (C, C), jnp.float32, -s, s)
        W_k = jax.random.uniform(ks[2], (C, C), jnp.float32, -s, s)
        W_v = jax.random.uniform(ks[3], (C, C), jnp.float32, -s, s)
        mu_r = jax.random.uniform(ks[4], (C,), jnp.float32)
        mu_k = jax.random.uniform(ks[5], (C,), jnp.float32)
        return {'x': x, 'W_r': W_r, 'W_k': W_k, 'W_v': W_v, 'mu_r': mu_r, 'mu_k': mu_k}
    _L0_ffn_in = _L0_ffn_setup()
    _d = {'L0_attn_hidden_states': _L0_attn_in['hidden_states'], 'L0_attn_Wq': _L0_attn_in['Wq'], 'L0_attn_Wk': _L0_attn_in['Wk'], 'L0_attn_Wv': _L0_attn_in['Wv'], 'L0_attn_Wb': _L0_attn_in['Wb'], 'L0_attn_conv_q': _L0_attn_in['conv_q'], 'L0_attn_conv_k': _L0_attn_in['conv_k'], 'L0_attn_conv_v': _L0_attn_in['conv_v'], 'L0_attn_fir_s': _L0_attn_in['fir_s'], 'L0_attn_fir_m': _L0_attn_in['fir_m'], 'L0_attn_fir_l': _L0_attn_in['fir_l'], 'L0_attn_gate_w': _L0_attn_in['gate_w'], 'L0_attn_gate_b': _L0_attn_in['gate_b'], 'L0_attn_log_temp': _L0_attn_in['log_temp'], 'L0_attn_eps_param': _L0_attn_in['eps_param'], 'L0_attn_norm_w': _L0_attn_in['norm_w'], 'L0_attn_Wo': _L0_attn_in['Wo'], 'L0_ffn_W_r': _L0_ffn_in['W_r'], 'L0_ffn_W_k': _L0_ffn_in['W_k'], 'L0_ffn_W_v': _L0_ffn_in['W_v'], 'L0_ffn_mu_r': _L0_ffn_in['mu_r'], 'L0_ffn_mu_k': _L0_ffn_in['mu_k']}
    _x0 = _d['L0_attn_hidden_states']
    _d['L0_attn_hidden_states'] = jax.random.normal(jax.random.fold_in(jax.random.key(seed), 1), (4, 1024, 256), dtype=_x0.dtype)
    del _x0
    return _d

def reference(L0_attn_hidden_states, L0_attn_Wq, L0_attn_Wk, L0_attn_Wv, L0_attn_Wb, L0_attn_conv_q, L0_attn_conv_k, L0_attn_conv_v, L0_attn_fir_s, L0_attn_fir_m, L0_attn_fir_l, L0_attn_gate_w, L0_attn_gate_b, L0_attn_log_temp, L0_attn_eps_param, L0_attn_norm_w, L0_attn_Wo, L0_ffn_W_r, L0_ffn_W_k, L0_ffn_W_v, L0_ffn_mu_r, L0_ffn_mu_k):

    def _L0_attn_ref(hidden_states, Wq, Wk, Wv, Wb, conv_q, conv_k, conv_v, fir_s, fir_m, fir_l, gate_w, gate_b, log_temp, eps_param, norm_w, Wo):
        import jax, jax.numpy as jnp
        import numpy as np
        from jax.scipy.linalg import solve_triangular
        B, L, D, H = (1, 512, 256, 4)
        DK = DV = D // H
        CONV = 4
        FIR_S, FIR_M, FIR_L = (3, 15, 63)
        CHUNK = 32

        def _l2norm(x):
            return x * jax.lax.rsqrt(jnp.sum(x * x, -1, keepdims=True) + 1e-06)

        def _short_conv(x, w):
            K = w.shape[-1]
            l = x.shape[1]
            xp = jnp.pad(x, ((0, 0), (K - 1, 0), (0, 0)))
            y = sum((xp[:, j:j + l, :] * w[:, j] for j in range(K)))
            return jax.nn.silu(y)

        def _fir(x, filt):
            b, l, h, d = x.shape
            K = filt.shape[-1]
            xf = jnp.transpose(x.reshape(b, l, h * d), (0, 2, 1))
            y = jax.lax.conv_general_dilated(xf, filt.reshape(h * d, 1, K), (1,), [(K - 1, 0)], feature_group_count=h * d)
            return jnp.transpose(y, (0, 2, 1)).reshape(b, l, h, d)

        def _delta_rule_chunkwise(q, k, v, beta):
            b, h, Lq, dk = q.shape
            c = CHUNK
            n = Lq // c
            q = _l2norm(q)
            k = _l2norm(k)
            v = v * beta[..., None]
            kb = k * beta[..., None]
            rs = lambda t: t.reshape(b, h, n, c, t.shape[-1])
            qc, kc, vc, kbc = (rs(q), rs(k), rs(v), rs(kb))
            tri_strict = jnp.tril(jnp.ones((c, c), bool), -1)
            A = jnp.where(tri_strict, -(kbc @ jnp.swapaxes(kc, -1, -2)), 0.0)
            eye = jnp.eye(c, dtype=q.dtype)
            M = eye - A
            T = solve_triangular(M, jnp.broadcast_to(eye, M.shape), lower=True)
            u = T @ vc
            w = T @ kbc
            causal = jnp.tril(jnp.ones((c, c), bool))

            def step(S, inp):
                q_i, k_i, u_i, w_i = inp
                attn = jnp.where(causal, q_i @ jnp.swapaxes(k_i, -1, -2), 0.0)
                u_adj = u_i - w_i @ S
                o_i = q_i @ S + attn @ u_adj
                return (S + jnp.swapaxes(k_i, -1, -2) @ u_adj, o_i)
            S0 = jnp.zeros((b, h, dk, v.shape[-1]), q.dtype)
            mv = lambda t: jnp.moveaxis(t, 2, 0)
            _, o = jax.lax.scan(step, S0, (mv(qc), mv(kc), mv(u), mv(w)))
            return jnp.moveaxis(o, 0, 2).reshape(b, h, Lq, -1)

        def _rmsnorm(x, w, eps=1e-05):
            return x * jax.lax.rsqrt(jnp.mean(x * x, -1, keepdims=True) + eps) * w
        b, l, d = hidden_states.shape
        q = _short_conv(hidden_states @ Wq.T, conv_q).reshape(b, l, H, DK)
        k = _short_conv(hidden_states @ Wk.T, conv_k).reshape(b, l, H, DK)
        v_direct = _short_conv(hidden_states @ Wv.T, conv_v).reshape(b, l, H, DV)
        beta = jax.nn.sigmoid(hidden_states @ Wb.T)
        tp = lambda t: jnp.transpose(t, (0, 2, 1, 3))
        delta_out = tp(_delta_rule_chunkwise(tp(q), tp(k), tp(v_direct), jnp.transpose(beta, (0, 2, 1))))
        local_s = _fir(v_direct, fir_s)
        local_m = _fir(v_direct, fir_m)
        local_l = _fir(v_direct, fir_l)
        logits = jnp.einsum('bld,hpd->blhp', hidden_states, gate_w) + gate_b
        temp = jnp.exp(log_temp).reshape(1, 1, H, 1)
        probs = jax.nn.softmax(logits / temp, -1)
        eps = jnp.clip(eps_param, 0.0, 0.2).reshape(1, 1, H, 1)
        probs = probs * (1.0 - 5.0 * eps) + eps
        o = probs[..., 0:1] * local_s + probs[..., 1:2] * local_m + probs[..., 2:3] * local_l + probs[..., 3:4] * delta_out + probs[..., 4:5] * v_direct
        o = _rmsnorm(o, norm_w)
        return o.reshape(b, l, H * DV) @ Wo.T

    def _L0_ffn_ref(x, W_r, W_k, W_v, mu_r, mu_k):
        import jax, jax.numpy as jnp
        import numpy as np
        DIM = 256

        def _reference_tuple_inner(x, W_r, W_k, W_v, mu_r, mu_k):
            B, T, C = x.shape
            x_prev = jnp.concatenate([jnp.zeros((B, 1, C), x.dtype), x[:, :-1, :]], axis=1)
            xr = mu_r * x + (1.0 - mu_r) * x_prev
            xk = mu_k * x + (1.0 - mu_k) * x_prev
            r = jax.nn.sigmoid(jnp.einsum('btc,dc->btd', xr, W_r))
            k = jnp.einsum('btc,dc->btd', xk, W_k)
            k_act = jnp.square(jax.nn.relu(k))
            out = r * jnp.einsum('btc,dc->btd', k_act, W_v)
            new_state = x[:, -1, :]
            return (out, new_state)
        return _reference_tuple_inner(x, W_r, W_k, W_v, mu_r, mu_k)[0]
    x = L0_attn_hidden_states
    x = x + _layernorm(_L0_attn_ref(_layernorm(x, axis=-1), L0_attn_Wq, L0_attn_Wk, L0_attn_Wv, L0_attn_Wb, L0_attn_conv_q, L0_attn_conv_k, L0_attn_conv_v, L0_attn_fir_s, L0_attn_fir_m, L0_attn_fir_l, L0_attn_gate_w, L0_attn_gate_b, L0_attn_log_temp, L0_attn_eps_param, L0_attn_norm_w, L0_attn_Wo), axis=-1)
    x = x + _layernorm(_L0_ffn_ref(_layernorm(x, axis=-1), L0_ffn_W_r, L0_ffn_W_k, L0_ffn_W_v, L0_ffn_mu_r, L0_ffn_mu_k), axis=-1)
    return x

_drawn_inputs = setup_inputs


def setup_inputs(seed=0):
    import zlib

    import numpy as np

    out = dict(_drawn_inputs(seed))
    spreads = {'L0_attn_gate_b': (0.0, 0.301),
     'L0_attn_log_temp': (0.0, 0.545),
     'L0_attn_eps_param': (0.019999999552965164, 0.6),
     'L0_attn_norm_w': (1.0, 0.2)}
    factors = {}
    for name, (base, spread) in spreads.items():
        noise = np.random.default_rng([zlib.crc32(name.encode()), seed]).standard_normal(out[name].shape)
        drawn = base * np.exp(spread * noise) if base else spread * noise
        out[name] = jnp.asarray(drawn.astype(out[name].dtype))
    for name, factor in factors.items():
        out[name] = (out[name] * factor).astype(out[name].dtype)
    return out
```

```python
from contextlib import ExitStack

import concourse.bass as bass
from concourse import mybir

F32 = mybir.dt.float32
ALU = mybir.AluOpType
ACT = mybir.ActivationFunctionType
AX = mybir.AxisListType.X

P = 128
B, L, D, H = 4, 1024, 256, 4
DK = D // H
C = 64
N = L // C
HALVES = D // P
PAIRS = H // 2
U = PAIRS * B
G4 = B
BLK = B * N
TAPS = 4
PAD = TAPS - 1
LP = L + PAD
NG = 6
MS0 = 48
ROWS = 2 * P - C
LEVELS = (2, 4, 8, 16, 32)
NL = len(LEVELS)
GC = 64
FG = D // GC
EPS, L2EPS = 1e-5, 1e-6
G_SHIFTED, G_STEPS = 5, 11

C_ID, C_R, C_LOW, C_UP, C_NM1, C_LV, C_HS = 0, 128, 192, 256, 320, 384, 384 + 64 * NL
NCONST = C_HS + 2
NSMALL = 3 * HALVES * TAPS + 2 * HALVES + 1 + PAIRS * 5 + 2 * PAIRS


def build(nc, x, out, wgate, consts, smalls, wq, wk, wv, wo, wr, wfk, wfv, fl, fms):
    ctx = ExitStack()
    with ctx:
        def sb(name, shape):
            return ctx.enter_context(nc.sbuf_tensor(name, shape, F32))

        def sem(name):
            return ctx.enter_context(nc.semaphore(name))

        xnT_dram = nc.dram_tensor("xnT_scratch", (P, HALVES, B, LP), F32, kind="Internal").ap()
        v_dram = nc.dram_tensor("v_scratch", (N, P, U, DK), F32, kind="Internal").ap()

        cst = sb("cst", [P, NCONST])
        ident = cst[:, C_ID:C_ID + P]
        rstack = cst[:, C_R:C_R + C]
        low = cst[:, C_LOW:C_LOW + C]
        up = cst[:, C_UP:C_UP + C]
        negpairs = cst[:, C_NM1:C_NM1 + C]
        headsel = cst[:, C_HS:C_HS + 2]

        def level_mask(l):
            return cst[:, C_LV + C * l:C_LV + C * (l + 1)]

        w = {k: sb("w_" + k, [P, HALVES, D]) for k in ("q", "k", "v", "o", "r", "fk", "fv")}
        w_gate = sb("w_gate", [P, HALVES, H * NG])
        small = sb("small", [P, NSMALL])
        conv_w = small[:, 0:24].rearrange("p (i h k) -> p i h k", i=3, h=HALVES)
        mu = small[:, 24:28].rearrange("p (i h) -> p i h", i=2)
        norm_w = small[:, 28:29]
        gb = small[:, 29:39].rearrange("p (r g) -> p r g", r=PAIRS)
        inv_temp = small[:, 39:41]
        mix_eps = small[:, 41:43]
        neg_half = sb("neg_half", [P, 16])
        mix_scale = sb("mix_scale", [P, PAIRS])

        gates = sb("gates", [P, NG, PAIRS, BLK])
        gmax = sb("gmax", [P, PAIRS, BLK])
        fir = sb("fir", [P, DK, PAIRS, BLK])

        A_V = BLK * D
        A_T = 3 * C * GC
        arena = sb("arena", [P, A_V + A_T])
        vwin = arena[:, 0:A_V].rearrange("p (c w) -> p c w", w=BLK)
        toep_l = arena[:, A_V:A_V + C * GC].rearrange("p (t c) -> p t c", c=GC)
        toep_ms = arena[:, A_V + C * GC:A_V + A_T].rearrange("p (f t c) -> p f t c", f=2, c=GC)

        def carve(whole, at, *shape):
            n = 1
            for k in shape:
                n *= k
            view = whole[:, at[0]:at[0] + n]
            at[0] += n
            if len(shape) == 2:
                return view.rearrange("p (a b) -> p a b", b=shape[1])
            if len(shape) == 3:
                return view.rearrange("p (a b c) -> p a b c", b=shape[1], c=shape[2])
            return view

        M_TILES = L // P
        SA = 2 * M_TILES * D + HALVES * LP + HALVES * (C + L) + N * PAIRS * DK
        seq = sb("seq", [P, SA])
        sa = [0]
        xa = carve(seq, sa, M_TILES, D)
        xna = carve(seq, sa, M_TILES, D)
        xnT = carve(seq, sa, HALVES, LP)
        vT = carve(seq, sa, HALVES, C + L)
        vb = carve(seq, sa, N, PAIRS, DK)
        sc = [0]
        kT_bd, qT_bd, k_bd, atT_bd, M_bd, X_bd, Z_bd, wT_bd, o_bd = (carve(seq, sc, U, P) for _ in range(9))
        bd_all = seq[:, 0:sc[0]]
        fprod = carve(seq, sc, 2, 512)

        stats_a = sb("stats_a", [P, M_TILES, 6])
        mv_a = sb("mv_a", [P, M_TILES, 2])
        ve_a = sb("ve_a", [P, M_TILES])
        rs_a = sb("rs_a", [P, M_TILES])
        cva = sb("cva", [P, 2, 256])
        ac = [0]

        def take(*shape):
            return carve(arena, ac, *shape)

        xwin, v_c, cv, kq, sq = take(HALVES, B, C + PAD), take(U, DK), take(4, B, C), take(U, 2, C), take(2 * U, 2, C)
        Mt, Mc, X2, Z, Zs, Pm = (take(U, C) for _ in range(6))
        vp, S, ut, ov, o1, o2, osq, oT = (take(U, DK) for _ in range(8))
        x_in, t1, x1, xn2, th, f2, t3, y_out = (take(2, D) for _ in range(8))
        xf = take(HALVES, B, C + 1)
        dx, xr, xk, rl, ka = (take(HALVES, B * C) for _ in range(5))
        ssel, rk = take(2, U), take(2, U)
        bv, d2, qs, oms, ro = (take(1, U) for _ in range(5))
        bn, mv, ve, rs = take(3, 2, 6), take(3, 2, 2), take(3, 2), take(3, 2)
        assert ac[0] <= A_V + A_T and sc[0] <= SA

        bank = [ctx.enter_context(nc.psum_tensor(f"bank{i}", [P, 512], F32)) for i in range(8)]

        s = {n: sem(n) for n in (
            "consts_in", "weights_in", "half_set", "pads_set",
            "xa_in", "a_stats", "a_rs", "a_normed", "a_xT", "a_xT_out", "a_xT_stored", "a_proj",
            "a_tap", "a_conv", "a_vT", "a_win", "a_win_out", "a_vb", "a_vb_stored", "a_gate",
            "a_gate_out",
            "g_step", "g_exp",
            "toep_zero", "toep_l_in", "toep_ms_in", "fir_mm", "fir_prod", "fir_sum",
            "bd_zero", "state_zero", "window_in", "v_in", "x_in", "proj", "tap", "conv", "silu", "square", "bd",
            "sumsq", "sumsq_out", "scal", "vp", "ov", "ktr", "kbd", "gram", "mt", "mc", "x2", "at",
            "mbd", "xbd0", "z", "mm1", "pm", "mm2", "xbd", "zs", "zbd", "wmm", "wbd",
            "umm", "ut", "state", "omm", "S", "o1", "o2", "osq", "oms", "ro", "obd", "oT_mm", "oT",
            "ymm", "st1", "r1", "t1", "x1", "st2", "r2", "xn2", "xT", "halo", "xf", "dx", "mix",
            "rmm", "kmm", "th", "rl", "ka", "vmm", "f2", "st3", "r3", "t3", "y_out", "stored")}

        block = ctx.enter_context(nc.Block())
        x4 = x.rearrange("b (n t) c -> b n t c", t=C)
        out4 = out.rearrange("b (n t) c -> b n t c", t=C)
        HH = [slice(0, 64), slice(64, 128)]
        N_W = 7 + 1 + 1

        def alone(eng):
            eng.nop(nofuse=True)

        def grp(g):
            return slice(G4 * g, G4 * g + G4)

        def units(ap, k=C):
            return ap.rearrange("p (u k) -> p u k", k=k)

        @block.sync
        def _(sp):
            xam = [x[b].rearrange("(m p) c -> p m c", p=P) for b in range(B)]
            sp.dma_start(xa, xam[0]).then_inc(s["xa_in"], 16)
            sp.dma_start(cst[:, :], consts).then_inc(s["consts_in"], 16)
            for key, src in (("v", wv), ("q", wq), ("k", wk), ("o", wo), ("r", wr), ("fk", wfk), ("fv", wfv)):
                sp.dma_start(w[key][:, :, :], src.rearrange("(h p) d -> p h d", p=P)).then_inc(s["weights_in"], 16)
            sp.dma_start(w_gate[:, :, :], wgate.rearrange("(h p) d -> p h d", p=P)).then_inc(s["weights_in"], 16)
            sp.dma_start(small[:, :], smalls).then_inc(s["weights_in"], 16)

            def load_l(g):
                sp.dma_start(toep_l, runs(fl[g], 0, P)).then_inc(s["toep_l_in"], 16)

            def load_ms(g):
                for i in range(2):
                    sp.dma_start(toep_ms[MS0:P, i], runs(fms[i, g], MS0, P - MS0)).then_inc(s["toep_ms_in"], 16)

            def runs(taps, first, rows):
                return bass.AP(taps.tensor, taps.offset + (first + C - 1) * GC, [[GC, rows], [-GC, C], [1, GC]])

            x_flat = x.rearrange("b (m p) c -> p b m c", p=P)
            v_dst = v_dram.rearrange("n p (r b) d -> p r b n d", b=B)
            sp.wait_ge(s["toep_zero"], 1)
            load_l(0)
            load_ms(0)

            def xT_store(b):
                sp.wait_ge(s["a_xT_out"], b * 4 + 4)
                alone(sp)
                sp.dma_start(xnT_dram[:, :, b, :], xnT).then_inc(s["a_xT_stored"], 16)

            def v_store(b):
                sp.wait_ge(s["a_vb"], b * 16 + 16)
                alone(sp)
                for pr in range(PAIRS):
                    sp.dma_start(v_dst[:, pr, b], vb[:, :, pr, :]).then_inc(s["a_vb_stored"], 16)

            def sequence(b):
                xT_store(b)
                sp.wait_ge(s["a_normed"], b * 8 + 8)
                alone(sp)
                sp.dma_start(xa, x_flat[:, b + 1]).then_inc(s["xa_in"], 16)
                v_store(b)

            sequence(0)
            with sp.Fori(1, B - 1) as b:
                sequence(b)
            xT_store(B - 1)
            v_store(B - 1)

            for g in range(1, FG):
                sp.wait_ge(s["fir_mm"], g * 12 - 8)
                load_l(g)
                sp.wait_ge(s["fir_mm"], g * 12)
                load_ms(g)

            def chunk_in(n):
                sp.wait_ge(s["proj"], n * 4)
                alone(sp)
                for hf in range(HALVES):
                    sp.dma_start(xwin[:, hf], xnT_dram[:, hf, :, bass.ds(n * C, C + PAD)]).then_inc(s["window_in"], 16)
                sp.wait_ge(s["vp"], n * 1)
                alone(sp)
                sp.wait_ge(s["ov"], n * 2)
                alone(sp)
                sp.dma_start(v_c, v_dram[n]).then_inc(s["v_in"], 16)

            def rows_in(n):
                sp.wait_ge(s["x1"], n * 1)
                alone(sp)
                for bb in range(2):
                    for j in range(2):
                        sp.dma_start(x_in[HH[bb], j, :], x4[2 * j + bb, n]).then_inc(s["x_in"], 16)

            def rows_out(n):
                sp.wait_ge(s["y_out"], n * 1 + 1)
                alone(sp)
                for bb in range(2):
                    for j in range(2):
                        sp.dma_start(out4[2 * j + bb, n], y_out[HH[bb], j, :]).then_inc(s["stored"], 16)

            sp.wait_ge(s["fir_mm"], 12 * FG)
            sp.wait_ge(s["a_xT_stored"], 16 * B)
            sp.wait_ge(s["a_vb_stored"], 32 * B)
            chunk_in(0)
            def chunk_step(n):
                rows_in(n)
                chunk_in(n + 1)
                rows_out(n)

            chunk_step(0)
            with sp.Fori(1, N - 1) as n:
                chunk_step(n)
            rows_in(N - 1)
            rows_out(N - 1)
            sp.wait_ge(s["stored"], 64 * N)

        @block.gpsimd
        def _(pool):
            pool.memset(neg_half[:, :], -0.5).then_inc(s["half_set"], 1)
            pool.memset(xnT[:, :, 0:PAD], 0.0).then_inc(s["pads_set"], 1)
            pool.memset(vT[:, :, 0:C], 0.0).then_inc(s["pads_set"], 1)
            pool.memset(arena[:, A_V:A_V + A_T], 0.0).then_inc(s["toep_zero"], 1)
            pool.wait_ge(s["half_set"], 1)
            def sequence(b):
                pool.wait_ge(s["a_stats"], b * 3 + 3)
                pool.tensor_tensor(rs_a[:, :], ve_a[:, :], neg_half[:, 0:M_TILES], ALU.pow).then_inc(s["a_rs"], 1)

            sequence(0)
            with pool.Fori(1, B) as b:
                sequence(b)

            pool.wait_ge(s["a_win"], 8 * B)
            pool.wait_ge(s["a_gate"], B)
            pool.wait_ge(s["a_xT_stored"], 16 * B)
            pool.wait_ge(s["a_vb_stored"], 32 * B)
            pool.memset(bd_all, 0.0).then_inc(s["bd_zero"], 1)

            for g in range(FG):
                for f in range(1, 3):
                    for j in range(4):
                        q = 8 * g + 4 * (f - 1) + j
                        acc = fir[:, 32 * (g % 2) + 8 * j:32 * (g % 2) + 8 * j + 8, g // 2, :]
                        pool.wait_ge(s["fir_prod"], 12 * g + 4 * f + j + 1)
                        if f == 2:
                            pool.wait_ge(s["fir_sum"], q - 3)
                        pool.tensor_tensor(acc, acc, fprod[:, q % 2, :].rearrange("p (c w) -> p c w", w=BLK),
                                           ALU.add).then_inc(s["fir_sum"], 1)

            pool.wait_ge(s["fir_mm"], 12 * FG)
            pool.wait_ge(s["fir_sum"], 8 * FG)
            pool.wait_ge(s["g_step"], G_STEPS)
            pool.wait_ge(s["bd_zero"], 1)
            pool.memset(S, 0.0).then_inc(s["S"], 1)
            pool.memset(xf, 0.0).then_inc(s["state_zero"], 1)
            pool.wait_ge(s["state_zero"], 1)

            def two(n, sem_name, dst, src, g):
                alone(pool)
                for hh in range(2):
                    pool.tensor_copy(dst[HH[hh], grp(g), HH[hh]], src[HH[hh], grp(g), :]).then_inc(s[sem_name], 1)

            def bd_qk(n):
                for t in range(4):
                    kind, g = t // 2, t % 2
                    pool.wait_ge(s["silu"], n * 4 + t + 1)
                    if kind == 0:
                        pool.wait_ge(s["gram"], n * 2)
                    else:
                        pool.wait_ge(s["omm"], n * 1)
                    two(n, "bd", (kT_bd, qT_bd)[kind], kq[:, :, kind, :], g)
                pool.wait_ge(s["bd"], n * 8 + 8)

            def scalars(n):
                pool.wait_ge(s["sumsq_out"], n * 2 + 2)
                pool.wait_ge(s["scal"], n * 4)
                pool.wait_ge(s["vp"], n * 1)
                pool.tensor_tensor(rk, ssel, neg_half[:, :].rearrange("p (a b) -> p a b", b=U), ALU.pow).then_inc(s["scal"], 1)
                pool.wait_ge(s["scal"], n * 4 + 1)
                beta = gates[:, 5, :, :].rearrange("p r (b n) -> p (r b) n", n=N)[:, :, bass.ds(n, 1)]
                p3 = gates[:, 3, :, :].rearrange("p r (b n) -> p (r b) n", n=N)[:, :, bass.ds(n, 1)]
                rr = rk.rearrange("p a (u o) -> p a u o", o=1)
                one = lambda t: t.rearrange("p a (u o) -> p (a u) o", o=1)
                pool.tensor_tensor(one(bv), beta, rr[:, 0], ALU.mult).then_inc(s["scal"], 1)
                pool.wait_ge(s["o1"], n * 1)
                pool.tensor_tensor(one(qs), p3, rr[:, 1], ALU.mult).then_inc(s["scal"], 1)
                pool.wait_ge(s["scal"], n * 4 + 2)
                pool.wait_ge(s["zs"], n * 2)
                pool.tensor_tensor(d2, bv, rk[:, 0:1], ALU.mult).then_inc(s["scal"], 1)

            def values(n):
                pool.wait_ge(s["v_in"], n * 16 + 16)
                pool.wait_ge(s["umm"], n * 1)
                pool.tensor_tensor(vp, v_c, bv.rearrange("p a (u o) -> p (a u) o", o=1).broadcast_to((P, U, DK)),
                                   ALU.mult).then_inc(s["vp"], 1)

            def direct(n):
                p4 = gates[:, 4, :, :].rearrange("p r (b n) -> p (r b) n", n=N)[:, :, bass.ds(n, 1)]
                local = fir[:, :, :, :].rearrange("p d r (b n) -> p (r b) d n", n=N)[:, :, :, bass.ds(n, 1)]
                pool.wait_ge(s["o2"], n * 1)
                pool.tensor_tensor(ov, v_c, p4.broadcast_to((P, U, DK)), ALU.mult).then_inc(s["ov"], 1)
                pool.wait_ge(s["ov"], n * 2 + 1)
                ov4 = ov.rearrange("p u (d o) -> p u d o", o=1)
                pool.tensor_tensor(ov4, ov4, local, ALU.add).then_inc(s["ov"], 1)

            def bd_m(n):
                for g in range(2):
                    pool.wait_ge(s["mc"], n * 2 + g + 1)
                    two(n, "mbd", M_bd, Mc, g)
                for g in range(2):
                    pool.wait_ge(s["x2"], n * 4 + 2 * g + 2)
                    two(n, "xbd0", X_bd, X2, g)
                pool.wait_ge(s["xbd0"], n * 4 + 4)

            def bd_z(n):
                pool.wait_ge(s["umm"], n * 1)
                for g in range(2):
                    pool.wait_ge(s["z"], n * 12 + 10 + g + 1)
                    two(n, "zbd", Z_bd, Z, g)
                pool.wait_ge(s["zbd"], n * 4 + 4)

            def power(n, src_sem, per, dst_sem, dst, src, k):
                pool.wait_ge(s[src_sem], n * per + per)
                pool.tensor_tensor(dst, src, neg_half[:, 0:k].rearrange("p (a b) -> p a b", a=1) if k == U
                                   else neg_half[:, 0:k], ALU.pow).then_inc(s[dst_sem], 1)

            def halo(n):
                pool.wait_ge(s["mix"], n * 4)
                pool.wait_ge(s["xf"], n * 2)
                alone(pool)
                pool.tensor_copy(xf[:, :, :, 0:1], xf[:, :, :, C:C + 1]).then_inc(s["halo"], 1)

            def first(n):
                bd_qk(n)
                scalars(n)
                pool.wait_ge(s["scal"], n * 4 + 4)
                bd_m(n)
                values(n)
                direct(n)
                pool.wait_ge(s["ov"], n * 2 + 2)
                bd_z(n)

            first(0)
            def chunk_step(n):
                bd_qk(n + 1)
                power(n, "oms", 2, "ro", ro, oms, U)
                scalars(n + 1)
                pool.wait_ge(s["scal"], n * 4 + 8)
                bd_m(n + 1)
                values(n + 1)
                direct(n + 1)
                power(n, "st1", 3, "r1", rs[:, 0], ve[:, 0], 2)
                halo(n)
                power(n, "st2", 3, "r2", rs[:, 1], ve[:, 1], 2)
                power(n, "st3", 3, "r3", rs[:, 2], ve[:, 2], 2)
                pool.wait_ge(s["r3"], n * 1 + 1)
                bd_z(n + 1)

            chunk_step(0)
            with pool.Fori(1, N - 1) as n:
                chunk_step(n)
            n = N - 1
            power(n, "oms", 2, "ro", ro, oms, U)
            power(n, "st1", 3, "r1", rs[:, 0], ve[:, 0], 2)
            halo(n)
            power(n, "st2", 3, "r2", rs[:, 1], ve[:, 1], 2)
            power(n, "st3", 3, "r3", rs[:, 2], ve[:, 2], 2)

        @block.scalar
        def _(act):
            act.wait_ge(s["weights_in"], 16 * N_W)
            act.wait_ge(s["pads_set"], 2)

            def a_xT_out(b, q):
                act.wait_ge(s["a_xT"], b * 4 + q + 1)
                if q == 0:
                    act.wait_ge(s["a_proj"], b * 8)
                    act.wait_ge(s["a_gate"], b * 1)
                    act.wait_ge(s["a_xT_stored"], b * 16)
                act.activation(xnT[:, :, PAD + 256 * q:PAD + 256 * q + 256],
                               bank[q % 2][:, :].rearrange("p (h t) -> p h t", h=HALVES), ACT.Copy).then_inc(s["a_xT_out"], 1)

            def a_tap(b, i):
                act.wait_ge(s["a_proj"], b * 8 + i + 1)
                act.wait_ge(s["a_vT"], b * 8 + (i - 1 if i >= 2 else 0))
                act.activation(cva[:, i % 2, :], bank[2 + i % 2][:, PAD:PAD + 256], ACT.Copy,
                               scale=conv_w[:, 2, i % 2, PAD:PAD + 1]).then_inc(s["a_tap"], 1)

            def a_silu(b, i):
                act.wait_ge(s["a_conv"], b * 24 + 3 * i + 3)
                act.wait_ge(s["a_win"], b * 8)
                act.activation(vT[:, i % 2, C + 256 * (i // 2):C + 256 * (i // 2) + 256], cva[:, i % 2, :],
                               ACT.Silu).then_inc(s["a_vT"], 1)

            def a_win_out(b, i):
                act.wait_ge(s["a_vb"], b * 16 + 2 * i + 2)
                act.activation(vwin[:, P * (i % 2):P * (i % 2) + P, bass.ds(b * N + 4 * (i // 2), 4)],
                               bank[4 + i % 2][:, :].rearrange("p (k c) -> p c k", k=4), ACT.Copy).then_inc(s["a_win_out"], 1)

            def sequence(b):
                a_xT_out(b, 0)
                a_xT_out(b, 1)
                for q in range(4):
                    a_tap(b, 2 * q)
                    a_tap(b, 2 * q + 1)
                    if q < 2:
                        a_xT_out(b, q + 2)
                    a_silu(b, 2 * q)
                    a_silu(b, 2 * q + 1)
                    if q >= 1:
                        a_win_out(b, 2 * q - 2)
                        a_win_out(b, 2 * q - 1)
                a_win_out(b, 6)
                a_win_out(b, 7)

            sequence(0)
            with act.Fori(1, B) as b:
                sequence(b)

            act.activation(inv_temp[:, :], inv_temp[:, :], ACT.Exp, scale=-1.0).then_inc(s["g_exp"], 1)
            act.wait_ge(s["a_gate_out"], 8 * B)
            act.activation(gates[:, 5], gates[:, 5], ACT.Tanh, scale=0.5).then_inc(s["g_exp"], 1)
            act.wait_ge(s["g_step"], G_SHIFTED)
            act.activation(gates[:, 0:5], gates[:, 0:5], ACT.Exp).then_inc(s["g_exp"], 1)

            act.wait_ge(s["fir_mm"], 12 * FG)
            act.wait_ge(s["bd_zero"], 1)

            def tap(n, t):
                act.wait_ge(s["proj"], n * 4 + t + 1)
                act.wait_ge(s["silu"], n * 4)
                act.activation(cv[:, t], bank[t % 2][:, 0:B * (C + PAD)].rearrange("p (b t) -> p b t", b=B)[:, :, PAD:],
                               ACT.Copy, scale=conv_w[:, 1 - t // 2, t % 2, PAD:PAD + 1]).then_inc(s["tap"], 1)

            def silu(n, t):
                kind, g = t // 2, t % 2
                act.wait_ge(s["conv"], n * 12 + 3 * t + 3)
                act.wait_ge(s["gram"], n * 2)
                act.wait_ge(s["bd"], n * 8)
                act.wait_ge(s["square"], n * 4)
                act.activation(kq[:, grp(g), kind, :], cv[:, t], ACT.Silu).then_inc(s["silu"], 1)

            def square(n, t):
                kind, g = t // 2, t % 2
                act.wait_ge(s["silu"], n * 4 + t + 1)
                act.wait_ge(s["sumsq"], n * 1)
                for twice in range(2):
                    last = act.activation(sq[:, U * kind + G4 * g:U * kind + G4 * g + G4, twice, :], kq[:, grp(g), kind, :],
                                          ACT.Square)
                last.then_inc(s["square"], 1)

            def kbd_out(n):
                act.wait_ge(s["state"], n * 1)
                for g in range(2):
                    act.wait_ge(s["ktr"], n * 2 + g + 1)
                    act.activation(k_bd[:, grp(g), :], units(bank[g][:, :], P), ACT.Copy).then_inc(s["kbd"], 1)

            def wbd_out(n):
                act.wait_ge(s["umm"], n * 1)
                for g in range(2):
                    act.wait_ge(s["wmm"], n * 2 + g + 1)
                    for hh in range(2):
                        act.activation(wT_bd[HH[hh], grp(g), HH[hh]], units(bank[2 + g][HH[hh], 0:256]), ACT.Copy,
                                       scale=-1.0).then_inc(s["wbd"], 1)

            def u_out(n):
                act.wait_ge(s["umm"], n * 1 + 1)
                act.activation(ut, units(bank[4][:, :]), ACT.Copy).then_inc(s["ut"], 1)

            def state_out(n):
                act.wait_ge(s["state"], n * 1 + 1)
                act.wait_ge(s["omm"], n * 1 + 1)
                act.activation(S, units(bank[7][:, :]), ACT.Copy).then_inc(s["S"], 1)

            def o_square(n):
                act.wait_ge(s["o2"], n * 1 + 1)
                act.activation(osq, o2, ACT.Square).then_inc(s["osq"], 1)

            def oT_out(n):
                act.wait_ge(s["oT_mm"], n * 1 + 1)
                act.activation(oT, units(bank[4][:, :]), ACT.Copy, scale=norm_w[:, 0:1]).then_inc(s["oT"], 1)

            def xf_out(n):
                act.wait_ge(s["xT"], n * 1 + 1)
                act.wait_ge(s["halo"], n * 1 + 1)
                for hf in range(HALVES):
                    act.activation(xf[:, hf, :, 1:], bank[4][:, 256 * hf:256 * hf + 256].rearrange("p (b t) -> p b t", b=B),
                                   ACT.Copy).then_inc(s["xf"], 1)

            def ffn_act(n):
                act.wait_ge(s["kmm"], n * 1 + 1)
                act.wait_ge(s["ka"], n * 1)
                act.activation(rl, bank[5][:, :].rearrange("p (h t) -> p h t", h=2), ACT.Relu).then_inc(s["rl"], 1)
                act.wait_ge(s["rl"], n * 1 + 1)
                act.activation(ka, rl, ACT.Square).then_inc(s["ka"], 1)
                act.wait_ge(s["rmm"], n * 1 + 1)
                act.activation(th, bank[6][:, :].rearrange("p (j c) -> p j c", j=2), ACT.Tanh, scale=0.5).then_inc(s["th"], 1)

            def qk(n, kind):
                for g in range(2):
                    tap(n, 2 * kind + g)
                for g in range(2):
                    silu(n, 2 * kind + g)
                for g in range(2):
                    square(n, 2 * kind + g)

            qk(0, 0)
            qk(0, 1)
            kbd_out(0)
            wbd_out(0)
            def chunk_step(n):
                u_out(n)
                for g in range(2):
                    tap(n + 1, g)
                state_out(n)
                for g in range(2):
                    silu(n + 1, g)
                for g in range(2):
                    square(n + 1, g)
                o_square(n)
                qk(n + 1, 1)
                kbd_out(n + 1)
                oT_out(n)
                xf_out(n)
                ffn_act(n)
                wbd_out(n + 1)

            chunk_step(0)
            with act.Fori(1, N - 1) as n:
                chunk_step(n)
            n = N - 1
            u_out(n)
            state_out(n)
            o_square(n)
            oT_out(n)
            xf_out(n)
            ffn_act(n)

        @block.vector
        def _(dve):
            dve.wait_ge(s["weights_in"], 16 * N_W)
            dve.wait_ge(s["consts_in"], 16)

            def a_norm(b):
                dve.wait_ge(s["xa_in"], b * 16 + 16)
                dve.wait_ge(s["a_normed"], b * 8)
                for m in range(M_TILES):
                    last = nc.vector.bn_stats(stats_a[:, m, :], xa[:, m, :])
                last.then_inc(s["a_stats"], 1)
                dve.wait_ge(s["a_stats"], b * 3 + 1)
                alone(dve)
                for m in range(M_TILES):
                    last = nc.vector.bn_aggr(mv_a[:, m, :], stats_a[:, m, :])
                last.then_inc(s["a_stats"], 1)
                dve.wait_ge(s["a_stats"], b * 3 + 2)
                nc.vector.tensor_scalar(ve_a[:, :].rearrange("p (m o) -> p m o", o=1), mv_a[:, :, 1:2], EPS, None,
                                        ALU.add).then_inc(s["a_stats"], 1)
                dve.wait_ge(s["a_rs"], b * 1 + 1)
                dve.wait_ge(s["a_xT"], b * 4)
                for m in range(M_TILES):
                    nc.vector.tensor_scalar(xna[:, m, :], xa[:, m, :], mv_a[:, m, 0:1], rs_a[:, m:m + 1],
                                            ALU.subtract, ALU.mult).then_inc(s["a_normed"], 1)

            def a_conv(b, i):
                for j in range(PAD):
                    if j == 0:
                        dve.wait_ge(s["a_tap"], b * 8 + i + 1)
                    else:
                        dve.wait_ge(s["a_conv"], b * 24 + 3 * i + j)
                    nc.vector.scalar_tensor_tensor(cva[:, i % 2, :], bank[2 + i % 2][:, j:j + 256],
                                                   conv_w[:, 2, i % 2, j:j + 1], cva[:, i % 2, :],
                                                   ALU.mult, ALU.add).then_inc(s["a_conv"], 1)

            def a_vb(b, i):
                q, pr = i // 2, i % 2
                dve.wait_ge(s["a_win"], b * 8 + i + 1)
                dve.wait_ge(s["a_vb_stored"], b * 32)
                for hh in range(2):
                    nc.vector.tensor_copy(vb[HH[hh], 4 * q:4 * q + 4, pr, :],
                                          units(bank[4 + pr][64:128, :], P)[:, :, HH[hh]]).then_inc(s["a_vb"], 1)

            def a_gates(b):
                dve.wait_ge(s["a_gate"], b * 1 + 1)
                dst = gates.rearrange("p g r (b m two) -> p b g r m two", b=B, two=2)
                for par in range(2):
                    src = bank[6][HH[par], 0:M_TILES * H * NG].rearrange("p (m h g) -> p h g m", h=H, g=NG)
                    for hh in range(2):
                        for pr in range(PAIRS):
                            nc.vector.tensor_copy(dst[HH[hh], b, :, pr, :, par], src[:, 2 * pr + hh]).then_inc(s["a_gate_out"], 1)

            def sequence(b):
                a_norm(b)
                for q in range(4):
                    a_conv(b, 2 * q)
                    a_conv(b, 2 * q + 1)
                    if q >= 1:
                        a_vb(b, 2 * q - 2)
                        a_vb(b, 2 * q - 1)
                a_vb(b, 6)
                a_vb(b, 7)
                a_gates(b)

            sequence(0)
            with dve.Fori(1, B) as b:
                sequence(b)

            steps = [0]

            def then(ins):
                steps[0] += 1
                ins.then_inc(s["g_step"], 1)
                dve.wait_ge(s["g_step"], steps[0])

            G5 = gates[:, 0:5]
            mx4 = gmax[:, :, :].rearrange("p r (w o) -> p o r w", o=1).broadcast_to((P, 5, PAIRS, BLK))
            dve.wait_ge(s["a_gate_out"], 8 * B)
            dve.wait_ge(s["g_exp"], 1)
            then(nc.vector.tensor_scalar(mix_eps[:, :], mix_eps[:, :], 0.0, 0.2, ALU.max, ALU.min))
            then(nc.vector.tensor_scalar(mix_scale[:, :], mix_eps[:, :], -5.0, 1.0, ALU.mult, ALU.add))
            for g in range(5):
                for pr in range(PAIRS):
                    last = nc.vector.tensor_scalar(gates[:, g, pr, :], gates[:, g, pr, :], gb[:, pr, g:g + 1],
                                                   inv_temp[:, pr:pr + 1], ALU.add, ALU.mult)
            then(last)
            then(nc.vector.tensor_reduce(gmax[:, :, :], G5.rearrange("p g r w -> p r w g"), AX, ALU.max))
            then(nc.vector.tensor_tensor(G5, G5, mx4, ALU.subtract))
            assert steps[0] == G_SHIFTED
            dve.wait_ge(s["g_exp"], 3)
            then(nc.vector.tensor_reduce(gmax[:, :, :], G5.rearrange("p g r w -> p r w g"), AX, ALU.add))
            then(nc.vector.reciprocal(gmax[:, :, :], gmax[:, :, :]))
            for pr in range(PAIRS):
                last = nc.vector.tensor_scalar(gmax[:, pr, :], gmax[:, pr, :], mix_scale[:, pr:pr + 1], None, ALU.mult)
            then(last)
            then(nc.vector.tensor_tensor(G5, G5, mx4, ALU.mult))
            for pr in range(PAIRS):
                last = nc.vector.tensor_scalar(G5[:, :, pr, :], G5[:, :, pr, :], mix_eps[:, pr:pr + 1], None, ALU.add)
            then(last)
            then(nc.vector.tensor_scalar(gates[:, 5], gates[:, 5], 0.5, 0.5, ALU.mult, ALU.add))
            assert steps[0] == G_STEPS

            dve.wait_ge(s["bd_zero"], 1)
            for g in range(FG):
                for f in range(3):
                    wt = gates[:, 2 - f, g // 2, :].rearrange("p (o w) -> p o w", o=1).broadcast_to((P, 8, BLK))
                    for j in range(4):
                        k = 12 * g + 4 * f + j
                        q = 8 * g + 4 * (f - 1) + j
                        dve.wait_ge(s["fir_mm"], k + 1)
                        if f == 0:
                            dst = fir[:, 32 * (g % 2) + 8 * j:32 * (g % 2) + 8 * j + 8, g // 2, :]
                        else:
                            dst = fprod[:, q % 2, :].rearrange("p (c w) -> p c w", w=BLK)
                            if q >= 2:
                                dve.wait_ge(s["fir_sum"], q - 1)
                        nc.vector.tensor_tensor(dst, bank[k % 8][:, :].rearrange("p (c w) -> p c w", w=BLK), wt,
                                                ALU.mult).then_inc(s["fir_prod"], 1)

            dve.wait_ge(s["fir_mm"], 12 * FG)
            dve.wait_ge(s["bd_zero"], 1)

            def over(ap, u=G4):
                return ap.rearrange("p (o k) -> p o k", o=1).broadcast_to((ap.shape[0], u, C))

            def per_row(ap, g=None):
                v = ap.rearrange("p a (u o) -> p (a u) o", o=1)
                return v.broadcast_to((P, U, C)) if g is None else v[:, grp(g)].broadcast_to((P, G4, C))

            def conv(n, t):
                ps = bank[t % 2][:, 0:B * (C + PAD)].rearrange("p (b t) -> p b t", b=B)
                for j in range(PAD):
                    if j == 0:
                        dve.wait_ge(s["tap"], n * 4 + t + 1)
                    else:
                        dve.wait_ge(s["conv"], n * 12 + 3 * t + j)
                    nc.vector.scalar_tensor_tensor(cv[:, t], ps[:, :, j:j + C], conv_w[:, 1 - t // 2, t % 2, j:j + 1],
                                                   cv[:, t], ALU.mult, ALU.add).then_inc(s["conv"], 1)

            def sumsq_out(n):
                dve.wait_ge(s["sumsq"], n * 1 + 1)
                src = bank[2][:, 0:4 * U].rearrange("p (a u h) -> p a u h", a=2, h=2)
                for hh in range(2):
                    nc.vector.tensor_scalar(ssel[HH[hh]].rearrange("p a (u o) -> p a u o", o=1),
                                            src[HH[hh], :, :, hh:hh + 1], L2EPS, None, ALU.add).then_inc(s["sumsq_out"], 1)

            def m_parts(n):
                for g in range(2):
                    dve.wait_ge(s["gram"], n * 2 + g + 1)
                    dve.wait_ge(s["mc"], n * 2)
                    nc.vector.tensor_tensor(Mt[:, grp(g)], units(bank[g][:, :], P)[:, :, 0:C], over(low), ALU.mult).then_inc(s["mt"], 1)
                for g in range(2):
                    dve.wait_ge(s["mt"], n * 2 + g + 1)
                    dve.wait_ge(s["scal"], n * 4 + 4)
                    dve.wait_ge(s["x2"], n * 4)
                    nc.vector.tensor_tensor(Mc[:, grp(g)], Mt[:, grp(g)], per_row(d2, g), ALU.mult).then_inc(s["mc"], 1)
                for g in range(2):
                    dve.wait_ge(s["mc"], n * 2 + g + 1)
                    dve.wait_ge(s["z"], n * 12)
                    nc.vector.tensor_tensor(X2[:, grp(g)], Mc[:, grp(g)], over(negpairs), ALU.mult).then_inc(s["x2"], 1)
                    dve.wait_ge(s["x2"], n * 4 + 2 * g + 1)
                    nc.vector.tensor_tensor(X2[:, grp(g)], X2[:, grp(g)], over(rstack), ALU.add).then_inc(s["x2"], 1)
                for g in range(2):
                    dve.wait_ge(s["x2"], n * 4 + 2 * g + 2)
                    dve.wait_ge(s["zs"], n * 2)
                    dve.wait_ge(s["zbd"], n * 4)
                    nc.vector.transpose(Z[:, grp(g)], X2[:, grp(g)]).then_inc(s["z"], 1)

            def at_parts(n):
                dve.wait_ge(s["omm"], n * 1)
                for g in range(2):
                    for hh in range(2):
                        nc.vector.tensor_tensor(atT_bd[HH[hh], grp(g), HH[hh]], units(bank[g][HH[hh], :], P)[:, :, C:P],
                                                over(up[HH[hh]]), ALU.mult).then_inc(s["at"], 1)

            def level(n, l):
                for g in range(2):
                    dve.wait_ge(s["mm1"], n * 2 * NL + 2 * l + g + 1)
                    nc.vector.tensor_tensor(Pm[:, grp(g)], units(bank[2 + g][:, 0:256]), over(level_mask(l)),
                                            ALU.mult).then_inc(s["pm"], 1)
                for g in range(2):
                    dve.wait_ge(s["mm2"], n * 2 * NL + 2 * l + g + 1)
                    nc.vector.tensor_tensor(Z[:, grp(g)], Z[:, grp(g)], units(bank[2 + g][:, 256:512]),
                                            ALU.subtract).then_inc(s["z"], 1)
                    if l < NL - 1:
                        dve.wait_ge(s["z"], n * 12 + 2 * (l + 1) + g + 1)
                        for hh in range(2):
                            nc.vector.transpose(X_bd[HH[hh], grp(g), HH[hh]], Z[HH[hh], grp(g)]).then_inc(s["xbd"], 1)

            def z_scaled(n):
                for g in range(2):
                    dve.wait_ge(s["z"], n * 12 + 10 + g + 1)
                    nc.vector.tensor_tensor(Zs[:, grp(g)], Z[:, grp(g)], per_row(d2, g), ALU.mult).then_inc(s["zs"], 1)

            def o_parts(n):
                dve.wait_ge(s["omm"], n * 1 + 1)
                dve.wait_ge(s["o2"], n * 1)
                nc.vector.tensor_tensor(o1, units(bank[5][:, :]), per_row(qs), ALU.mult).then_inc(s["o1"], 1)
                dve.wait_ge(s["o1"], n * 1 + 1)
                dve.wait_ge(s["ov"], n * 2 + 2)
                dve.wait_ge(s["obd"], n * 2)
                nc.vector.tensor_tensor(o2, o1, ov, ALU.add).then_inc(s["o2"], 1)

            def o_meansq(n):
                dve.wait_ge(s["osq"], n * 1 + 1)
                nc.vector.tensor_reduce(oms[:, 0], osq, AX, ALU.add).then_inc(s["oms"], 1)
                dve.wait_ge(s["oms"], n * 2 + 1)
                nc.vector.tensor_scalar(oms[:, 0], oms[:, 0], 1.0 / DK, EPS, ALU.mult, ALU.add).then_inc(s["oms"], 1)

            def o_normed(n):
                dve.wait_ge(s["ro"], n * 1 + 1)
                for hh in range(2):
                    nc.vector.tensor_tensor(o_bd[HH[hh], :, HH[hh]], o2[HH[hh]], per_row(ro)[HH[hh]], ALU.mult).then_inc(s["obd"], 1)

            def row_stats(n, i, name, src, eps, normed):
                dve.wait_ge(s[normed], n * 1)
                dve.wait_ge(s[name], n * 3)
                for j in range(2):
                    last = nc.vector.bn_stats(bn[:, i, j, :], src[:, j, :])
                last.then_inc(s[name], 1)
                dve.wait_ge(s[name], n * 3 + 1)
                alone(dve)
                for j in range(2):
                    last = nc.vector.bn_aggr(mv[:, i, j, :], bn[:, i, j, :])
                last.then_inc(s[name], 1)
                dve.wait_ge(s[name], n * 3 + 2)
                nc.vector.tensor_scalar(ve[:, i].rearrange("p (j o) -> p j o", o=1), mv[:, i, :, 1:2], eps, None,
                                        ALU.add).then_inc(s[name], 1)

            def row_norm(n, i, dst, src, name):
                for j in range(2):
                    last = nc.vector.tensor_scalar(dst[:, j, :], src[:, j, :], mv[:, i, j, 0:1], rs[:, i, j:j + 1],
                                                   ALU.subtract, ALU.mult)
                last.then_inc(s[name], 1)

            def y_stats(n):
                dve.wait_ge(s["ymm"], n * 1 + 1)
                row_stats(n, 0, "st1", bank[5][:, :].rearrange("p (j c) -> p j c", j=2), EPS, "t1")

            def residual(n):
                dve.wait_ge(s["r1"], n * 1 + 1)
                dve.wait_ge(s["x1"], n * 1)
                row_norm(n, 0, t1, bank[5][:, :].rearrange("p (j c) -> p j c", j=2), "t1")
                dve.wait_ge(s["t1"], n * 1 + 1)
                dve.wait_ge(s["x_in"], n * 64 + 64)
                dve.wait_ge(s["y_out"], n * 1)
                nc.vector.tensor_tensor(x1, t1, x_in, ALU.add).then_inc(s["x1"], 1)
                dve.wait_ge(s["x1"], n * 1 + 1)
                row_stats(n, 1, "st2", x1, EPS, "xn2")

            def x_normed(n):
                dve.wait_ge(s["r2"], n * 1 + 1)
                row_norm(n, 1, xn2, x1, "xn2")

            def mixes(n):
                dve.wait_ge(s["xf"], n * 2 + 2)
                dve.wait_ge(s["mix"], n * 4)
                for hf in range(HALVES):
                    nc.vector.tensor_tensor(dx[:, hf].rearrange("p (b t) -> p b t", b=B), xf[:, hf, :, 1:],
                                            xf[:, hf, :, 0:C], ALU.subtract).then_inc(s["dx"], 1)
                dve.wait_ge(s["dx"], n * 2 + 2)
                for i, dst in ((1, xk), (0, xr)):
                    for hf in range(HALVES):
                        nc.vector.scalar_tensor_tensor(dst[:, hf].rearrange("p (b t) -> p b t", b=B),
                                                       dx[:, hf].rearrange("p (b t) -> p b t", b=B), mu[:, i, hf:hf + 1],
                                                       xf[:, hf, :, 0:C], ALU.mult, ALU.add).then_inc(s["mix"], 1)

            def ffn_out(n):
                dve.wait_ge(s["vmm"], n * 1 + 1)
                dve.wait_ge(s["th"], n * 1 + 1)
                dve.wait_ge(s["t3"], n * 1)
                nc.vector.scalar_tensor_tensor(f2, th, 1.0, bank[6][:, :].rearrange("p (j c) -> p j c", j=2),
                                               ALU.add, ALU.mult).then_inc(s["f2"], 1)
                dve.wait_ge(s["f2"], n * 1 + 1)
                row_stats(n, 2, "st3", f2, 4 * EPS, "t3")

            def store_ready(n):
                dve.wait_ge(s["r3"], n * 1 + 1)
                dve.wait_ge(s["y_out"], n * 1)
                row_norm(n, 2, t3, f2, "t3")
                dve.wait_ge(s["t3"], n * 1 + 1)
                dve.wait_ge(s["stored"], n * 64)
                nc.vector.tensor_tensor(y_out, t3, x1, ALU.add).then_inc(s["y_out"], 1)

            for t in range(4):
                conv(0, t)
            sumsq_out(0)
            m_parts(0)
            at_parts(0)
            for l in range(NL):
                level(0, l)
            z_scaled(0)
            def chunk_step(n):
                conv(n + 1, 0)
                conv(n + 1, 1)
                o_parts(n)
                conv(n + 1, 2)
                conv(n + 1, 3)
                o_meansq(n)
                sumsq_out(n + 1)
                m_parts(n + 1)
                o_normed(n)
                at_parts(n + 1)
                level(n + 1, 0)
                y_stats(n)
                level(n + 1, 1)
                residual(n)
                x_normed(n)
                level(n + 1, 2)
                mixes(n)
                level(n + 1, 3)
                ffn_out(n)
                level(n + 1, 4)
                store_ready(n)
                z_scaled(n + 1)

            chunk_step(0)
            with dve.Fori(1, N - 1) as n:
                chunk_step(n)
            n = N - 1
            o_parts(n)
            o_meansq(n)
            o_normed(n)
            y_stats(n)
            residual(n)
            x_normed(n)
            mixes(n)
            ffn_out(n)
            store_ready(n)

        @block.tensor
        def _(pe):
            mm = nc.tensor.matmul
            pe.wait_ge(s["consts_in"], 16)
            pe.wait_ge(s["weights_in"], 16 * N_W)

            def a_xT(b, q):
                pe.wait_ge(s["a_normed"], b * 8 + 2 * q + 2)
                pe.wait_ge(s["a_xT_out"], b * 4 + (q - 1 if q >= 1 else 0))
                for hf in range(HALVES):
                    for k in range(2):
                        last = nc.tensor.transpose(bank[q % 2][:, 256 * hf + P * k:256 * hf + P * k + P],
                                                   xna[:, 2 * q + k, P * hf:P * hf + P], ident)
                last.then_inc(s["a_xT"], 1)

            def a_proj(b, q):
                pe.wait_ge(s["a_xT_out"], b * 4 + q + 1)
                for oh in range(2):
                    i = 2 * q + oh
                    pe.wait_ge(s["a_conv"], b * 24 + (3 * (i - 1) if i >= 2 else 0))
                    for kh in range(HALVES):
                        last = mm(bank[2 + oh][:, 0:PAD + 256], w["v"][:, kh, P * oh:P * oh + P],
                                  xnT[:, kh, 256 * q:256 * q + 256 + PAD], start=(kh == 0), stop=(kh == 1))
                    last.then_inc(s["a_proj"], 1)

            def a_win(b, i):
                q, pr = i // 2, i % 2
                pe.wait_ge(s["a_vT"], b * 8 + i + 1)
                pe.wait_ge(s["a_win_out"], b * 8 + (i - 1 if i >= 2 else 0))
                pe.wait_ge(s["a_vb"], b * 16 + (2 * (i - 1) if i >= 2 else 0))
                for k in range(4):
                    at_ = C * (4 * q + k)
                    last = nc.tensor.transpose(bank[4 + pr][:, P * k:P * k + P], vT[:, pr, at_:at_ + P], ident)
                last.then_inc(s["a_win"], 1)

            def a_gate(b):
                pe.wait_ge(s["a_gate_out"], b * 8)
                for m in range(M_TILES):
                    for kh in range(HALVES):
                        last = mm(bank[6][:, H * NG * m:H * NG * (m + 1)], xnT[:, kh, PAD + P * m:PAD + P * m + P],
                                  w_gate[:, kh, :], start=(kh == 0), stop=(kh == 1))
                last.then_inc(s["a_gate"], 1)

            def sequence(b):
                a_xT(b, 0)
                a_xT(b, 1)
                a_proj(b, 0)
                a_xT(b, 2)
                a_proj(b, 1)
                a_win(b, 0)
                a_win(b, 1)
                a_xT(b, 3)
                a_proj(b, 2)
                a_win(b, 2)
                a_win(b, 3)
                a_proj(b, 3)
                a_win(b, 4)
                a_win(b, 5)
                a_gate(b)
                a_win(b, 6)
                a_win(b, 7)

            sequence(0)
            with pe.Fori(1, B) as b:
                sequence(b)

            pe.wait_ge(s["a_win_out"], 8 * B)
            pe.wait_ge(s["a_gate_out"], 8 * B)
            pe.wait_ge(s["a_conv"], 24 * B)
            pe.wait_ge(s["a_vb"], 16 * B)
            for g in range(FG):
                for f in range(3):
                    if f == 0:
                        pe.wait_ge(s["toep_l_in"], 16 * (g + 1))
                    elif f == 1:
                        pe.wait_ge(s["toep_ms_in"], 32 * (g + 1))
                    toep = toep_l if f == 0 else toep_ms[:, f - 1]
                    for j in range(4):
                        k = 12 * g + 4 * f + j
                        if k >= 8:
                            pe.wait_ge(s["fir_prod"], k - 7)
                        for hh in range(2):
                            for d in range(8):
                                c = P * (g // 2) + 64 * hh + 32 * (g % 2) + 8 * j + d
                                last = mm(bank[k % 8][HH[hh], BLK * d:BLK * d + BLK],
                                          toep[:, :, 32 * hh + 8 * j + d], vwin[:, c, :], start=True, stop=True)
                        last.then_inc(s["fir_mm"], 1)

            pe.wait_ge(s["fir_prod"], 12 * FG)
            pe.wait_ge(s["state_zero"], 1)
            for hf in range(HALVES):
                mm(bank[7][:, 256 * hf:256 * hf + 256], ident, xf[:, 0, 0:B, 0:C], start=True, stop=True)

            def proj(n, kind):
                pe.wait_ge(s["window_in"], n * 32 + 32)
                for g in range(2):
                    if kind == 0:
                        pe.wait_ge(s["at"], n * 4)
                        pe.wait_ge(s["mt"], n * 2)
                    else:
                        pe.wait_ge(s["conv"], n * 12 + 3 * g + 3)
                    for kh in range(HALVES):
                        last = mm(bank[g][:, 0:B * (C + PAD)], w["kq"[kind]][:, kh, P * g:P * g + P],
                                  xwin[:, kh], start=(kh == 0), stop=(kh == 1))
                    last.then_inc(s["proj"], 1)

            def sumsq(n):
                pe.wait_ge(s["square"], n * 4 + 4)
                pe.wait_ge(s["wbd"], n * 4)
                for a in range(2 * U):
                    last = mm(bank[2][:, 2 * a:2 * a + 2], sq[:, a].rearrange("p two t -> p (two t)"), headsel, start=True, stop=True)
                last.then_inc(s["sumsq"], 1)

            def k_turn(n):
                for g in range(2):
                    pe.wait_ge(s["bd"], n * 8 + 2 * g + 2)
                    pe.wait_ge(s["conv"], n * 12 + 3 * (2 + g) + 3)
                    for u in range(G4):
                        last = nc.tensor.transpose(bank[g][:, P * u:P * u + P], kT_bd[:, G4 * g + u, :], ident)
                    last.then_inc(s["ktr"], 1)

            def gram(n):
                pe.wait_ge(s["silu"], n * 4 + 4)
                for g in range(2):
                    pe.wait_ge(s["kbd"], n * 2 + g + 1)
                    for u in range(G4):
                        last = mm(bank[g][:, P * u:P * u + P], kT_bd[:, G4 * g + u, :], kq[:, G4 * g + u],
                                  start=True, stop=True)
                    last.then_inc(s["gram"], 1)

            def level(n, l):
                for g in range(2):
                    pe.wait_ge(s["z"], n * 12 + 2 * l + g + 1)
                    if l == 0:
                        pe.wait_ge(s["mbd"], n * 4 + 2 * g + 2)
                    for u in range(G4):
                        last = mm(bank[2 + g][:, C * u:C * u + C], M_bd[:, G4 * g + u, :], Z[:, G4 * g + u, :],
                                  start=True, stop=True)
                    last.then_inc(s["mm1"], 1)
                for g in range(2):
                    pe.wait_ge(s["pm"], n * 2 * NL + 2 * l + g + 1)
                    if l == 0:
                        pe.wait_ge(s["xbd0"], n * 4 + 2 * g + 2)
                    else:
                        pe.wait_ge(s["xbd"], n * 4 * (NL - 1) + 4 * (l - 1) + 2 * g + 2)
                    for u in range(G4):
                        last = mm(bank[2 + g][:, 256 + C * u:256 + C * u + C], X_bd[:, G4 * g + u, :],
                                  Pm[:, G4 * g + u, :], start=True, stop=True)
                    last.then_inc(s["mm2"], 1)

            def w_rows(n):
                for g in range(2):
                    pe.wait_ge(s["zs"], n * 2 + g + 1)
                    for u in range(G4):
                        last = mm(bank[2 + g][:, C * u:C * u + C], k_bd[:, G4 * g + u, :], Zs[:, G4 * g + u, :],
                                  start=True, stop=True)
                    last.then_inc(s["wmm"], 1)

            def scan_u(n):
                pe.wait_ge(s["zbd"], n * 4 + 4)
                pe.wait_ge(s["vp"], n * 1 + 1)
                pe.wait_ge(s["wbd"], n * 4 + 4)
                pe.wait_ge(s["S"], n * 1 + 1)
                pe.wait_ge(s["xf"], n * 2)
                for u in range(U):
                    mm(bank[4][:, C * u:C * u + C], Z_bd[:, u, :], vp[:, u, :], start=True, stop=False)
                    last = mm(bank[4][:, C * u:C * u + C], wT_bd[:, u, :], S[:, u, :], start=False, stop=True)
                last.then_inc(s["umm"], 1)

            def scan_state(n):
                pe.wait_ge(s["ut"], n * 1 + 1)
                for u in range(U):
                    last = mm(bank[7][:, C * u:C * u + C], k_bd[:, u, :], ut[:, u, :], start=False, stop=False,
                              skip_group_check=True)
                last.then_inc(s["state"], 1)

            def scan_o(n):
                pe.wait_ge(s["bd"], n * 8 + 8)
                pe.wait_ge(s["at"], n * 4 + 4)
                pe.wait_ge(s["rl"], n * 1)
                for u in range(U):
                    mm(bank[5][:, C * u:C * u + C], qT_bd[:, u, :], S[:, u, :], start=True, stop=False)
                    last = mm(bank[5][:, C * u:C * u + C], atT_bd[:, u, :], ut[:, u, :], start=False, stop=True)
                last.then_inc(s["omm"], 1)

            def o_turn(n):
                pe.wait_ge(s["obd"], n * 2 + 2)
                for u in range(U):
                    last = mm(bank[4][:, C * u:C * u + C], o_bd[:, u, :], rstack, start=True, stop=True)
                last.then_inc(s["oT_mm"], 1)

            def tokens(lhs, wt, dst, k_first=0):
                for j in range(2):
                    for kh in range(HALVES):
                        last = mm(dst[:, 256 * j:256 * j + 256], lhs[:, kh, P * j:P * j + P], wt[:, kh, :],
                                  start=(kh == 0), stop=(kh == 1))
                return last

            def y_rows(n):
                pe.wait_ge(s["oT"], n * 1 + 1)
                pe.wait_ge(s["o1"], n * 1 + 1)
                tokens(oT.rearrange("p (r b) t -> p r (b t)", r=PAIRS), w["o"], bank[5]).then_inc(s["ymm"], 1)

            def x_turn(n):
                pe.wait_ge(s["xn2"], n * 1 + 1)
                for hf in range(HALVES):
                    for j in range(2):
                        last = nc.tensor.transpose(bank[4][:, 256 * hf + P * j:256 * hf + P * j + P],
                                                   xn2[:, j, P * hf:P * hf + P], ident)
                last.then_inc(s["xT"], 1)

            def ffn_in(n):
                pe.wait_ge(s["mix"], n * 4 + 2)
                pe.wait_ge(s["t1"], n * 1 + 1)
                for oh in range(2):
                    for kh in range(HALVES):
                        last = mm(bank[5][:, 256 * oh:256 * oh + 256], w["fk"][:, kh, P * oh:P * oh + P], xk[:, kh, :],
                                  start=(kh == 0), stop=(kh == 1))
                last.then_inc(s["kmm"], 1)
                pe.wait_ge(s["mix"], n * 4 + 4)
                pe.wait_ge(s["f2"], n * 1)
                tokens(xr, w["r"], bank[6]).then_inc(s["rmm"], 1)

            def ffn_v(n):
                pe.wait_ge(s["ka"], n * 1 + 1)
                pe.wait_ge(s["th"], n * 1 + 1)
                tokens(ka, w["fv"], bank[6]).then_inc(s["vmm"], 1)

            proj(0, 0)
            proj(0, 1)
            sumsq(0)
            k_turn(0)
            gram(0)
            for l in range(NL):
                level(0, l)
            w_rows(0)
            def chunk_step(n):
                scan_u(n)
                proj(n + 1, 0)
                scan_state(n)
                scan_o(n)
                proj(n + 1, 1)
                sumsq(n + 1)
                k_turn(n + 1)
                gram(n + 1)
                o_turn(n)
                y_rows(n)
                level(n + 1, 0)
                level(n + 1, 1)
                x_turn(n)
                level(n + 1, 2)
                ffn_in(n)
                level(n + 1, 3)
                ffn_v(n)
                level(n + 1, 4)
                w_rows(n + 1)

            chunk_step(0)
            with pe.Fori(1, N - 1) as n:
                chunk_step(n)
            n = N - 1
            scan_u(n)
            scan_state(n)
            scan_o(n)
            o_turn(n)
            y_rows(n)
            x_turn(n)
            ffn_in(n)
            ffn_v(n)


def constants():
    import numpy as np

    c = np.zeros((P, NCONST), np.float32)
    i = np.arange(P) % C
    j = np.arange(C)
    c[:, C_ID:C_ID + P] = np.eye(P)
    c[:, C_R:C_R + C] = i[:, None] == j[None, :]
    c[:, C_LOW:C_LOW + C] = i[:, None] > j[None, :]
    c[:, C_UP:C_UP + C] = i[:, None] <= j[None, :]
    c[:, C_NM1:C_NM1 + C] = -1.0 * ((i[:, None] // 2 == j[None, :] // 2) & (i[:, None] > j[None, :]))
    for l, size in enumerate(LEVELS):
        same = i[:, None] // (2 * size) == j[None, :] // (2 * size)
        c[:, C_LV + C * l:C_LV + C * (l + 1)] = same & (i[:, None] // size % 2 == 0) & (j[None, :] // size % 2 == 1)
    c[:, C_HS] = np.arange(P) < C
    c[:, C_HS + 1] = np.arange(P) >= C
    return c


def kernel(**inputs):
    import numpy as np
    import concourse.bacc as bacc
    from concourse.bass_utils import run_bass_kernel_spmd

    g = {k[3:]: np.asarray(v) for k, v in inputs.items()}
    order = np.arange(D).reshape(PAIRS, 2, 2, 32).transpose(0, 2, 1, 3).reshape(D)

    def padded(f):
        taps = f.reshape(D, -1)[order].T
        rows = np.zeros((ROWS, D), f.dtype)
        rows[P - taps.shape[0]:P] = taps
        return rows.reshape(ROWS, FG, GC).transpose(1, 0, 2)

    def per_head(v):
        return np.repeat(v.reshape(PAIRS, 2, -1).transpose(1, 0, 2).reshape(2, -1), C, axis=0)

    arrays = {
        "x": g["attn_hidden_states"],
        "wgate": np.concatenate([g["attn_gate_w"], g["attn_Wb"][:, None, :]], axis=1).reshape(H * NG, D).T,
        "consts": constants(),
        "wq": g["attn_Wq"].T, "wk": g["attn_Wk"].T, "wv": g["attn_Wv"].T, "wo": g["attn_Wo"].T,
        "wr": g["ffn_W_r"].T, "wfk": g["ffn_W_k"].T, "wfv": g["ffn_W_v"].T,
        "smalls": np.concatenate([
            *(g[k].reshape(HALVES, P, TAPS).transpose(1, 0, 2).reshape(P, -1) for k in ("attn_conv_q", "attn_conv_k", "attn_conv_v")),
            *(g[k].reshape(HALVES, P).T for k in ("ffn_mu_r", "ffn_mu_k")),
            np.tile(g["attn_norm_w"], 2)[:, None],
            *(per_head(g[k]) for k in ("attn_gate_b", "attn_log_temp", "attn_eps_param"))], axis=1),
        "fl": padded(g["attn_fir_l"]),
        "fms": np.stack([padded(g["attn_fir_m"]), padded(g["attn_fir_s"])]),
    }
    arrays = {k: np.ascontiguousarray(v) for k, v in arrays.items()}
    nc = bacc.Bacc("TRN2", target_bir_lowering=False, num_devices=1)
    a = {k: nc.dram_tensor(k, v.shape, F32, kind="ExternalInput").ap() for k, v in arrays.items()}
    out = nc.dram_tensor("out", (B, L, D), F32, kind="ExternalOutput").ap()
    build(nc, a["x"], out, *(a[k] for k in (
        "wgate", "consts", "smalls", "wq", "wk", "wv", "wo", "wr", "wfk", "wfv", "fl", "fms")))
    r = run_bass_kernel_spmd(nc, [arrays], core_ids=[0])
    return r.results[0]["out"]
```

```python
from contextlib import ExitStack

import concourse.bass as bass
from concourse import mybir

F32 = mybir.dt.float32
ALU = mybir.AluOpType
ACT = mybir.ActivationFunctionType
AX = mybir.AxisListType.X

P = 128
B, L, D, H = 4, 1024, 256, 4
DK = D // H
C = 64
N = L // C
HALVES = D // P
PAIRS = H // 2
U = PAIRS * B
G4 = B
G5 = G4 + 1
BLK = B * N
TAPS = 4
PAD = TAPS - 1
LP = L + PAD
NG = 6
MS0 = 48
ROWS = 2 * P - C
LEVELS = (2, 4, 8, 16, 32)
NL = len(LEVELS)
GC = 64
FG = D // GC
EPS, L2EPS = 1e-5, 1e-6
G_SHIFTED, G_STEPS = 5, 11

C_ID, C_R, C_LOW, C_UP, C_NM1, C_LV, C_ONE = 0, 128, 192, 256, 320, 384, 384 + 64 * NL
NCONST = C_ONE + 1
NSMALL = 3 * HALVES * TAPS + 2 * HALVES + 1 + PAIRS * 5 + 2 * PAIRS


def build(nc, x, out, wgate, consts, smalls, wq, wk, wv, wo, wr, wfk, wfv, fl, fms):
    ctx = ExitStack()
    with ctx:
        def sb(name, shape):
            return ctx.enter_context(nc.sbuf_tensor(name, shape, F32))

        def sem(name):
            return ctx.enter_context(nc.semaphore(name))

        xnT_dram = nc.dram_tensor("xnT_scratch", (P, HALVES, B, LP), F32, kind="Internal").ap()
        v_dram = nc.dram_tensor("v_scratch", (N, P, U, DK), F32, kind="Internal").ap()

        cst = sb("cst", [P, NCONST])
        ident = cst[:, C_ID:C_ID + P]
        rstack = cst[:, C_R:C_R + C]
        low = cst[:, C_LOW:C_LOW + C]
        up = cst[:, C_UP:C_UP + C]
        negpairs = cst[:, C_NM1:C_NM1 + C]
        ones = cst[:, C_ONE:C_ONE + 1]

        def level_mask(l):
            return cst[:, C_LV + C * l:C_LV + C * (l + 1)]

        w = {k: sb("w_" + k, [P, HALVES, D]) for k in ("q", "k", "v", "o", "r", "fk", "fv")}
        w_gate = sb("w_gate", [P, HALVES, H * NG])
        small = sb("small", [P, NSMALL])
        conv_w = small[:, 0:24].rearrange("p (i h k) -> p i h k", i=3, h=HALVES)
        mu = small[:, 24:28].rearrange("p (i h) -> p i h", i=2)
        norm_w = small[:, 28:29]
        gb = small[:, 29:39].rearrange("p (r g) -> p r g", r=PAIRS)
        inv_temp = small[:, 39:41]
        mix_eps = small[:, 41:43]
        neg_half = sb("neg_half", [P, 16])
        mix_scale = sb("mix_scale", [P, PAIRS])

        gates = sb("gates", [P, NG, PAIRS, BLK])
        gmax = sb("gmax", [P, PAIRS, BLK])
        fir = sb("fir", [P, DK, PAIRS, BLK])

        A_V = BLK * D
        A_T = 3 * C * GC
        arena = sb("arena", [P, A_V + A_T])
        vwin = arena[:, 0:A_V].rearrange("p (c w) -> p c w", w=BLK)
        toep_l = arena[:, A_V:A_V + C * GC].rearrange("p (t c) -> p t c", c=GC)
        toep_ms = arena[:, A_V + C * GC:A_V + A_T].rearrange("p (f t c) -> p f t c", f=2, c=GC)

        def carve(whole, at, *shape):
            n = 1
            for k in shape:
                n *= k
            view = whole[:, at[0]:at[0] + n]
            at[0] += n
            if len(shape) == 2:
                return view.rearrange("p (a b) -> p a b", b=shape[1])
            if len(shape) == 3:
                return view.rearrange("p (a b c) -> p a b c", b=shape[1], c=shape[2])
            return view

        M_TILES = L // P
        SA = 2 * M_TILES * D + HALVES * LP + HALVES * (C + L) + N * PAIRS * DK
        seq = sb("seq", [P, SA])
        sa = [0]
        xa = carve(seq, sa, M_TILES, D)
        xna = carve(seq, sa, M_TILES, D)
        xnT = carve(seq, sa, HALVES, LP)
        vT = carve(seq, sa, HALVES, C + L)
        vb = carve(seq, sa, N, PAIRS, DK)
        sc = [0]
        kT_bd, qT_bd, k_bd, atT_bd, M_bd, X_bd, Z_bd, wT_bd, o_bd = (carve(seq, sc, U, P) for _ in range(9))
        bd_all = seq[:, 0:sc[0]]
        fprod = carve(seq, sc, 2, 512)

        stats_a = sb("stats_a", [P, M_TILES, 6])
        mv_a = sb("mv_a", [P, M_TILES, 2])
        ve_a = sb("ve_a", [P, M_TILES])
        rs_a = sb("rs_a", [P, M_TILES])
        cva = sb("cva", [P, 2, 256])
        ac = [0]

        def take(*shape):
            return carve(arena, ac, *shape)

        xwin, v_c, cv, kq, sq = take(HALVES, B, C + PAD), take(U, DK), take(4, B, C), take(U, 2, C), take(2 * U, P)
        Mt, Mc, X2, Zs = (take(U, C) for _ in range(4))
        Z, Pm = (take(2 * G5, C) for _ in range(2))
        vp, S, ut, ov, o1, o2, osq, oT = (take(U, DK) for _ in range(8))
        x_in, t1, x1, xn2, th, f2, t3, y_out = (take(2, D) for _ in range(8))
        xf = take(HALVES, B, C + 1)
        dx, xr, xk, rl, ka = (take(HALVES, B * C) for _ in range(5))
        ssel, rk = take(2, U), take(2, U)
        bv, d2, qs, oms, ro = (take(1, U) for _ in range(5))
        bn, mv, ve, rs = take(3, 2, 6), take(3, 2, 2), take(3, 2), take(3, 2)
        assert ac[0] <= A_V + A_T and sc[0] <= SA

        bank = [ctx.enter_context(nc.psum_tensor(f"bank{i}", [P, 512], F32)) for i in range(8)]

        s = {n: sem(n) for n in (
            "consts_in", "weights_in", "half_set", "pads_set",
            "xa_in", "a_stats", "a_rs", "a_normed", "a_xT", "a_xT_out", "a_xT_stored", "a_proj",
            "a_tap", "a_conv", "a_vT", "a_win", "a_win_out", "a_vb", "a_vb_stored", "a_gate",
            "a_gate_out",
            "g_step", "g_exp",
            "toep_zero", "toep_l_in", "toep_ms_in", "fir_mm", "fir_prod", "fir_sum",
            "bd_zero", "state_zero", "pad_zero", "window_in", "v_in", "x_in", "proj", "tap", "conv", "silu", "square", "bd",
            "sumsq_k", "sumsq_q", "ssk", "ssq", "k_scal", "q_scal", "vp", "ov", "ktr", "kbd", "gram_k", "gram_q", "mt", "mc", "x2", "at",
            "mbd", "xbd0", "z", "mm1", "pm", "mm2", "xbd", "zs", "zbd", "wmm", "wbd",
            "umm", "ut", "state", "omm", "S", "o1", "o2", "osq", "oms", "ro", "obd", "oT_mm", "oT",
            "ymm", "st1", "r1", "t1", "x1", "st2", "r2", "xn2", "xT", "halo", "xf", "dx", "mix",
            "rmm", "kmm", "th", "rl", "ka", "vmm", "f2", "st3", "r3", "t3", "y_out", "stored")}

        block = ctx.enter_context(nc.Block())
        x4 = x.rearrange("b (n t) c -> b n t c", t=C)
        out4 = out.rearrange("b (n t) c -> b n t c", t=C)
        HH = [slice(0, 64), slice(64, 128)]
        N_W = 7 + 1 + 1

        def alone(eng):
            eng.nop(nofuse=True)

        def grp(g):
            return slice(G4 * g, G4 * g + G4)

        def padded(g):
            return slice(G5 * g, G5 * g + G4)

        def units(ap, k=C):
            return ap.rearrange("p (u k) -> p u k", k=k)

        @block.sync
        def _(sp):
            xam = [x[b].rearrange("(m p) c -> p m c", p=P) for b in range(B)]
            sp.dma_start(xa, xam[0]).then_inc(s["xa_in"], 16)
            sp.dma_start(cst[:, :], consts).then_inc(s["consts_in"], 16)
            for key, src in (("v", wv), ("q", wq), ("k", wk), ("o", wo), ("r", wr), ("fk", wfk), ("fv", wfv)):
                sp.dma_start(w[key][:, :, :], src.rearrange("(h p) d -> p h d", p=P)).then_inc(s["weights_in"], 16)
            sp.dma_start(w_gate[:, :, :], wgate.rearrange("(h p) d -> p h d", p=P)).then_inc(s["weights_in"], 16)
            sp.dma_start(small[:, :], smalls).then_inc(s["weights_in"], 16)

            def load_l(g):
                sp.dma_start(toep_l, runs(fl[g], 0, P)).then_inc(s["toep_l_in"], 16)

            def load_ms(g):
                for i in range(2):
                    sp.dma_start(toep_ms[MS0:P, i], runs(fms[i, g], MS0, P - MS0)).then_inc(s["toep_ms_in"], 16)

            def runs(taps, first, rows):
                return bass.AP(taps.tensor, taps.offset + (first + C - 1) * GC, [[GC, rows], [-GC, C], [1, GC]])

            x_flat = x.rearrange("b (m p) c -> p b m c", p=P)
            v_dst = v_dram.rearrange("n p (r b) d -> p r b n d", b=B)
            sp.wait_ge(s["toep_zero"], 1)
            load_l(0)
            load_ms(0)

            def xT_store(b):
                sp.wait_ge(s["a_xT_out"], b * 4 + 4)
                alone(sp)
                sp.dma_start(xnT_dram[:, :, b, :], xnT).then_inc(s["a_xT_stored"], 16)

            def v_store(b):
                sp.wait_ge(s["a_vb"], b * 16 + 16)
                alone(sp)
                for pr in range(PAIRS):
                    sp.dma_start(v_dst[:, pr, b], vb[:, :, pr, :]).then_inc(s["a_vb_stored"], 16)

            def sequence(b):
                xT_store(b)
                sp.wait_ge(s["a_normed"], b * 8 + 8)
                alone(sp)
                sp.dma_start(xa, x_flat[:, b + 1]).then_inc(s["xa_in"], 16)
                v_store(b)

            sequence(0)
            with sp.Fori(1, B - 1) as b:
                sequence(b)
            xT_store(B - 1)
            v_store(B - 1)

            for g in range(1, FG):
                sp.wait_ge(s["fir_mm"], g * 12 - 8)
                load_l(g)
                sp.wait_ge(s["fir_mm"], g * 12)
                load_ms(g)

            def window_in(n):
                sp.wait_ge(s["proj"], n * 4)
                alone(sp)
                for hf in range(HALVES):
                    sp.dma_start(xwin[:, hf], xnT_dram[:, hf, :, bass.ds(n * C, C + PAD)]).then_inc(s["window_in"], 16)

            def values_in(n):
                sp.wait_ge(s["vp"], n * 1)
                alone(sp)
                sp.wait_ge(s["ov"], n * 2)
                alone(sp)
                sp.dma_start(v_c, v_dram[n]).then_inc(s["v_in"], 16)

            def rows_in(n):
                sp.wait_ge(s["x1"], n * 1)
                alone(sp)
                for bb in range(2):
                    for j in range(2):
                        sp.dma_start(x_in[HH[bb], j, :], x4[2 * j + bb, n]).then_inc(s["x_in"], 16)

            def rows_out(n):
                sp.wait_ge(s["y_out"], n * 1 + 1)
                alone(sp)
                for bb in range(2):
                    for j in range(2):
                        sp.dma_start(out4[2 * j + bb, n], y_out[HH[bb], j, :]).then_inc(s["stored"], 16)

            sp.wait_ge(s["fir_mm"], 12 * FG)
            sp.wait_ge(s["a_xT_stored"], 16 * B)
            sp.wait_ge(s["a_vb_stored"], 32 * B)
            window_in(0)
            values_in(0)
            rows_in(0)
            window_in(1)
            values_in(1)

            def chunk_step(n):
                window_in(n + 2)
                values_in(n + 2)
                rows_in(n + 1)
                rows_out(n)

            chunk_step(0)
            with sp.Fori(1, N - 2) as n:
                chunk_step(n)
            rows_in(N - 1)
            rows_out(N - 2)
            rows_out(N - 1)
            sp.wait_ge(s["stored"], 64 * N)

        @block.gpsimd
        def _(pool):
            pool.memset(neg_half[:, :], -0.5).then_inc(s["half_set"], 1)
            pool.memset(xnT[:, :, 0:PAD], 0.0).then_inc(s["pads_set"], 1)
            pool.memset(vT[:, :, 0:C], 0.0).then_inc(s["pads_set"], 1)
            pool.memset(arena[:, A_V:A_V + A_T], 0.0).then_inc(s["toep_zero"], 1)
            half8 = neg_half[:, 0:U].rearrange("p (a u) -> p a u", a=1)
            pool.wait_ge(s["half_set"], 1)
            def sequence(b):
                pool.wait_ge(s["a_stats"], b * 3 + 3)
                pool.tensor_tensor(rs_a[:, :], ve_a[:, :], neg_half[:, 0:M_TILES], ALU.pow).then_inc(s["a_rs"], 1)

            sequence(0)
            with pool.Fori(1, B) as b:
                sequence(b)

            pool.wait_ge(s["a_win"], 8 * B)
            pool.wait_ge(s["a_gate"], B)
            pool.wait_ge(s["a_xT_stored"], 16 * B)
            pool.wait_ge(s["a_vb_stored"], 32 * B)
            pool.memset(bd_all, 0.0).then_inc(s["bd_zero"], 1)

            for g in range(FG):
                for f in range(1, 3):
                    for j in range(4):
                        q = 8 * g + 4 * (f - 1) + j
                        acc = fir[:, 32 * (g % 2) + 8 * j:32 * (g % 2) + 8 * j + 8, g // 2, :]
                        pool.wait_ge(s["fir_prod"], 12 * g + 4 * f + j + 1)
                        if f == 2:
                            pool.wait_ge(s["fir_sum"], q - 3)
                        pool.tensor_tensor(acc, acc, fprod[:, q % 2, :].rearrange("p (c w) -> p c w", w=BLK),
                                           ALU.add).then_inc(s["fir_sum"], 1)

            pool.wait_ge(s["fir_mm"], 12 * FG)
            pool.wait_ge(s["fir_sum"], 8 * FG)
            pool.wait_ge(s["g_step"], G_STEPS)
            pool.wait_ge(s["bd_zero"], 1)
            pool.memset(S, 0.0).then_inc(s["S"], 1)
            pool.memset(xf, 0.0).then_inc(s["state_zero"], 1)
            pool.memset(Z, 0.0).then_inc(s["pad_zero"], 1)
            pool.memset(Pm, 0.0).then_inc(s["pad_zero"], 1)
            pool.wait_ge(s["state_zero"], 1)

            def row_gate(g, n):
                return gates[:, g, :, :].rearrange("p r (b n) -> p (r b) n", n=N)[:, :, bass.ds(n, 1)]

            def k_scalars(n):
                pool.wait_ge(s["ssk"], n * 1 + 1)
                pool.wait_ge(s["k_scal"], n * 3)
                pool.tensor_tensor(rk[:, 0:1], ssel[:, 0:1], half8, ALU.pow).then_inc(s["k_scal"], 1)
                pool.wait_ge(s["k_scal"], n * 3 + 1)
                pool.wait_ge(s["vp"], n * 1)
                pool.tensor_tensor(bv.rearrange("p a (u o) -> p (a u) o", o=1), row_gate(5, n),
                                   rk[:, 0].rearrange("p (u o) -> p u o", o=1), ALU.mult).then_inc(s["k_scal"], 1)
                pool.wait_ge(s["k_scal"], n * 3 + 2)
                pool.wait_ge(s["zs"], n * 2)
                pool.tensor_tensor(d2, bv, rk[:, 0:1], ALU.mult).then_inc(s["k_scal"], 1)

            def q_scalars(n):
                pool.wait_ge(s["ssq"], n * 1 + 1)
                pool.wait_ge(s["q_scal"], n * 2)
                pool.tensor_tensor(rk[:, 1:2], ssel[:, 1:2], half8, ALU.pow).then_inc(s["q_scal"], 1)
                pool.wait_ge(s["q_scal"], n * 2 + 1)
                pool.wait_ge(s["o1"], n * 1)
                pool.tensor_tensor(qs.rearrange("p a (u o) -> p (a u) o", o=1), row_gate(3, n),
                                   rk[:, 1].rearrange("p (u o) -> p u o", o=1), ALU.mult).then_inc(s["q_scal"], 1)

            def values(n):
                pool.wait_ge(s["v_in"], n * 16 + 16)
                pool.wait_ge(s["k_scal"], n * 3 + 3)
                pool.wait_ge(s["umm"], n * 1)
                pool.tensor_tensor(vp, v_c, bv.rearrange("p a (u o) -> p (a u) o", o=1).broadcast_to((P, U, DK)),
                                   ALU.mult).then_inc(s["vp"], 1)

            def direct(n):
                pool.wait_ge(s["v_in"], n * 16 + 16)
                local = fir[:, :, :, :].rearrange("p d r (b n) -> p (r b) d n", n=N)[:, :, :, bass.ds(n, 1)]
                pool.wait_ge(s["o2"], n * 1)
                pool.tensor_tensor(ov, v_c, row_gate(4, n).broadcast_to((P, U, DK)), ALU.mult).then_inc(s["ov"], 1)
                pool.wait_ge(s["ov"], n * 2 + 1)
                ov4 = ov.rearrange("p u (d o) -> p u d o", o=1)
                pool.tensor_tensor(ov4, ov4, local, ALU.add).then_inc(s["ov"], 1)

            def power(n, src_sem, per, dst_sem, dst, src, k):
                pool.wait_ge(s[src_sem], n * per + per)
                pool.tensor_tensor(dst, src, half8 if k == U else neg_half[:, 0:k], ALU.pow).then_inc(s[dst_sem], 1)

            def halo(n):
                pool.wait_ge(s["mix"], n * 4)
                pool.wait_ge(s["xf"], n * 2)
                alone(pool)
                pool.tensor_copy(xf[:, :, :, 0:1], xf[:, :, :, C:C + 1]).then_inc(s["halo"], 1)

            def output(n):
                pool.wait_ge(s["t3"], n * 1 + 1)
                pool.wait_ge(s["stored"], n * 64)
                pool.tensor_tensor(y_out, t3, x1, ALU.add).then_inc(s["y_out"], 1)

            k_scalars(0)
            direct(0)
            q_scalars(0)
            values(0)

            def chunk_step(n):
                power(n, "oms", 2, "ro", ro, oms, U)
                k_scalars(n + 1)
                power(n, "st1", 3, "r1", rs[:, 0], ve[:, 0], 2)
                halo(n)
                direct(n + 1)
                power(n, "st2", 3, "r2", rs[:, 1], ve[:, 1], 2)
                q_scalars(n + 1)
                values(n + 1)
                power(n, "st3", 3, "r3", rs[:, 2], ve[:, 2], 2)
                output(n)

            chunk_step(0)
            with pool.Fori(1, N - 1) as n:
                chunk_step(n)
            n = N - 1
            power(n, "oms", 2, "ro", ro, oms, U)
            power(n, "st1", 3, "r1", rs[:, 0], ve[:, 0], 2)
            halo(n)
            power(n, "st2", 3, "r2", rs[:, 1], ve[:, 1], 2)
            power(n, "st3", 3, "r3", rs[:, 2], ve[:, 2], 2)
            output(n)

        @block.scalar
        def _(act):
            act.wait_ge(s["weights_in"], 16 * N_W)
            act.wait_ge(s["pads_set"], 2)

            def a_xT_out(b, q):
                act.wait_ge(s["a_xT"], b * 4 + q + 1)
                if q == 0:
                    act.wait_ge(s["a_proj"], b * 8)
                    act.wait_ge(s["a_gate"], b * 1)
                    act.wait_ge(s["a_xT_stored"], b * 16)
                act.activation(xnT[:, :, PAD + 256 * q:PAD + 256 * q + 256],
                               bank[q % 2][:, :].rearrange("p (h t) -> p h t", h=HALVES), ACT.Copy).then_inc(s["a_xT_out"], 1)

            def a_tap(b, i):
                act.wait_ge(s["a_proj"], b * 8 + i + 1)
                act.wait_ge(s["a_vT"], b * 8 + (i - 1 if i >= 2 else 0))
                act.activation(cva[:, i % 2, :], bank[2 + i % 2][:, PAD:PAD + 256], ACT.Copy,
                               scale=conv_w[:, 2, i % 2, PAD:PAD + 1]).then_inc(s["a_tap"], 1)

            def a_silu(b, i):
                act.wait_ge(s["a_conv"], b * 24 + 3 * i + 3)
                act.wait_ge(s["a_win"], b * 8)
                act.activation(vT[:, i % 2, C + 256 * (i // 2):C + 256 * (i // 2) + 256], cva[:, i % 2, :],
                               ACT.Silu).then_inc(s["a_vT"], 1)

            def a_win_out(b, i):
                act.wait_ge(s["a_vb"], b * 16 + 2 * i + 2)
                act.activation(vwin[:, P * (i % 2):P * (i % 2) + P, bass.ds(b * N + 4 * (i // 2), 4)],
                               bank[4 + i % 2][:, :].rearrange("p (k c) -> p c k", k=4), ACT.Copy).then_inc(s["a_win_out"], 1)

            def sequence(b):
                a_xT_out(b, 0)
                a_xT_out(b, 1)
                for q in range(4):
                    a_tap(b, 2 * q)
                    a_tap(b, 2 * q + 1)
                    if q < 2:
                        a_xT_out(b, q + 2)
                    a_silu(b, 2 * q)
                    a_silu(b, 2 * q + 1)
                    if q >= 1:
                        a_win_out(b, 2 * q - 2)
                        a_win_out(b, 2 * q - 1)
                a_win_out(b, 6)
                a_win_out(b, 7)

            sequence(0)
            with act.Fori(1, B) as b:
                sequence(b)

            act.activation(inv_temp[:, :], inv_temp[:, :], ACT.Exp, scale=-1.0).then_inc(s["g_exp"], 1)
            act.wait_ge(s["a_gate_out"], 8 * B)
            act.activation(gates[:, 5], gates[:, 5], ACT.Tanh, scale=0.5).then_inc(s["g_exp"], 1)
            act.wait_ge(s["g_step"], G_SHIFTED)
            act.activation(gates[:, 0:5], gates[:, 0:5], ACT.Exp).then_inc(s["g_exp"], 1)

            act.wait_ge(s["fir_mm"], 12 * FG)
            act.wait_ge(s["bd_zero"], 1)

            def tap(n, t):
                act.wait_ge(s["proj"], n * 4 + t + 1)
                act.wait_ge(s["silu"], n * 4)
                act.activation(cv[:, t], bank[t % 2][:, 0:B * (C + PAD)].rearrange("p (b t) -> p b t", b=B)[:, :, PAD:],
                               ACT.Copy, scale=conv_w[:, 1 - t // 2, t % 2, PAD:PAD + 1]).then_inc(s["tap"], 1)

            def silu(n, t):
                kind, g = t // 2, t % 2
                act.wait_ge(s["conv"], n * 12 + 3 * t + 3)
                act.wait_ge(s["gram_k" if kind == 0 else "gram_q"], n * 1)
                if kind == 0:
                    act.wait_ge(s["gram_q"], n * 1)
                    act.wait_ge(s["ktr"], n * 2)
                else:
                    act.wait_ge(s["omm"], n * 1)
                act.wait_ge(s["square"], n * 4)
                for hh in range(2):
                    act.activation((kT_bd, qT_bd)[kind][HH[hh], grp(g), HH[hh]], cv[HH[hh], t], ACT.Silu).then_inc(s["bd"], 1)
                act.activation(kq[:, grp(g), kind, :], cv[:, t], ACT.Silu).then_inc(s["silu"], 1)

            def square(n, t):
                kind, g = t // 2, t % 2
                act.wait_ge(s["bd"], n * 8 + 2 * t + 2)
                act.wait_ge(s["sumsq_k" if kind == 0 else "sumsq_q"], n * 1)
                act.activation(sq[:, U * kind + G4 * g:U * kind + G4 * g + G4, :], (kT_bd, qT_bd)[kind][:, grp(g)],
                               ACT.Square).then_inc(s["square"], 1)

            def blocks(dst, src, g, done, scale=1.0):
                for hh in range(2):
                    act.activation(dst[HH[hh], grp(g), HH[hh]], src[HH[hh]], ACT.Copy, scale=scale).then_inc(done, 1)

            def mbd_out(n, g):
                act.wait_ge(s["mc"], n * 2 + g + 1)
                act.wait_ge(s["mm1"], n * 2 * NL)
                blocks(M_bd, Mc[:, grp(g)], g, s["mbd"])

            def xbd0_out(n, g):
                act.wait_ge(s["x2"], n * 4 + 2 * g + 2)
                act.wait_ge(s["mm2"], n * 2 * NL)
                blocks(X_bd, X2[:, grp(g)], g, s["xbd0"])

            def zbd_out(n, g):
                act.wait_ge(s["z"], n * 12 + 10 + g + 1)
                act.wait_ge(s["umm"], n * 1)
                blocks(Z_bd, Z[:, padded(g)], g, s["zbd"])

            def kbd_out(n, g):
                act.wait_ge(s["state"], n * 1)
                act.wait_ge(s["ktr"], n * 2 + g + 1)
                act.activation(k_bd[:, grp(g), :], units(bank[g][:, :], P), ACT.Copy).then_inc(s["kbd"], 1)

            def wbd_out(n, g):
                act.wait_ge(s["umm"], n * 1)
                act.wait_ge(s["wmm"], n * 2 + g + 1)
                blocks(wT_bd, units(bank[2 + g][:, 0:256]), g, s["wbd"], scale=-1.0)

            def u_out(n):
                act.wait_ge(s["umm"], n * 1 + 1)
                act.activation(ut, units(bank[4][:, :]), ACT.Copy).then_inc(s["ut"], 1)

            def state_out(n):
                act.wait_ge(s["state"], n * 1 + 1)
                act.wait_ge(s["omm"], n * 1 + 1)
                act.activation(S, units(bank[7][:, :]), ACT.Copy).then_inc(s["S"], 1)

            def o_square(n):
                act.wait_ge(s["o2"], n * 1 + 1)
                act.activation(osq, o2, ACT.Square).then_inc(s["osq"], 1)

            def oT_out(n):
                act.wait_ge(s["oT_mm"], n * 1 + 1)
                act.activation(oT, units(bank[4][:, :]), ACT.Copy, scale=norm_w[:, 0:1]).then_inc(s["oT"], 1)

            def xf_out(n):
                act.wait_ge(s["xT"], n * 1 + 1)
                act.wait_ge(s["halo"], n * 1 + 1)
                for hf in range(HALVES):
                    act.activation(xf[:, hf, :, 1:], bank[4][:, 256 * hf:256 * hf + 256].rearrange("p (b t) -> p b t", b=B),
                                   ACT.Copy).then_inc(s["xf"], 1)

            def k_relu(n):
                act.wait_ge(s["kmm"], n * 1 + 1)
                act.wait_ge(s["ka"], n * 1)
                act.activation(rl, bank[5][:, :].rearrange("p (h t) -> p h t", h=2), ACT.Relu).then_inc(s["rl"], 1)

            def k_square(n):
                act.wait_ge(s["rl"], n * 1 + 1)
                act.wait_ge(s["vmm"], n * 1)
                act.activation(ka, rl, ACT.Square).then_inc(s["ka"], 1)

            def r_tanh(n):
                act.wait_ge(s["rmm"], n * 1 + 1)
                act.wait_ge(s["f2"], n * 1)
                act.activation(th, bank[6][:, :].rearrange("p (j c) -> p j c", j=2), ACT.Tanh, scale=0.5).then_inc(s["th"], 1)

            tap(0, 0)
            tap(0, 1)
            silu(0, 0)
            square(0, 0)
            silu(0, 1)
            tap(0, 2)
            square(0, 1)
            silu(0, 2)
            tap(0, 3)
            square(0, 2)
            kbd_out(0, 0)
            mbd_out(0, 0)
            xbd0_out(0, 0)
            mbd_out(0, 1)
            silu(0, 3)
            xbd0_out(0, 1)
            square(0, 3)
            kbd_out(0, 1)
            zbd_out(0, 0)
            wbd_out(0, 0)
            wbd_out(0, 1)
            zbd_out(0, 1)

            def chunk_step(n):
                tap(n + 1, 0)
                tap(n + 1, 1)
                u_out(n)
                silu(n + 1, 0)
                square(n + 1, 0)
                silu(n + 1, 1)
                o_square(n)
                tap(n + 1, 2)
                square(n + 1, 1)
                silu(n + 1, 2)
                tap(n + 1, 3)
                square(n + 1, 2)
                oT_out(n)
                kbd_out(n + 1, 0)
                mbd_out(n + 1, 0)
                xbd0_out(n + 1, 0)
                mbd_out(n + 1, 1)
                silu(n + 1, 3)
                xbd0_out(n + 1, 1)
                square(n + 1, 3)
                xf_out(n)
                kbd_out(n + 1, 1)
                state_out(n)
                zbd_out(n + 1, 0)
                k_relu(n)
                k_square(n)
                r_tanh(n)
                wbd_out(n + 1, 0)
                wbd_out(n + 1, 1)
                zbd_out(n + 1, 1)

            chunk_step(0)
            with act.Fori(1, N - 1) as n:
                chunk_step(n)
            n = N - 1
            u_out(n)
            o_square(n)
            oT_out(n)
            xf_out(n)
            state_out(n)
            k_relu(n)
            k_square(n)
            r_tanh(n)

        @block.vector
        def _(dve):
            dve.wait_ge(s["weights_in"], 16 * N_W)
            dve.wait_ge(s["consts_in"], 16)

            def a_norm(b):
                dve.wait_ge(s["xa_in"], b * 16 + 16)
                dve.wait_ge(s["a_normed"], b * 8)
                for m in range(M_TILES):
                    last = nc.vector.bn_stats(stats_a[:, m, :], xa[:, m, :])
                last.then_inc(s["a_stats"], 1)
                dve.wait_ge(s["a_stats"], b * 3 + 1)
                alone(dve)
                for m in range(M_TILES):
                    last = nc.vector.bn_aggr(mv_a[:, m, :], stats_a[:, m, :])
                last.then_inc(s["a_stats"], 1)
                dve.wait_ge(s["a_stats"], b * 3 + 2)
                nc.vector.tensor_scalar(ve_a[:, :].rearrange("p (m o) -> p m o", o=1), mv_a[:, :, 1:2], EPS, None,
                                        ALU.add).then_inc(s["a_stats"], 1)
                dve.wait_ge(s["a_rs"], b * 1 + 1)
                dve.wait_ge(s["a_xT"], b * 4)
                for m in range(M_TILES):
                    nc.vector.tensor_scalar(xna[:, m, :], xa[:, m, :], mv_a[:, m, 0:1], rs_a[:, m:m + 1],
                                            ALU.subtract, ALU.mult).then_inc(s["a_normed"], 1)

            def a_conv(b, i):
                for j in range(PAD):
                    if j == 0:
                        dve.wait_ge(s["a_tap"], b * 8 + i + 1)
                    else:
                        dve.wait_ge(s["a_conv"], b * 24 + 3 * i + j)
                    nc.vector.scalar_tensor_tensor(cva[:, i % 2, :], bank[2 + i % 2][:, j:j + 256],
                                                   conv_w[:, 2, i % 2, j:j + 1], cva[:, i % 2, :],
                                                   ALU.mult, ALU.add).then_inc(s["a_conv"], 1)

            def a_vb(b, i):
                q, pr = i // 2, i % 2
                dve.wait_ge(s["a_win"], b * 8 + i + 1)
                dve.wait_ge(s["a_vb_stored"], b * 32)
                for hh in range(2):
                    nc.vector.tensor_copy(vb[HH[hh], 4 * q:4 * q + 4, pr, :],
                                          units(bank[4 + pr][64:128, :], P)[:, :, HH[hh]]).then_inc(s["a_vb"], 1)

            def a_gates(b):
                dve.wait_ge(s["a_gate"], b * 1 + 1)
                dst = gates.rearrange("p g r (b m two) -> p b g r m two", b=B, two=2)
                for par in range(2):
                    src = bank[6][HH[par], 0:M_TILES * H * NG].rearrange("p (m h g) -> p h g m", h=H, g=NG)
                    for hh in range(2):
                        for pr in range(PAIRS):
                            nc.vector.tensor_copy(dst[HH[hh], b, :, pr, :, par], src[:, 2 * pr + hh]).then_inc(s["a_gate_out"], 1)

            def sequence(b):
                a_norm(b)
                for q in range(4):
                    a_conv(b, 2 * q)
                    a_conv(b, 2 * q + 1)
                    if q >= 1:
                        a_vb(b, 2 * q - 2)
                        a_vb(b, 2 * q - 1)
                a_vb(b, 6)
                a_vb(b, 7)
                a_gates(b)

            sequence(0)
            with dve.Fori(1, B) as b:
                sequence(b)

            steps = [0]

            def then(ins):
                steps[0] += 1
                ins.then_inc(s["g_step"], 1)
                dve.wait_ge(s["g_step"], steps[0])

            mixing = gates[:, 0:5]
            mx4 = gmax[:, :, :].rearrange("p r (w o) -> p o r w", o=1).broadcast_to((P, 5, PAIRS, BLK))
            dve.wait_ge(s["a_gate_out"], 8 * B)
            dve.wait_ge(s["g_exp"], 1)
            then(nc.vector.tensor_scalar(mix_eps[:, :], mix_eps[:, :], 0.0, 0.2, ALU.max, ALU.min))
            then(nc.vector.tensor_scalar(mix_scale[:, :], mix_eps[:, :], -5.0, 1.0, ALU.mult, ALU.add))
            for g in range(5):
                for pr in range(PAIRS):
                    last = nc.vector.tensor_scalar(gates[:, g, pr, :], gates[:, g, pr, :], gb[:, pr, g:g + 1],
                                                   inv_temp[:, pr:pr + 1], ALU.add, ALU.mult)
            then(last)
            then(nc.vector.tensor_reduce(gmax[:, :, :], mixing.rearrange("p g r w -> p r w g"), AX, ALU.max))
            then(nc.vector.tensor_tensor(mixing, mixing, mx4, ALU.subtract))
            assert steps[0] == G_SHIFTED
            dve.wait_ge(s["g_exp"], 3)
            then(nc.vector.tensor_reduce(gmax[:, :, :], mixing.rearrange("p g r w -> p r w g"), AX, ALU.add))
            then(nc.vector.reciprocal(gmax[:, :, :], gmax[:, :, :]))
            for pr in range(PAIRS):
                last = nc.vector.tensor_scalar(gmax[:, pr, :], gmax[:, pr, :], mix_scale[:, pr:pr + 1], None, ALU.mult)
            then(last)
            then(nc.vector.tensor_tensor(mixing, mixing, mx4, ALU.mult))
            for pr in range(PAIRS):
                last = nc.vector.tensor_scalar(mixing[:, :, pr, :], mixing[:, :, pr, :], mix_eps[:, pr:pr + 1], None, ALU.add)
            then(last)
            then(nc.vector.tensor_scalar(gates[:, 5], gates[:, 5], 0.5, 0.5, ALU.mult, ALU.add))
            assert steps[0] == G_STEPS

            dve.wait_ge(s["bd_zero"], 1)
            for g in range(FG):
                for f in range(3):
                    wt = gates[:, 2 - f, g // 2, :].rearrange("p (o w) -> p o w", o=1).broadcast_to((P, 8, BLK))
                    for j in range(4):
                        k = 12 * g + 4 * f + j
                        q = 8 * g + 4 * (f - 1) + j
                        dve.wait_ge(s["fir_mm"], k + 1)
                        if f == 0:
                            dst = fir[:, 32 * (g % 2) + 8 * j:32 * (g % 2) + 8 * j + 8, g // 2, :]
                        else:
                            dst = fprod[:, q % 2, :].rearrange("p (c w) -> p c w", w=BLK)
                            if q >= 2:
                                dve.wait_ge(s["fir_sum"], q - 1)
                        nc.vector.tensor_tensor(dst, bank[k % 8][:, :].rearrange("p (c w) -> p c w", w=BLK), wt,
                                                ALU.mult).then_inc(s["fir_prod"], 1)

            dve.wait_ge(s["fir_mm"], 12 * FG)
            dve.wait_ge(s["bd_zero"], 1)
            dve.wait_ge(s["pad_zero"], 2)

            def changed(ap, l):
                size = LEVELS[l]
                if size == C // 2:
                    return ap[:, :, size:]
                return ap.rearrange("p u (k two s) -> p u k two s", two=2, s=size)[:, :, :, 1]

            def over(ap, u=G4):
                return ap.rearrange("p (o k) -> p o k", o=1).broadcast_to((ap.shape[0], u, C))

            def per_row(ap, g=None):
                v = ap.rearrange("p a (u o) -> p (a u) o", o=1)
                return v.broadcast_to((P, U, C)) if g is None else v[:, grp(g)].broadcast_to((P, G4, C))

            def conv(n, t):
                ps = bank[t % 2][:, 0:B * (C + PAD)].rearrange("p (b t) -> p b t", b=B)
                for j in range(PAD):
                    if j == 0:
                        dve.wait_ge(s["tap"], n * 4 + t + 1)
                    else:
                        dve.wait_ge(s["conv"], n * 12 + 3 * t + j)
                    nc.vector.scalar_tensor_tensor(cv[:, t], ps[:, :, j:j + C], conv_w[:, 1 - t // 2, t % 2, j:j + 1],
                                                   cv[:, t], ALU.mult, ALU.add).then_inc(s["conv"], 1)

            def sumsq_out(n, kind):
                dve.wait_ge(s[("sumsq_k", "sumsq_q")[kind]], n * 1 + 1)
                if kind == 0:
                    dve.wait_ge(s["k_scal"], n * 3)
                else:
                    dve.wait_ge(s["q_scal"], n * 2)
                nc.vector.tensor_scalar(ssel[:, kind], bank[(3, 1)[kind]][:, 0:U], L2EPS, None,
                                        ALU.add).then_inc(s[("ssk", "ssq")[kind]], 1)

            def m_lower(n):
                dve.wait_ge(s["gram_k"], n * 1 + 1)
                dve.wait_ge(s["mc"], n * 2)
                nc.vector.tensor_tensor(Mt, units(bank[2][:, :]), over(low, U), ALU.mult).then_inc(s["mt"], 1)

            def m_scaled(n, g):
                dve.wait_ge(s["mt"], n * 1 + 1)
                dve.wait_ge(s["k_scal"], n * 3 + 3)
                dve.wait_ge(s["x2"], n * 4)
                dve.wait_ge(s["mbd"], n * 4)
                nc.vector.tensor_tensor(Mc[:, grp(g)], Mt[:, grp(g)], per_row(d2, g), ALU.mult).then_inc(s["mc"], 1)

            def x_first(n, g):
                dve.wait_ge(s["mc"], n * 2 + g + 1)
                dve.wait_ge(s["z"], n * 12)
                dve.wait_ge(s["xbd0"], n * 4)
                nc.vector.tensor_tensor(X2[:, grp(g)], Mc[:, grp(g)], over(negpairs), ALU.mult).then_inc(s["x2"], 1)
                dve.wait_ge(s["x2"], n * 4 + 2 * g + 1)
                nc.vector.tensor_tensor(X2[:, grp(g)], X2[:, grp(g)], over(rstack), ALU.add).then_inc(s["x2"], 1)
                dve.wait_ge(s["x2"], n * 4 + 2 * g + 2)
                dve.wait_ge(s["zs"], n * 2)
                dve.wait_ge(s["zbd"], n * 4)
                nc.vector.transpose(Z[:, padded(g)], X2[:, grp(g)]).then_inc(s["z"], 1)

            def at_parts(n):
                dve.wait_ge(s["gram_q"], n * 1 + 1)
                dve.wait_ge(s["omm"], n * 1)
                for hh in range(2):
                    nc.vector.tensor_tensor(atT_bd[HH[hh], :, HH[hh]], units(bank[0][HH[hh], :]),
                                            over(up[HH[hh]], U), ALU.mult).then_inc(s["at"], 1)

            def p_masked(n, l, g):
                dve.wait_ge(s["mm1"], n * 2 * NL + 2 * l + g + 1)
                nc.vector.tensor_tensor(changed(Pm[:, padded(g)], l), changed(units(bank[2 + g][:, :], P)[:, :, 0:C], l),
                                        changed(over(level_mask(l)), l), ALU.mult).then_inc(s["pm"], 1)

            def z_next(n, l, g):
                dve.wait_ge(s["mm2"], n * 2 * NL + 2 * l + g + 1)
                nc.vector.tensor_tensor(changed(Z[:, padded(g)], l), changed(Z[:, padded(g)], l),
                                        changed(units(bank[2 + g][:, :], P)[:, :, 0:C], l), ALU.subtract).then_inc(s["z"], 1)

            def x_next(n, l, g):
                dve.wait_ge(s["z"], n * 12 + 2 * (l + 1) + g + 1)
                for hh in range(2):
                    nc.vector.transpose(X_bd[HH[hh], grp(g), HH[hh]], Z[HH[hh], padded(g)]).then_inc(s["xbd"], 1)

            def z_scaled(n, g):
                dve.wait_ge(s["z"], n * 12 + 10 + g + 1)
                dve.wait_ge(s["wmm"], n * 2)
                nc.vector.tensor_tensor(Zs[:, grp(g)], Z[:, padded(g)], per_row(d2, g), ALU.mult).then_inc(s["zs"], 1)

            def o_scaled(n):
                dve.wait_ge(s["omm"], n * 1 + 1)
                dve.wait_ge(s["q_scal"], n * 2 + 2)
                dve.wait_ge(s["o2"], n * 1)
                nc.vector.tensor_tensor(o1, units(bank[5][:, :]), per_row(qs), ALU.mult).then_inc(s["o1"], 1)

            def o_summed(n):
                dve.wait_ge(s["o1"], n * 1 + 1)
                dve.wait_ge(s["ov"], n * 2 + 2)
                dve.wait_ge(s["obd"], n * 2)
                nc.vector.tensor_tensor(o2, o1, ov, ALU.add).then_inc(s["o2"], 1)

            def o_meansq(n):
                dve.wait_ge(s["osq"], n * 1 + 1)
                nc.vector.tensor_reduce(oms[:, 0], osq, AX, ALU.add).then_inc(s["oms"], 1)
                dve.wait_ge(s["oms"], n * 2 + 1)
                nc.vector.tensor_scalar(oms[:, 0], oms[:, 0], 1.0 / DK, EPS, ALU.mult, ALU.add).then_inc(s["oms"], 1)

            def o_normed(n):
                dve.wait_ge(s["ro"], n * 1 + 1)
                for hh in range(2):
                    nc.vector.tensor_tensor(o_bd[HH[hh], :, HH[hh]], o2[HH[hh]], per_row(ro)[HH[hh]], ALU.mult).then_inc(s["obd"], 1)

            def row_stats(n, i, name, src, eps, normed):
                dve.wait_ge(s[normed], n * 1)
                dve.wait_ge(s[name], n * 3)
                for j in range(2):
                    last = nc.vector.bn_stats(bn[:, i, j, :], src[:, j, :])
                last.then_inc(s[name], 1)
                dve.wait_ge(s[name], n * 3 + 1)
                alone(dve)
                for j in range(2):
                    last = nc.vector.bn_aggr(mv[:, i, j, :], bn[:, i, j, :])
                last.then_inc(s[name], 1)
                dve.wait_ge(s[name], n * 3 + 2)
                nc.vector.tensor_scalar(ve[:, i].rearrange("p (j o) -> p j o", o=1), mv[:, i, :, 1:2], eps, None,
                                        ALU.add).then_inc(s[name], 1)

            def row_norm(n, i, dst, src, name):
                for j in range(2):
                    last = nc.vector.tensor_scalar(dst[:, j, :], src[:, j, :], mv[:, i, j, 0:1], rs[:, i, j:j + 1],
                                                   ALU.subtract, ALU.mult)
                last.then_inc(s[name], 1)

            def y_stats(n):
                dve.wait_ge(s["ymm"], n * 1 + 1)
                row_stats(n, 0, "st1", bank[5][:, :].rearrange("p (j c) -> p j c", j=2), EPS, "t1")

            def residual(n):
                dve.wait_ge(s["r1"], n * 1 + 1)
                dve.wait_ge(s["x1"], n * 1)
                row_norm(n, 0, t1, bank[5][:, :].rearrange("p (j c) -> p j c", j=2), "t1")
                dve.wait_ge(s["t1"], n * 1 + 1)
                dve.wait_ge(s["x_in"], n * 64 + 64)
                dve.wait_ge(s["y_out"], n * 1)
                nc.vector.tensor_tensor(x1, t1, x_in, ALU.add).then_inc(s["x1"], 1)

            def x_stats(n):
                dve.wait_ge(s["x1"], n * 1 + 1)
                row_stats(n, 1, "st2", x1, EPS, "xn2")

            def x_normed(n):
                dve.wait_ge(s["r2"], n * 1 + 1)
                row_norm(n, 1, xn2, x1, "xn2")

            def shifted(n):
                dve.wait_ge(s["xf"], n * 2 + 2)
                dve.wait_ge(s["mix"], n * 4)
                for hf in range(HALVES):
                    nc.vector.tensor_tensor(dx[:, hf].rearrange("p (b t) -> p b t", b=B), xf[:, hf, :, 1:],
                                            xf[:, hf, :, 0:C], ALU.subtract).then_inc(s["dx"], 1)

            def mix(n, i, dst):
                dve.wait_ge(s["dx"], n * 2 + 2)
                dve.wait_ge(s["kmm"], n * 1)
                dve.wait_ge(s["rmm"], n * 1)
                for hf in range(HALVES):
                    nc.vector.scalar_tensor_tensor(dst[:, hf].rearrange("p (b t) -> p b t", b=B),
                                                   dx[:, hf].rearrange("p (b t) -> p b t", b=B), mu[:, i, hf:hf + 1],
                                                   xf[:, hf, :, 0:C], ALU.mult, ALU.add).then_inc(s["mix"], 1)

            def ffn_out(n):
                dve.wait_ge(s["vmm"], n * 1 + 1)
                dve.wait_ge(s["th"], n * 1 + 1)
                dve.wait_ge(s["t3"], n * 1)
                nc.vector.scalar_tensor_tensor(f2, th, 1.0, bank[6][:, :].rearrange("p (j c) -> p j c", j=2),
                                               ALU.add, ALU.mult).then_inc(s["f2"], 1)

            def f_stats(n):
                dve.wait_ge(s["f2"], n * 1 + 1)
                row_stats(n, 2, "st3", f2, 4 * EPS, "t3")

            def f_normed(n):
                dve.wait_ge(s["r3"], n * 1 + 1)
                dve.wait_ge(s["y_out"], n * 1)
                row_norm(n, 2, t3, f2, "t3")

            conv(0, 0)
            conv(0, 1)
            conv(0, 2)
            sumsq_out(0, 0)
            m_lower(0)
            conv(0, 3)
            m_scaled(0, 0)
            m_scaled(0, 1)
            x_first(0, 0)
            x_first(0, 1)
            p_masked(0, 0, 0)
            z_next(0, 0, 0)
            p_masked(0, 0, 1)
            x_next(0, 0, 0)
            p_masked(0, 1, 0)
            z_next(0, 0, 1)
            x_next(0, 0, 1)
            p_masked(0, 1, 1)
            z_next(0, 1, 0)
            z_next(0, 1, 1)
            p_masked(0, 2, 0)
            x_next(0, 1, 0)
            p_masked(0, 2, 1)
            x_next(0, 1, 1)
            z_next(0, 2, 0)
            x_next(0, 2, 0)
            p_masked(0, 3, 0)
            z_next(0, 2, 1)
            x_next(0, 2, 1)
            z_next(0, 3, 0)
            x_next(0, 3, 0)
            p_masked(0, 3, 1)
            p_masked(0, 4, 0)
            sumsq_out(0, 1)
            z_next(0, 3, 1)
            z_next(0, 4, 0)
            z_scaled(0, 0)
            x_next(0, 3, 1)
            p_masked(0, 4, 1)
            at_parts(0)
            z_next(0, 4, 1)
            z_scaled(0, 1)

            def chunk_step(n):
                conv(n + 1, 0)
                conv(n + 1, 1)
                o_scaled(n)
                o_summed(n)
                o_meansq(n)
                conv(n + 1, 2)
                sumsq_out(n + 1, 0)
                m_lower(n + 1)
                o_normed(n)
                conv(n + 1, 3)
                m_scaled(n + 1, 0)
                m_scaled(n + 1, 1)
                x_first(n + 1, 0)
                x_first(n + 1, 1)
                p_masked(n + 1, 0, 0)
                y_stats(n)
                z_next(n + 1, 0, 0)
                p_masked(n + 1, 0, 1)
                x_next(n + 1, 0, 0)
                residual(n)
                p_masked(n + 1, 1, 0)
                z_next(n + 1, 0, 1)
                x_stats(n)
                x_next(n + 1, 0, 1)
                p_masked(n + 1, 1, 1)
                z_next(n + 1, 1, 0)
                x_normed(n)
                z_next(n + 1, 1, 1)
                p_masked(n + 1, 2, 0)
                x_next(n + 1, 1, 0)
                p_masked(n + 1, 2, 1)
                x_next(n + 1, 1, 1)
                z_next(n + 1, 2, 0)
                shifted(n)
                x_next(n + 1, 2, 0)
                p_masked(n + 1, 3, 0)
                z_next(n + 1, 2, 1)
                mix(n, 1, xk)
                x_next(n + 1, 2, 1)
                z_next(n + 1, 3, 0)
                x_next(n + 1, 3, 0)
                p_masked(n + 1, 3, 1)
                mix(n, 0, xr)
                p_masked(n + 1, 4, 0)
                sumsq_out(n + 1, 1)
                z_next(n + 1, 3, 1)
                z_next(n + 1, 4, 0)
                z_scaled(n + 1, 0)
                x_next(n + 1, 3, 1)
                p_masked(n + 1, 4, 1)
                at_parts(n + 1)
                z_next(n + 1, 4, 1)
                z_scaled(n + 1, 1)
                ffn_out(n)
                f_stats(n)
                f_normed(n)

            chunk_step(0)
            with dve.Fori(1, N - 1) as n:
                chunk_step(n)
            n = N - 1
            o_scaled(n)
            o_summed(n)
            o_meansq(n)
            o_normed(n)
            y_stats(n)
            residual(n)
            x_stats(n)
            x_normed(n)
            shifted(n)
            mix(n, 1, xk)
            mix(n, 0, xr)
            ffn_out(n)
            f_stats(n)
            f_normed(n)

        @block.tensor
        def _(pe):
            mm = nc.tensor.matmul
            pe.wait_ge(s["consts_in"], 16)
            pe.wait_ge(s["weights_in"], 16 * N_W)

            def a_xT(b, q):
                pe.wait_ge(s["a_normed"], b * 8 + 2 * q + 2)
                pe.wait_ge(s["a_xT_out"], b * 4 + (q - 1 if q >= 1 else 0))
                for hf in range(HALVES):
                    for k in range(2):
                        last = nc.tensor.transpose(bank[q % 2][:, 256 * hf + P * k:256 * hf + P * k + P],
                                                   xna[:, 2 * q + k, P * hf:P * hf + P], ident)
                last.then_inc(s["a_xT"], 1)

            def a_proj(b, q):
                pe.wait_ge(s["a_xT_out"], b * 4 + q + 1)
                for oh in range(2):
                    i = 2 * q + oh
                    pe.wait_ge(s["a_conv"], b * 24 + (3 * (i - 1) if i >= 2 else 0))
                    for kh in range(HALVES):
                        last = mm(bank[2 + oh][:, 0:PAD + 256], w["v"][:, kh, P * oh:P * oh + P],
                                  xnT[:, kh, 256 * q:256 * q + 256 + PAD], start=(kh == 0), stop=(kh == 1))
                    last.then_inc(s["a_proj"], 1)

            def a_win(b, i):
                q, pr = i // 2, i % 2
                pe.wait_ge(s["a_vT"], b * 8 + i + 1)
                pe.wait_ge(s["a_win_out"], b * 8 + (i - 1 if i >= 2 else 0))
                pe.wait_ge(s["a_vb"], b * 16 + (2 * (i - 1) if i >= 2 else 0))
                for k in range(4):
                    at_ = C * (4 * q + k)
                    last = nc.tensor.transpose(bank[4 + pr][:, P * k:P * k + P], vT[:, pr, at_:at_ + P], ident)
                last.then_inc(s["a_win"], 1)

            def a_gate(b):
                pe.wait_ge(s["a_gate_out"], b * 8)
                for m in range(M_TILES):
                    for kh in range(HALVES):
                        last = mm(bank[6][:, H * NG * m:H * NG * (m + 1)], xnT[:, kh, PAD + P * m:PAD + P * m + P],
                                  w_gate[:, kh, :], start=(kh == 0), stop=(kh == 1))
                last.then_inc(s["a_gate"], 1)

            def sequence(b):
                a_xT(b, 0)
                a_xT(b, 1)
                a_proj(b, 0)
                a_xT(b, 2)
                a_proj(b, 1)
                a_win(b, 0)
                a_win(b, 1)
                a_xT(b, 3)
                a_proj(b, 2)
                a_win(b, 2)
                a_win(b, 3)
                a_proj(b, 3)
                a_win(b, 4)
                a_win(b, 5)
                a_gate(b)
                a_win(b, 6)
                a_win(b, 7)

            sequence(0)
            with pe.Fori(1, B) as b:
                sequence(b)

            pe.wait_ge(s["a_win_out"], 8 * B)
            pe.wait_ge(s["a_gate_out"], 8 * B)
            pe.wait_ge(s["a_conv"], 24 * B)
            pe.wait_ge(s["a_vb"], 16 * B)
            for g in range(FG):
                for f in range(3):
                    if f == 0:
                        pe.wait_ge(s["toep_l_in"], 16 * (g + 1))
                    elif f == 1:
                        pe.wait_ge(s["toep_ms_in"], 32 * (g + 1))
                    toep = toep_l if f == 0 else toep_ms[:, f - 1]
                    for j in range(4):
                        k = 12 * g + 4 * f + j
                        if k >= 8:
                            pe.wait_ge(s["fir_prod"], k - 7)
                        for hh in range(2):
                            for d in range(8):
                                c = P * (g // 2) + 64 * hh + 32 * (g % 2) + 8 * j + d
                                last = mm(bank[k % 8][HH[hh], BLK * d:BLK * d + BLK],
                                          toep[:, :, 32 * hh + 8 * j + d], vwin[:, c, :], start=True, stop=True)
                        last.then_inc(s["fir_mm"], 1)

            pe.wait_ge(s["fir_prod"], 12 * FG)
            pe.wait_ge(s["state_zero"], 1)
            for hf in range(HALVES):
                mm(bank[7][:, 256 * hf:256 * hf + 256], ident, xf[:, 0, 0:B, 0:C], start=True, stop=True)

            def proj(n, kind, g):
                if kind == 0:
                    pe.wait_ge(s["window_in"], n * 32 + 32)
                    pe.wait_ge(s["at"], n * 2)
                    pe.wait_ge(s["ssq"], n * 1)
                else:
                    pe.wait_ge(s["conv"], n * 12 + 3 * g + 3)
                for kh in range(HALVES):
                    last = mm(bank[g][:, 0:B * (C + PAD)], w["kq"[kind]][:, kh, P * g:P * g + P],
                              xwin[:, kh], start=(kh == 0), stop=(kh == 1))
                last.then_inc(s["proj"], 1)

            def sumsq(n, kind):
                pe.wait_ge(s["square"], n * 4 + 2 * kind + 2)
                if kind == 0:
                    pe.wait_ge(s["wbd"], n * 4)
                else:
                    pe.wait_ge(s["kbd"], n * 2 + 2)
                for u in range(U):
                    last = mm(bank[(3, 1)[kind]][:, u:u + 1], sq[:, U * kind + u], ones, start=True, stop=True)
                last.then_inc(s[("sumsq_k", "sumsq_q")[kind]], 1)

            def k_turn(n, g):
                pe.wait_ge(s["bd"], n * 8 + 2 * g + 2)
                pe.wait_ge(s["conv"], n * 12 + 3 * (2 + g) + 3)
                for u in range(G4):
                    last = nc.tensor.transpose(bank[g][:, P * u:P * u + P], kT_bd[:, G4 * g + u, :], ident)
                last.then_inc(s["ktr"], 1)

            def gram(n, kind):
                pe.wait_ge(s["silu"], n * 4 + 2 * kind + 2)
                if kind == 0:
                    pe.wait_ge(s["wbd"], n * 4)
                else:
                    pe.wait_ge(s["kbd"], n * 2 + 1)
                for u in range(U):
                    last = mm(bank[(2, 0)[kind]][:, C * u:C * u + C], kT_bd[:, u, :], kq[:, u, kind],
                              start=True, stop=True)
                last.then_inc(s[("gram_k", "gram_q")[kind]], 1)

            def mz(n, l, g):
                pe.wait_ge(s["z"], n * 12 + 2 * l + g + 1)
                if l == 0:
                    pe.wait_ge(s["mbd"], n * 4 + 2 * g + 2)
                    pe.wait_ge(s["mt"], n * 1 + 1)
                    pe.wait_ge(s["ssk"], n * 1 + 1)
                for u in range(G4):
                    last = mm(bank[2 + g][:, P * u:P * u + P], M_bd[:, G4 * g + u, :],
                              Z[:, G5 * g + u:G5 * g + u + 2, :], start=True, stop=True)
                last.then_inc(s["mm1"], 1)

            def zp(n, l, g):
                pe.wait_ge(s["pm"], n * 2 * NL + 2 * l + g + 1)
                if l == 0:
                    pe.wait_ge(s["xbd0"], n * 4 + 2 * g + 2)
                else:
                    pe.wait_ge(s["xbd"], n * 4 * (NL - 1) + 4 * (l - 1) + 2 * g + 2)
                for u in range(G4):
                    last = mm(bank[2 + g][:, P * u:P * u + P], X_bd[:, G4 * g + u, :],
                              Pm[:, G5 * g + u:G5 * g + u + 2, :], start=True, stop=True)
                last.then_inc(s["mm2"], 1)

            def w_rows(n, g):
                pe.wait_ge(s["zs"], n * 2 + g + 1)
                pe.wait_ge(s["kbd"], n * 2 + 2)
                for u in range(G4):
                    last = mm(bank[2 + g][:, C * u:C * u + C], k_bd[:, G4 * g + u, :], Zs[:, G4 * g + u, :],
                              start=True, stop=True)
                last.then_inc(s["wmm"], 1)

            def scan_u(n):
                pe.wait_ge(s["zbd"], n * 4 + 4)
                pe.wait_ge(s["vp"], n * 1 + 1)
                pe.wait_ge(s["wbd"], n * 4 + 4)
                pe.wait_ge(s["S"], n * 1 + 1)
                pe.wait_ge(s["xf"], n * 2)
                for u in range(U):
                    mm(bank[4][:, C * u:C * u + C], Z_bd[:, u, :], vp[:, u, :], start=True, stop=False)
                    last = mm(bank[4][:, C * u:C * u + C], wT_bd[:, u, :], S[:, u, :], start=False, stop=True)
                last.then_inc(s["umm"], 1)

            def scan_state(n):
                pe.wait_ge(s["ut"], n * 1 + 1)
                for u in range(U):
                    last = mm(bank[7][:, C * u:C * u + C], k_bd[:, u, :], ut[:, u, :], start=False, stop=False,
                              skip_group_check=True)
                last.then_inc(s["state"], 1)

            def scan_o(n):
                pe.wait_ge(s["bd"], n * 8 + 8)
                pe.wait_ge(s["at"], n * 2 + 2)
                pe.wait_ge(s["ut"], n * 1 + 1)
                pe.wait_ge(s["S"], n * 1 + 1)
                pe.wait_ge(s["rl"], n * 1)
                for u in range(U):
                    mm(bank[5][:, C * u:C * u + C], qT_bd[:, u, :], S[:, u, :], start=True, stop=False)
                    last = mm(bank[5][:, C * u:C * u + C], atT_bd[:, u, :], ut[:, u, :], start=False, stop=True)
                last.then_inc(s["omm"], 1)

            def o_turn(n):
                pe.wait_ge(s["obd"], n * 2 + 2)
                for u in range(U):
                    last = mm(bank[4][:, C * u:C * u + C], o_bd[:, u, :], rstack, start=True, stop=True)
                last.then_inc(s["oT_mm"], 1)

            def tokens(lhs, wt, dst, k_first=0):
                for j in range(2):
                    for kh in range(HALVES):
                        last = mm(dst[:, 256 * j:256 * j + 256], lhs[:, kh, P * j:P * j + P], wt[:, kh, :],
                                  start=(kh == 0), stop=(kh == 1))
                return last

            def y_rows(n):
                pe.wait_ge(s["oT"], n * 1 + 1)
                pe.wait_ge(s["o1"], n * 1 + 1)
                tokens(oT.rearrange("p (r b) t -> p r (b t)", r=PAIRS), w["o"], bank[5]).then_inc(s["ymm"], 1)

            def x_turn(n):
                pe.wait_ge(s["xn2"], n * 1 + 1)
                pe.wait_ge(s["oT"], n * 1 + 1)
                for hf in range(HALVES):
                    for j in range(2):
                        last = nc.tensor.transpose(bank[4][:, 256 * hf + P * j:256 * hf + P * j + P],
                                                   xn2[:, j, P * hf:P * hf + P], ident)
                last.then_inc(s["xT"], 1)

            def ffn_k(n):
                pe.wait_ge(s["mix"], n * 4 + 2)
                pe.wait_ge(s["t1"], n * 1 + 1)
                for oh in range(2):
                    for kh in range(HALVES):
                        last = mm(bank[5][:, 256 * oh:256 * oh + 256], w["fk"][:, kh, P * oh:P * oh + P], xk[:, kh, :],
                                  start=(kh == 0), stop=(kh == 1))
                last.then_inc(s["kmm"], 1)

            def ffn_r(n):
                pe.wait_ge(s["mix"], n * 4 + 4)
                pe.wait_ge(s["f2"], n * 1)
                tokens(xr, w["r"], bank[6]).then_inc(s["rmm"], 1)

            def ffn_v(n):
                pe.wait_ge(s["ka"], n * 1 + 1)
                pe.wait_ge(s["th"], n * 1 + 1)
                tokens(ka, w["fv"], bank[6]).then_inc(s["vmm"], 1)

            proj(0, 0, 0)
            proj(0, 0, 1)
            proj(0, 1, 0)
            gram(0, 0)
            sumsq(0, 0)
            proj(0, 1, 1)
            k_turn(0, 0)
            mz(0, 0, 0)
            mz(0, 0, 1)
            zp(0, 0, 0)
            mz(0, 1, 0)
            zp(0, 0, 1)
            zp(0, 1, 0)
            mz(0, 1, 1)
            k_turn(0, 1)
            gram(0, 1)
            zp(0, 1, 1)
            mz(0, 2, 0)
            mz(0, 2, 1)
            zp(0, 2, 0)
            zp(0, 2, 1)
            mz(0, 3, 0)
            sumsq(0, 1)
            zp(0, 3, 0)
            mz(0, 3, 1)
            mz(0, 4, 0)
            zp(0, 3, 1)
            zp(0, 4, 0)
            mz(0, 4, 1)
            zp(0, 4, 1)
            w_rows(0, 0)
            w_rows(0, 1)

            def chunk_step(n):
                proj(n + 1, 0, 0)
                proj(n + 1, 0, 1)
                scan_u(n)
                scan_o(n)
                proj(n + 1, 1, 0)
                gram(n + 1, 0)
                sumsq(n + 1, 0)
                proj(n + 1, 1, 1)
                k_turn(n + 1, 0)
                scan_state(n)
                o_turn(n)
                y_rows(n)
                mz(n + 1, 0, 0)
                mz(n + 1, 0, 1)
                zp(n + 1, 0, 0)
                mz(n + 1, 1, 0)
                zp(n + 1, 0, 1)
                zp(n + 1, 1, 0)
                mz(n + 1, 1, 1)
                k_turn(n + 1, 1)
                gram(n + 1, 1)
                zp(n + 1, 1, 1)
                mz(n + 1, 2, 0)
                x_turn(n)
                mz(n + 1, 2, 1)
                zp(n + 1, 2, 0)
                zp(n + 1, 2, 1)
                mz(n + 1, 3, 0)
                sumsq(n + 1, 1)
                zp(n + 1, 3, 0)
                mz(n + 1, 3, 1)
                ffn_k(n)
                mz(n + 1, 4, 0)
                zp(n + 1, 3, 1)
                zp(n + 1, 4, 0)
                mz(n + 1, 4, 1)
                ffn_r(n)
                zp(n + 1, 4, 1)
                w_rows(n + 1, 0)
                ffn_v(n)
                w_rows(n + 1, 1)

            chunk_step(0)
            with pe.Fori(1, N - 1) as n:
                chunk_step(n)
            n = N - 1
            scan_u(n)
            scan_o(n)
            scan_state(n)
            o_turn(n)
            y_rows(n)
            x_turn(n)
            ffn_k(n)
            ffn_r(n)
            ffn_v(n)


def constants():
    import numpy as np

    c = np.zeros((P, NCONST), np.float32)
    i = np.arange(P) % C
    j = np.arange(C)
    c[:, C_ID:C_ID + P] = np.eye(P)
    c[:, C_R:C_R + C] = i[:, None] == j[None, :]
    c[:, C_LOW:C_LOW + C] = i[:, None] > j[None, :]
    c[:, C_UP:C_UP + C] = i[:, None] <= j[None, :]
    c[:, C_NM1:C_NM1 + C] = -1.0 * ((i[:, None] // 2 == j[None, :] // 2) & (i[:, None] > j[None, :]))
    for l, size in enumerate(LEVELS):
        same = i[:, None] // (2 * size) == j[None, :] // (2 * size)
        c[:, C_LV + C * l:C_LV + C * (l + 1)] = same & (i[:, None] // size % 2 == 0) & (j[None, :] // size % 2 == 1)
    c[:, C_ONE] = 1.0
    return c


def kernel(**inputs):
    import numpy as np
    import concourse.bacc as bacc
    from concourse.bass_utils import run_bass_kernel_spmd

    g = {k[3:]: np.asarray(v) for k, v in inputs.items()}
    order = np.arange(D).reshape(PAIRS, 2, 2, 32).transpose(0, 2, 1, 3).reshape(D)

    def padded(f):
        taps = f.reshape(D, -1)[order].T
        rows = np.zeros((ROWS, D), f.dtype)
        rows[P - taps.shape[0]:P] = taps
        return rows.reshape(ROWS, FG, GC).transpose(1, 0, 2)

    def per_head(v):
        return np.repeat(v.reshape(PAIRS, 2, -1).transpose(1, 0, 2).reshape(2, -1), C, axis=0)

    arrays = {
        "x": g["attn_hidden_states"],
        "wgate": np.concatenate([g["attn_gate_w"], g["attn_Wb"][:, None, :]], axis=1).reshape(H * NG, D).T,
        "consts": constants(),
        "wq": g["attn_Wq"].T, "wk": g["attn_Wk"].T, "wv": g["attn_Wv"].T, "wo": g["attn_Wo"].T,
        "wr": g["ffn_W_r"].T, "wfk": g["ffn_W_k"].T, "wfv": g["ffn_W_v"].T,
        "smalls": np.concatenate([
            *(g[k].reshape(HALVES, P, TAPS).transpose(1, 0, 2).reshape(P, -1) for k in ("attn_conv_q", "attn_conv_k", "attn_conv_v")),
            *(g[k].reshape(HALVES, P).T for k in ("ffn_mu_r", "ffn_mu_k")),
            np.tile(g["attn_norm_w"], 2)[:, None],
            *(per_head(g[k]) for k in ("attn_gate_b", "attn_log_temp", "attn_eps_param"))], axis=1),
        "fl": padded(g["attn_fir_l"]),
        "fms": np.stack([padded(g["attn_fir_m"]), padded(g["attn_fir_s"])]),
    }
    arrays = {k: np.ascontiguousarray(v) for k, v in arrays.items()}
    nc = bacc.Bacc("TRN2", target_bir_lowering=False, num_devices=1)
    a = {k: nc.dram_tensor(k, v.shape, F32, kind="ExternalInput").ap() for k, v in arrays.items()}
    out = nc.dram_tensor("out", (B, L, D), F32, kind="ExternalOutput").ap()
    build(nc, a["x"], out, *(a[k] for k in (
        "wgate", "consts", "smalls", "wq", "wk", "wv", "wo", "wr", "wfk", "wfv", "fl", "fms")))
    r = run_bass_kernel_spmd(nc, [arrays], core_ids=[0])
    return r.results[0]["out"]
```

```python
from contextlib import ExitStack

import concourse.bass as bass
from concourse import mybir

F32 = mybir.dt.float32
ALU = mybir.AluOpType
ACT = mybir.ActivationFunctionType
AX = mybir.AxisListType.X

P = 128
B, L, D, H = 4, 1024, 256, 4
DK = D // H
C = 64
N = L // C
HALVES = D // P
PAIRS = H // 2
U = PAIRS * B
G4 = B
G5 = G4 + 1
BLK = B * N
TAPS = 4
PAD = TAPS - 1
LP = L + PAD
NG = 6
MS0 = 48
ROWS = 2 * P - C
LEVELS = (2, 4, 8, 16, 32)
NL = len(LEVELS)
GC = 64
FG = D // GC
EPS, L2EPS = 1e-5, 1e-6
G_SHIFTED, G_STEPS = 5, 11

C_R, C_ID, C_LOW, C_UP, C_NM1, C_HS, C_LV = 0, 64, 192, 256, 320, 384, 386
NCONST = C_LV + C * NL
NSMALL = 3 * HALVES * TAPS + 2 * HALVES + 1 + PAIRS * 5 + 2 * PAIRS


def build(nc, x, out, wgate, consts, smalls, wq, wk, wv, wo, wr, wfk, wfv, fl, fms):
    ctx = ExitStack()
    with ctx:
        def sb(name, shape):
            return ctx.enter_context(nc.sbuf_tensor(name, shape, F32))

        def sem(name):
            return ctx.enter_context(nc.semaphore(name))

        xnT_dram = nc.dram_tensor("xnT_scratch", (P, HALVES, B, LP), F32, kind="Internal").ap()
        v_dram = nc.dram_tensor("v_scratch", (N, P, U, DK), F32, kind="Internal").ap()

        cst = sb("cst", [P, NCONST])
        ident = cst[:, C_ID:C_ID + P]
        rstack = cst[:, C_R:C_R + C]
        low = cst[:, C_LOW:C_LOW + C]
        up = cst[:, C_UP:C_UP + C]
        negpairs = cst[:, C_NM1:C_NM1 + C]
        headsel = cst[:, C_HS:C_HS + 32]
        twice = cst[:, C_R:C_R + P]

        def level_mask(l):
            return cst[:, C_LV + C * l:C_LV + C * (l + 1)]

        w = {k: sb("w_" + k, [P, HALVES, D]) for k in ("q", "k", "v", "o", "r", "fk", "fv")}
        w_gate = sb("w_gate", [P, HALVES, H * NG])
        small = sb("small", [P, NSMALL])
        conv_w = small[:, 0:24].rearrange("p (i h k) -> p i h k", i=3, h=HALVES)
        mu = small[:, 24:28].rearrange("p (i h) -> p i h", i=2)
        norm_w = small[:, 28:29]
        gb = small[:, 29:39].rearrange("p (r g) -> p r g", r=PAIRS)
        inv_temp = small[:, 39:41]
        mix_eps = small[:, 41:43]
        neg_half = sb("neg_half", [P, U])
        powers = sb("powers", [P, 2, U])
        mix_scale = sb("mix_scale", [P, PAIRS])

        gates = sb("gates", [P, NG, PAIRS, BLK])
        gmax = sb("gmax", [P, PAIRS, BLK])
        fir = sb("fir", [P, DK, PAIRS, BLK])

        A_V = BLK * D
        A_T = 3 * C * GC
        arena = sb("arena", [P, A_V + A_T])
        vwin = arena[:, 0:A_V].rearrange("p (c w) -> p c w", w=BLK)
        toep_l = arena[:, A_V:A_V + C * GC].rearrange("p (t c) -> p t c", c=GC)
        toep_ms = arena[:, A_V + C * GC:A_V + A_T].rearrange("p (f t c) -> p f t c", f=2, c=GC)

        def carve(whole, at, *shape):
            n = 1
            for k in shape:
                n *= k
            view = whole[:, at[0]:at[0] + n]
            at[0] += n
            if len(shape) == 2:
                return view.rearrange("p (a b) -> p a b", b=shape[1])
            if len(shape) == 3:
                return view.rearrange("p (a b c) -> p a b c", b=shape[1], c=shape[2])
            return view

        M_TILES = L // P
        SA = 2 * M_TILES * D + HALVES * LP + HALVES * (C + L) + N * PAIRS * DK
        seq = sb("seq", [P, SA])
        sa = [0]
        xa = carve(seq, sa, M_TILES, D)
        xna = carve(seq, sa, M_TILES, D)
        xnT = carve(seq, sa, HALVES, LP)
        vT = carve(seq, sa, HALVES, C + L)
        vb = carve(seq, sa, N, PAIRS, DK)
        sc = [0]
        kT_bd, qT_bd, k_bd, atT_bd, M_bd, X_bd, Z_bd, o_bd = (carve(seq, sc, U, P) for _ in range(8))
        bd_all = seq[:, 0:sc[0]]
        fprod = carve(seq, sc, 2, 512)

        stats_a = sb("stats_a", [P, M_TILES, 6])
        mv_a = sb("mv_a", [P, M_TILES, 2])
        ve_a = sb("ve_a", [P, M_TILES])
        rs_a = sb("rs_a", [P, M_TILES])
        cva = sb("cva", [P, 2, 256])
        ac = [0]

        def take(*shape):
            return carve(arena, ac, *shape)

        xwin, v_c, cv, kq, sq = take(HALVES, B, C + PAD), take(U, DK), take(4, B, C), take(U, 2, C), take(2 * U, C)
        Mt, Mc, X2, rest = (take(U, C) for _ in range(4))
        Z, Pm = (take(2 * G5, C) for _ in range(2))
        vp, S, ut, ov, o1, o2, osq, oT = (take(U, DK) for _ in range(8))
        x_in, t1, x1, xn2, th, f2, t3, y_out = (take(2, D) for _ in range(8))
        xf = take(HALVES, B, C + 1)
        dx, xr, xk, rl, ka = (take(HALVES, B * C) for _ in range(5))
        ssel, rk = take(2, U), take(2, U)
        rr, d2, qs, oms, ro = (take(1, U) for _ in range(5))
        ss64 = take(4 * U)[0:C]
        bn, mv, ve, rs = take(3, 2, 6), take(3, 2, 2), take(3, 2), take(3, 2)
        assert ac[0] <= A_V + A_T and sc[0] <= SA

        bank = [ctx.enter_context(nc.psum_tensor(f"bank{i}", [P, 512], F32)) for i in range(8)]

        s = {n: sem(n) for n in (
            "consts_in", "weights_in", "half_set", "pads_set",
            "xa_in", "a_stats", "a_rs", "a_normed", "a_xT", "a_xT_out", "a_xT_stored", "a_proj",
            "a_tap", "a_conv", "a_vT", "a_win", "a_win_out", "a_vb", "a_vb_stored", "a_gate",
            "a_gate_out",
            "g_step", "g_exp",
            "toep_zero", "toep_l_in", "toep_ms_in", "fir_mm", "fir_prod", "fir_sum",
            "bd_zero", "state_zero", "pad_zero", "window_in", "v_in", "x_in", "proj", "tap", "conv", "silu", "square", "bd",
            "sumsq", "ss64", "both_mm", "ssel", "norms", "rate", "vp", "ov", "ktr", "kbd", "gram", "mt", "mc", "x2", "at",
            "mbd", "xbd0", "z", "mm1", "pm", "mm2", "xbd", "zbd", "ks_mm", "rest",
            "umm", "ut", "state", "omm", "S", "o1", "o2", "osq", "oms", "ro", "obd", "oT_mm", "oT",
            "ymm", "st1", "r1", "t1", "x1", "st2", "r2", "xn2", "xT", "halo", "xf", "dx", "mix",
            "rmm", "kmm", "th", "rl", "ka", "vmm", "f2", "st3", "r3", "t3", "y_out", "stored")}

        block = ctx.enter_context(nc.Block())
        x4 = x.rearrange("b (n t) c -> b n t c", t=C)
        out4 = out.rearrange("b (n t) c -> b n t c", t=C)
        UPPER = [slice(0, 32), slice(64, 96)]
        HH = [slice(0, 64), slice(64, 128)]
        N_W = 7 + 1 + 1

        def alone(eng):
            eng.nop(nofuse=True)

        def grp(g):
            return slice(G4 * g, G4 * g + G4)

        def padded(g):
            return slice(G5 * g, G5 * g + G4)

        def units(ap, k=C):
            return ap.rearrange("p (u k) -> p u k", k=k)

        @block.sync
        def _(sp):
            xam = [x[b].rearrange("(m p) c -> p m c", p=P) for b in range(B)]
            sp.dma_start(xa, xam[0]).then_inc(s["xa_in"], 16)
            sp.dma_start(cst[:, :], consts).then_inc(s["consts_in"], 16)
            for key, src in (("v", wv), ("q", wq), ("k", wk), ("o", wo), ("r", wr), ("fk", wfk), ("fv", wfv)):
                sp.dma_start(w[key][:, :, :], src.rearrange("(h p) d -> p h d", p=P)).then_inc(s["weights_in"], 16)
            sp.dma_start(w_gate[:, :, :], wgate.rearrange("(h p) d -> p h d", p=P)).then_inc(s["weights_in"], 16)
            sp.dma_start(small[:, :], smalls).then_inc(s["weights_in"], 16)

            def load_l(g):
                sp.dma_start(toep_l, runs(fl[g], 0, P)).then_inc(s["toep_l_in"], 16)

            def load_ms(g):
                for i in range(2):
                    sp.dma_start(toep_ms[MS0:P, i], runs(fms[i, g], MS0, P - MS0)).then_inc(s["toep_ms_in"], 16)

            def runs(taps, first, rows):
                return bass.AP(taps.tensor, taps.offset + (first + C - 1) * GC, [[GC, rows], [-GC, C], [1, GC]])

            x_flat = x.rearrange("b (m p) c -> p b m c", p=P)
            v_dst = v_dram.rearrange("n p (r b) d -> p r b n d", b=B)
            sp.wait_ge(s["toep_zero"], 1)
            load_l(0)
            load_ms(0)

            def xT_store(b):
                sp.wait_ge(s["a_xT_out"], b * 4 + 4)
                alone(sp)
                sp.dma_start(xnT_dram[:, :, b, :], xnT).then_inc(s["a_xT_stored"], 16)

            def v_store(b):
                sp.wait_ge(s["a_vb"], b * 16 + 16)
                alone(sp)
                for pr in range(PAIRS):
                    sp.dma_start(v_dst[:, pr, b], vb[:, :, pr, :]).then_inc(s["a_vb_stored"], 16)

            def sequence(b):
                xT_store(b)
                sp.wait_ge(s["a_normed"], b * 8 + 8)
                alone(sp)
                sp.dma_start(xa, x_flat[:, b + 1]).then_inc(s["xa_in"], 16)
                v_store(b)

            sequence(0)
            with sp.Fori(1, B - 1) as b:
                sequence(b)
            xT_store(B - 1)
            v_store(B - 1)

            for g in range(1, FG):
                sp.wait_ge(s["fir_mm"], g * 12 - 8)
                load_l(g)
                sp.wait_ge(s["fir_mm"], g * 12)
                load_ms(g)

            def window_in(n):
                sp.wait_ge(s["proj"], n * 4)
                alone(sp)
                for hf in range(HALVES):
                    sp.dma_start(xwin[:, hf], xnT_dram[:, hf, :, bass.ds(n * C, C + PAD)]).then_inc(s["window_in"], 16)

            def values_in(n):
                sp.wait_ge(s["vp"], n * 1)
                alone(sp)
                sp.wait_ge(s["ov"], n * 2)
                alone(sp)
                sp.dma_start(v_c, v_dram[n]).then_inc(s["v_in"], 16)

            def rows_in(n):
                sp.wait_ge(s["x1"], n * 1)
                alone(sp)
                for bb in range(2):
                    for j in range(2):
                        sp.dma_start(x_in[HH[bb], j, :], x4[2 * j + bb, n]).then_inc(s["x_in"], 16)

            def rows_out(n):
                sp.wait_ge(s["y_out"], n * 1 + 1)
                alone(sp)
                for bb in range(2):
                    for j in range(2):
                        sp.dma_start(out4[2 * j + bb, n], y_out[HH[bb], j, :]).then_inc(s["stored"], 16)

            sp.wait_ge(s["fir_mm"], 12 * FG)
            sp.wait_ge(s["a_xT_stored"], 16 * B)
            sp.wait_ge(s["a_vb_stored"], 32 * B)
            window_in(0)
            values_in(0)
            rows_in(0)
            window_in(1)
            values_in(1)

            def chunk_step(n):
                window_in(n + 2)
                values_in(n + 2)
                rows_in(n + 1)
                rows_out(n)

            chunk_step(0)
            with sp.Fori(1, N - 2) as n:
                chunk_step(n)
            rows_in(N - 1)
            rows_out(N - 2)
            rows_out(N - 1)
            sp.wait_ge(s["stored"], 64 * N)

        @block.gpsimd
        def _(pool):
            pool.memset(neg_half[:, :], -0.5).then_inc(s["half_set"], 1)
            pool.memset(powers[:, 0], 0.5).then_inc(s["half_set"], 1)
            pool.memset(powers[:, 1], -0.5).then_inc(s["half_set"], 1)
            pool.memset(xnT[:, :, 0:PAD], 0.0).then_inc(s["pads_set"], 1)
            pool.memset(vT[:, :, 0:C], 0.0).then_inc(s["pads_set"], 1)
            pool.memset(arena[:, A_V:A_V + A_T], 0.0).then_inc(s["toep_zero"], 1)
            half8 = neg_half[:, 0:U].rearrange("p (a u) -> p a u", a=1)
            pool.wait_ge(s["half_set"], 3)
            def sequence(b):
                pool.wait_ge(s["a_stats"], b * 3 + 3)
                pool.tensor_tensor(rs_a[:, :], ve_a[:, :], neg_half[:, 0:M_TILES], ALU.pow).then_inc(s["a_rs"], 1)

            sequence(0)
            with pool.Fori(1, B) as b:
                sequence(b)

            pool.wait_ge(s["a_win"], 8 * B)
            pool.wait_ge(s["a_gate"], B)
            pool.wait_ge(s["a_xT_stored"], 16 * B)
            pool.wait_ge(s["a_vb_stored"], 32 * B)
            pool.memset(bd_all, 0.0).then_inc(s["bd_zero"], 1)

            for g in range(FG):
                for f in range(1, 3):
                    for j in range(4):
                        q = 8 * g + 4 * (f - 1) + j
                        acc = fir[:, 32 * (g % 2) + 8 * j:32 * (g % 2) + 8 * j + 8, g // 2, :]
                        pool.wait_ge(s["fir_prod"], 12 * g + 4 * f + j + 1)
                        if f == 2:
                            pool.wait_ge(s["fir_sum"], q - 3)
                        pool.tensor_tensor(acc, acc, fprod[:, q % 2, :].rearrange("p (c w) -> p c w", w=BLK),
                                           ALU.add).then_inc(s["fir_sum"], 1)

            pool.wait_ge(s["fir_mm"], 12 * FG)
            pool.wait_ge(s["fir_sum"], 8 * FG)
            pool.wait_ge(s["g_step"], G_STEPS)
            pool.wait_ge(s["bd_zero"], 1)
            pool.memset(S, 0.0).then_inc(s["S"], 1)
            pool.memset(xf, 0.0).then_inc(s["state_zero"], 1)
            pool.memset(Z, 0.0).then_inc(s["pad_zero"], 1)
            pool.memset(Pm, 0.0).then_inc(s["pad_zero"], 1)
            pool.wait_ge(s["state_zero"], 1)

            def row_gate(g, n):
                return gates[:, g, :, :].rearrange("p r (b n) -> p (r b) n", n=N)[:, :, bass.ds(n, 1)]

            def norms(n):
                pool.wait_ge(s["ssel"], n * 2 + 2)
                pool.wait_ge(s["norms"], n * 2)
                pool.wait_ge(s["vp"], n * 1)
                pool.tensor_tensor(rk, ssel, powers[:, :, :], ALU.pow).then_inc(s["norms"], 1)
                pool.wait_ge(s["norms"], n * 2 + 1)
                pool.wait_ge(s["o1"], n * 1)
                pool.tensor_tensor(qs.rearrange("p a (u o) -> p (a u) o", o=1), row_gate(3, n),
                                   rk[:, 1].rearrange("p (u o) -> p u o", o=1), ALU.mult).then_inc(s["norms"], 1)

            def values(n):
                pool.wait_ge(s["v_in"], n * 16 + 16)
                pool.wait_ge(s["norms"], n * 2 + 1)
                pool.wait_ge(s["rest"], n * 1)
                pool.tensor_tensor(vp, v_c, rk[:, 0].rearrange("p (u o) -> p u o", o=1).broadcast_to((P, U, DK)),
                                   ALU.mult).then_inc(s["vp"], 1)

            def direct(n):
                pool.wait_ge(s["v_in"], n * 16 + 16)
                local = fir[:, :, :, :].rearrange("p d r (b n) -> p (r b) d n", n=N)[:, :, :, bass.ds(n, 1)]
                pool.wait_ge(s["o2"], n * 1)
                pool.tensor_tensor(ov, v_c, row_gate(4, n).broadcast_to((P, U, DK)), ALU.mult).then_inc(s["ov"], 1)
                pool.wait_ge(s["ov"], n * 2 + 1)
                ov4 = ov.rearrange("p u (d o) -> p u d o", o=1)
                pool.tensor_tensor(ov4, ov4, local, ALU.add).then_inc(s["ov"], 1)

            def power(n, src_sem, per, dst_sem, dst, src, k):
                pool.wait_ge(s[src_sem], n * per + per)
                pool.tensor_tensor(dst, src, half8 if k == U else neg_half[:, 0:k], ALU.pow).then_inc(s[dst_sem], 1)

            def halo(n):
                pool.wait_ge(s["mix"], n * 4)
                pool.wait_ge(s["xf"], n * 2)
                alone(pool)
                pool.tensor_copy(xf[:, :, :, 0:1], xf[:, :, :, C:C + 1]).then_inc(s["halo"], 1)

            def output(n):
                pool.wait_ge(s["t3"], n * 1 + 1)
                pool.wait_ge(s["stored"], n * 64)
                pool.tensor_tensor(y_out, t3, x1, ALU.add).then_inc(s["y_out"], 1)

            direct(0)
            norms(0)
            values(0)

            def chunk_step(n):
                halo(n)
                direct(n + 1)
                power(n, "oms", 2, "ro", ro, oms, U)
                power(n, "st1", 3, "r1", rs[:, 0], ve[:, 0], 2)
                norms(n + 1)
                power(n, "st2", 3, "r2", rs[:, 1], ve[:, 1], 2)
                power(n, "st3", 3, "r3", rs[:, 2], ve[:, 2], 2)
                values(n + 1)
                output(n)

            chunk_step(0)
            with pool.Fori(1, N - 1) as n:
                chunk_step(n)
            n = N - 1
            halo(n)
            power(n, "oms", 2, "ro", ro, oms, U)
            power(n, "st1", 3, "r1", rs[:, 0], ve[:, 0], 2)
            power(n, "st2", 3, "r2", rs[:, 1], ve[:, 1], 2)
            power(n, "st3", 3, "r3", rs[:, 2], ve[:, 2], 2)
            output(n)

        @block.scalar
        def _(act):
            act.wait_ge(s["weights_in"], 16 * N_W)
            act.wait_ge(s["pads_set"], 2)

            def a_xT_out(b, q):
                act.wait_ge(s["a_xT"], b * 4 + q + 1)
                if q == 0:
                    act.wait_ge(s["a_proj"], b * 8)
                    act.wait_ge(s["a_gate"], b * 1)
                    act.wait_ge(s["a_xT_stored"], b * 16)
                act.activation(xnT[:, :, PAD + 256 * q:PAD + 256 * q + 256],
                               bank[q % 2][:, :].rearrange("p (h t) -> p h t", h=HALVES), ACT.Copy).then_inc(s["a_xT_out"], 1)

            def a_tap(b, i):
                act.wait_ge(s["a_proj"], b * 8 + i + 1)
                act.wait_ge(s["a_vT"], b * 8 + (i - 1 if i >= 2 else 0))
                act.activation(cva[:, i % 2, :], bank[2 + i % 2][:, PAD:PAD + 256], ACT.Copy,
                               scale=conv_w[:, 2, i % 2, PAD:PAD + 1]).then_inc(s["a_tap"], 1)

            def a_silu(b, i):
                act.wait_ge(s["a_conv"], b * 24 + 6 * (i // 2) + 5 + i % 2)
                act.wait_ge(s["a_win"], b * 8)
                act.activation(vT[:, i % 2, C + 256 * (i // 2):C + 256 * (i // 2) + 256], cva[:, i % 2, :],
                               ACT.Silu).then_inc(s["a_vT"], 1)

            def a_win_out(b, i):
                act.wait_ge(s["a_win"], b * 8 + i + 1)
                act.activation(vwin[:, P * (i % 2):P * (i % 2) + P, bass.ds(b * N + 4 * (i // 2), 4)],
                               bank[4 + i % 2][:, :].rearrange("p (k c) -> p c k", k=4), ACT.Copy).then_inc(s["a_win_out"], 1)

            def a_vb(b, i):
                q, pr = i // 2, i % 2
                act.wait_ge(s["a_vb_stored"], b * 32)
                act.wait_ge(s["a_win"], b * 8 + i + 1)
                for hh in range(2):
                    act.activation(vb[HH[hh], 4 * q:4 * q + 4, pr, :], units(bank[4 + pr][64:128, :], P)[:, :, HH[hh]],
                                   ACT.Copy).then_inc(s["a_vb"], 1)

            def sequence(b):
                a_xT_out(b, 0)
                a_xT_out(b, 1)
                for q in range(4):
                    a_tap(b, 2 * q)
                    a_tap(b, 2 * q + 1)
                    if q < 2:
                        a_xT_out(b, q + 2)
                    a_silu(b, 2 * q)
                    a_silu(b, 2 * q + 1)
                    if q >= 1:
                        for i in (2 * q - 2, 2 * q - 1):
                            a_win_out(b, i)
                            a_vb(b, i)
                for i in (6, 7):
                    a_win_out(b, i)
                    a_vb(b, i)

            sequence(0)
            with act.Fori(1, B) as b:
                sequence(b)

            act.activation(inv_temp[:, :], inv_temp[:, :], ACT.Exp, scale=-1.0).then_inc(s["g_exp"], 1)
            act.wait_ge(s["a_gate_out"], 8 * B)
            act.activation(gates[:, 5], gates[:, 5], ACT.Tanh, scale=0.5).then_inc(s["g_exp"], 1)
            act.wait_ge(s["g_step"], G_SHIFTED)
            act.activation(gates[:, 0:5], gates[:, 0:5], ACT.Exp).then_inc(s["g_exp"], 1)

            act.wait_ge(s["fir_mm"], 12 * FG)
            act.wait_ge(s["bd_zero"], 1)

            def tap(n, t):
                act.wait_ge(s["proj"], n * 4 + t + 1)
                act.wait_ge(s["silu"], n * 4)
                act.activation(cv[:, t], bank[t % 2][:, 0:B * (C + PAD)].rearrange("p (b t) -> p b t", b=B)[:, :, PAD:],
                               ACT.Copy, scale=conv_w[:, 1 - t // 2, t % 2, PAD:PAD + 1]).then_inc(s["tap"], 1)

            def silu(n, t):
                kind, g = t // 2, t % 2
                act.wait_ge(s["conv"], n * 12 + 3 * t + 3)
                act.wait_ge(s["gram"], n * 2)
                if kind == 0:
                    act.wait_ge(s["ktr"], n * 2)
                    act.wait_ge(s["ks_mm"], n * 1)
                else:
                    act.wait_ge(s["omm"], n * 1)
                act.wait_ge(s["square"], n * 4)
                for hh in range(2):
                    act.activation((kT_bd, qT_bd)[kind][HH[hh], grp(g), HH[hh]], cv[HH[hh], t], ACT.Silu).then_inc(s["bd"], 1)
                act.activation(kq[:, grp(g), kind, :], cv[:, t], ACT.Silu).then_inc(s["silu"], 1)

            def square(n, t):
                kind, g = t // 2, t % 2
                act.wait_ge(s["silu"], n * 4 + t + 1)
                act.wait_ge(s["sumsq"], n * 1)
                act.activation(sq[:, U * kind + G4 * g:U * kind + G4 * g + G4, :], kq[:, grp(g), kind, :],
                               ACT.Square).then_inc(s["square"], 1)

            def blocks(dst, src, g, done):
                for hh in range(2):
                    act.activation(dst[HH[hh], grp(g), HH[hh]], src[HH[hh]], ACT.Copy).then_inc(done, 1)

            def mbd_out(n, g):
                act.wait_ge(s["mc"], n * 2 + g + 1)
                act.wait_ge(s["mm1"], n * 2 * NL)
                blocks(M_bd, Mc[:, grp(g)], g, s["mbd"])

            def xbd0_out(n, g):
                act.wait_ge(s["x2"], n * 4 + 2 * g + 2)
                act.wait_ge(s["mm2"], n * 2 * NL)
                blocks(X_bd, X2[:, grp(g)], g, s["xbd0"])

            def kbd_out(n, g):
                act.wait_ge(s["state"], n * 1)
                act.wait_ge(s["ktr"], n * 2 + g + 1)
                act.activation(k_bd[:, grp(g), :], units(bank[g][:, :], P), ACT.Copy).then_inc(s["kbd"], 1)

            def u_out(n):
                act.wait_ge(s["umm"], n * 1 + 1)
                act.activation(ut, units(bank[4][:, :]), ACT.Copy).then_inc(s["ut"], 1)

            def state_out(n):
                act.wait_ge(s["state"], n * 1 + 1)
                act.wait_ge(s["omm"], n * 1 + 1)
                act.activation(S, units(bank[7][:, :]), ACT.Copy).then_inc(s["S"], 1)

            def o_square(n):
                act.wait_ge(s["o2"], n * 1 + 1)
                act.activation(osq, o2, ACT.Square).then_inc(s["osq"], 1)

            def oT_out(n):
                act.wait_ge(s["oT_mm"], n * 1 + 1)
                act.activation(oT, units(bank[4][:, :]), ACT.Copy, scale=norm_w[:, 0:1]).then_inc(s["oT"], 1)

            def xf_out(n):
                act.wait_ge(s["xT"], n * 1 + 1)
                act.wait_ge(s["halo"], n * 1 + 1)
                for hf in range(HALVES):
                    act.activation(xf[:, hf, :, 1:], bank[4][:, 256 * hf:256 * hf + 256].rearrange("p (b t) -> p b t", b=B),
                                   ACT.Copy).then_inc(s["xf"], 1)

            def k_relu(n):
                act.wait_ge(s["kmm"], n * 1 + 1)
                act.wait_ge(s["ka"], n * 1)
                act.activation(rl, bank[5][:, :].rearrange("p (h t) -> p h t", h=2), ACT.Relu).then_inc(s["rl"], 1)

            def k_square(n):
                act.wait_ge(s["rl"], n * 1 + 1)
                act.wait_ge(s["vmm"], n * 1)
                act.activation(ka, rl, ACT.Square).then_inc(s["ka"], 1)

            def r_tanh(n):
                act.wait_ge(s["rmm"], n * 1 + 1)
                act.wait_ge(s["f2"], n * 1)
                act.activation(th, bank[6][:, :].rearrange("p (j c) -> p j c", j=2), ACT.Tanh, scale=0.5).then_inc(s["th"], 1)

            tap(0, 0)
            tap(0, 1)
            silu(0, 0)
            tap(0, 2)
            silu(0, 1)
            square(0, 0)
            square(0, 1)
            tap(0, 3)
            silu(0, 2)
            silu(0, 3)
            square(0, 2)
            square(0, 3)
            kbd_out(0, 0)
            mbd_out(0, 0)
            xbd0_out(0, 0)
            mbd_out(0, 1)
            xbd0_out(0, 1)
            kbd_out(0, 1)

            def chunk_step(n):
                tap(n + 1, 0)
                tap(n + 1, 1)
                silu(n + 1, 0)
                tap(n + 1, 2)
                u_out(n)
                silu(n + 1, 1)
                square(n + 1, 0)
                square(n + 1, 1)
                tap(n + 1, 3)
                silu(n + 1, 2)
                silu(n + 1, 3)
                square(n + 1, 2)
                square(n + 1, 3)
                o_square(n)
                kbd_out(n + 1, 0)
                mbd_out(n + 1, 0)
                oT_out(n)
                xbd0_out(n + 1, 0)
                mbd_out(n + 1, 1)
                xbd0_out(n + 1, 1)
                xf_out(n)
                k_relu(n)
                kbd_out(n + 1, 1)
                k_square(n)
                r_tanh(n)
                state_out(n)

            chunk_step(0)
            with act.Fori(1, N - 1) as n:
                chunk_step(n)
            n = N - 1
            u_out(n)
            o_square(n)
            oT_out(n)
            xf_out(n)
            k_relu(n)
            k_square(n)
            r_tanh(n)
            state_out(n)

        @block.vector
        def _(dve):
            dve.wait_ge(s["weights_in"], 16 * N_W)
            dve.wait_ge(s["consts_in"], 16)

            def a_row_stats(b):
                dve.wait_ge(s["xa_in"], b * 16 + 16)
                dve.wait_ge(s["a_normed"], b * 8)
                for m in range(M_TILES):
                    last = nc.vector.bn_stats(stats_a[:, m, :], xa[:, m, :])
                last.then_inc(s["a_stats"], 1)
                dve.wait_ge(s["a_stats"], b * 3 + 1)
                alone(dve)
                for m in range(M_TILES):
                    last = nc.vector.bn_aggr(mv_a[:, m, :], stats_a[:, m, :])
                last.then_inc(s["a_stats"], 1)
                dve.wait_ge(s["a_stats"], b * 3 + 2)
                nc.vector.tensor_scalar(ve_a[:, :].rearrange("p (m o) -> p m o", o=1), mv_a[:, :, 1:2], EPS, None,
                                        ALU.add).then_inc(s["a_stats"], 1)

            def a_norm(b):
                dve.wait_ge(s["a_rs"], b * 1 + 1)
                dve.wait_ge(s["a_xT"], b * 4)
                for m in range(M_TILES):
                    nc.vector.tensor_scalar(xna[:, m, :], xa[:, m, :], mv_a[:, m, 0:1], rs_a[:, m:m + 1],
                                            ALU.subtract, ALU.mult).then_inc(s["a_normed"], 1)

            def a_conv(b, q):
                for j in range(PAD):
                    for i in range(2):
                        if j == 0:
                            dve.wait_ge(s["a_tap"], b * 8 + 2 * q + i + 1)
                        else:
                            dve.wait_ge(s["a_conv"], b * 24 + 6 * q + 2 * (j - 1) + i + 1)
                        nc.vector.scalar_tensor_tensor(cva[:, i, :], bank[2 + i][:, j:j + 256],
                                                       conv_w[:, 2, i, j:j + 1], cva[:, i, :],
                                                       ALU.mult, ALU.add).then_inc(s["a_conv"], 1)

            def a_gates(b):
                dve.wait_ge(s["a_gate"], b * 1 + 1)
                dst = gates.rearrange("p g r (b m two) -> p b g r m two", b=B, two=2)
                for par in range(2):
                    src = bank[6][HH[par], 0:M_TILES * H * NG].rearrange("p (m h g) -> p h g m", h=H, g=NG)
                    for hh in range(2):
                        for pr in range(PAIRS):
                            nc.vector.tensor_copy(dst[HH[hh], b, :, pr, :, par], src[:, 2 * pr + hh]).then_inc(s["a_gate_out"], 1)

            def sequence(b, more):
                for q in range(4):
                    a_conv(b, q)
                    if more and q == 2:
                        a_row_stats(b + 1)
                    if more and q == 3:
                        a_norm(b + 1)
                a_gates(b)

            a_row_stats(0)
            a_norm(0)
            sequence(0, True)
            with dve.Fori(1, B - 1) as b:
                sequence(b, True)
            sequence(B - 1, False)

            steps = [0]

            def then(ins):
                steps[0] += 1
                ins.then_inc(s["g_step"], 1)
                dve.wait_ge(s["g_step"], steps[0])

            mixing = gates[:, 0:5]
            mx4 = gmax[:, :, :].rearrange("p r (w o) -> p o r w", o=1).broadcast_to((P, 5, PAIRS, BLK))
            dve.wait_ge(s["a_gate_out"], 8 * B)
            dve.wait_ge(s["g_exp"], 1)
            then(nc.vector.tensor_scalar(mix_eps[:, :], mix_eps[:, :], 0.0, 0.2, ALU.max, ALU.min))
            then(nc.vector.tensor_scalar(mix_scale[:, :], mix_eps[:, :], -5.0, 1.0, ALU.mult, ALU.add))
            for g in range(5):
                for pr in range(PAIRS):
                    last = nc.vector.tensor_scalar(gates[:, g, pr, :], gates[:, g, pr, :], gb[:, pr, g:g + 1],
                                                   inv_temp[:, pr:pr + 1], ALU.add, ALU.mult)
            then(last)
            then(nc.vector.tensor_reduce(gmax[:, :, :], mixing.rearrange("p g r w -> p r w g"), AX, ALU.max))
            then(nc.vector.tensor_tensor(mixing, mixing, mx4, ALU.subtract))
            assert steps[0] == G_SHIFTED
            dve.wait_ge(s["g_exp"], 3)
            then(nc.vector.tensor_reduce(gmax[:, :, :], mixing.rearrange("p g r w -> p r w g"), AX, ALU.add))
            then(nc.vector.reciprocal(gmax[:, :, :], gmax[:, :, :]))
            for pr in range(PAIRS):
                last = nc.vector.tensor_scalar(gmax[:, pr, :], gmax[:, pr, :], mix_scale[:, pr:pr + 1], None, ALU.mult)
            then(last)
            then(nc.vector.tensor_tensor(mixing, mixing, mx4, ALU.mult))
            for pr in range(PAIRS):
                last = nc.vector.tensor_scalar(mixing[:, :, pr, :], mixing[:, :, pr, :], mix_eps[:, pr:pr + 1], None, ALU.add)
            then(last)
            then(nc.vector.tensor_scalar(gates[:, 5], gates[:, 5], 0.5, 0.5, ALU.mult, ALU.add))
            assert steps[0] == G_STEPS

            dve.wait_ge(s["bd_zero"], 1)
            for g in range(FG):
                for f in range(3):
                    wt = gates[:, 2 - f, g // 2, :].rearrange("p (o w) -> p o w", o=1).broadcast_to((P, 8, BLK))
                    for j in range(4):
                        k = 12 * g + 4 * f + j
                        q = 8 * g + 4 * (f - 1) + j
                        dve.wait_ge(s["fir_mm"], k + 1)
                        if f == 0:
                            dst = fir[:, 32 * (g % 2) + 8 * j:32 * (g % 2) + 8 * j + 8, g // 2, :]
                        else:
                            dst = fprod[:, q % 2, :].rearrange("p (c w) -> p c w", w=BLK)
                            if q >= 2:
                                dve.wait_ge(s["fir_sum"], q - 1)
                        nc.vector.tensor_tensor(dst, bank[k % 8][:, :].rearrange("p (c w) -> p c w", w=BLK), wt,
                                                ALU.mult).then_inc(s["fir_prod"], 1)

            dve.wait_ge(s["fir_mm"], 12 * FG)
            dve.wait_ge(s["bd_zero"], 1)
            dve.wait_ge(s["pad_zero"], 2)

            def changed(ap, l):
                size = LEVELS[l]
                if size == C // 2:
                    return ap[:, :, size:]
                return ap.rearrange("p u (k two s) -> p u k two s", two=2, s=size)[:, :, :, 1]

            def over(ap, u=G4):
                return ap.rearrange("p (o k) -> p o k", o=1).broadcast_to((ap.shape[0], u, C))

            def per_row(ap, g=None):
                v = ap.rearrange("p a (u o) -> p (a u) o", o=1)
                return v.broadcast_to((P, U, C)) if g is None else v[:, grp(g)].broadcast_to((P, G4, C))

            def conv(n, t):
                ps = bank[t % 2][:, 0:B * (C + PAD)].rearrange("p (b t) -> p b t", b=B)
                for j in range(PAD):
                    if j == 0:
                        dve.wait_ge(s["tap"], n * 4 + t + 1)
                    else:
                        dve.wait_ge(s["conv"], n * 12 + 3 * t + j)
                    nc.vector.scalar_tensor_tensor(cv[:, t], ps[:, :, j:j + C], conv_w[:, 1 - t // 2, t % 2, j:j + 1],
                                                   cv[:, t], ALU.mult, ALU.add).then_inc(s["conv"], 1)

            def sumsq_out(n):
                dve.wait_ge(s["sumsq"], n * 1 + 1)
                dve.wait_ge(s["both_mm"], n * 1)
                nc.vector.tensor_scalar(ss64.rearrange("p (a h) -> p a h", h=2),
                                        bank[1][0:C, :].rearrange("p (a w) -> p a w", w=32)[:, :, 0:2], L2EPS, None, ALU.add).then_inc(s["ss64"], 1)

            def norms_in(n):
                dve.wait_ge(s["both_mm"], n * 1 + 1)
                dve.wait_ge(s["norms"], n * 2)
                dve.wait_ge(s["rate"], n * 2)
                src = bank[1][:, 0:4 * U].rearrange("p (a u h) -> p a u h", a=2, h=2)
                for hh in range(2):
                    nc.vector.tensor_copy(ssel[HH[hh]].rearrange("p a (u o) -> p a u o", o=1),
                                          src[HH[hh], :, :, hh:hh + 1]).then_inc(s["ssel"], 1)

            def k_rate(n):
                dve.wait_ge(s["ssel"], n * 2 + 2)
                nc.vector.reciprocal(rr[:, 0], ssel[:, 0]).then_inc(s["rate"], 1)
                beta = gates[:, 5, :, :].rearrange("p r (b n) -> p (r b) n", n=N)[:, :, bass.ds(n, 1)]
                dve.wait_ge(s["rate"], n * 2 + 1)
                dve.wait_ge(s["zbd"], n * 4)
                nc.vector.tensor_tensor(d2.rearrange("p a (u o) -> p (a u) o", o=1), beta,
                                        rr.rearrange("p a (u o) -> p (a u) o", o=1), ALU.mult).then_inc(s["rate"], 1)

            def m_lower(n, g):
                dve.wait_ge(s["gram"], n * 2 + g + 1)
                dve.wait_ge(s["mc"], n * 2)
                nc.vector.tensor_tensor(Mt[:, grp(g)], units(bank[2 + g][:, :], P)[:, :, 0:C], over(low),
                                        ALU.mult).then_inc(s["mt"], 1)

            def m_scaled(n, g):
                dve.wait_ge(s["mt"], n * 2 + g + 1)
                dve.wait_ge(s["rate"], n * 2 + 2)
                dve.wait_ge(s["x2"], n * 4)
                dve.wait_ge(s["mbd"], n * 4)
                nc.vector.tensor_tensor(Mc[:, grp(g)], Mt[:, grp(g)], per_row(d2, g), ALU.mult).then_inc(s["mc"], 1)

            def x_first(n, g):
                dve.wait_ge(s["mc"], n * 2 + g + 1)
                dve.wait_ge(s["z"], n * 12)
                dve.wait_ge(s["xbd0"], n * 4)
                nc.vector.tensor_tensor(X2[:, grp(g)], Mc[:, grp(g)], over(negpairs), ALU.mult).then_inc(s["x2"], 1)
                dve.wait_ge(s["x2"], n * 4 + 2 * g + 1)
                nc.vector.tensor_tensor(X2[:, grp(g)], X2[:, grp(g)], over(rstack), ALU.add).then_inc(s["x2"], 1)
                dve.wait_ge(s["x2"], n * 4 + 2 * g + 2)
                dve.wait_ge(s["zbd"], n * 4)
                nc.vector.transpose(Z[:, padded(g)], X2[:, grp(g)]).then_inc(s["z"], 1)

            def at_parts(n, g):
                dve.wait_ge(s["gram"], n * 2 + g + 1)
                dve.wait_ge(s["omm"], n * 1)
                for hh in range(2):
                    nc.vector.tensor_tensor(atT_bd[HH[hh], grp(g), HH[hh]], units(bank[2 + g][HH[hh], :], P)[:, :, C:P],
                                            over(up[HH[hh]]), ALU.mult).then_inc(s["at"], 1)

            def p_masked(n, l, g):
                dve.wait_ge(s["mm1"], n * 2 * NL + 2 * l + g + 1)
                for q in UPPER if l == NL - 1 else (slice(0, P),):
                    last = nc.vector.tensor_tensor(changed(Pm[q, padded(g)], l),
                                                   changed(units(bank[2 + g][q, :], P)[:, :, 0:C], l),
                                                   changed(over(level_mask(l)[q]), l), ALU.mult)
                last.then_inc(s["pm"], 1)

            def z_next(n, l, g):
                dve.wait_ge(s["mm2"], n * 2 * NL + 2 * l + g + 1)
                for q in UPPER if l == NL - 1 else (slice(0, P),):
                    last = nc.vector.tensor_tensor(changed(Z[q, padded(g)], l), changed(Z[q, padded(g)], l),
                                                   changed(units(bank[2 + g][q, :], P)[:, :, 0:C], l), ALU.subtract)
                last.then_inc(s["z"], 1)

            def x_next(n, l, g):
                dve.wait_ge(s["z"], n * 12 + 2 * (l + 1) + g + 1)
                for hh in range(2):
                    nc.vector.transpose(X_bd[HH[hh], grp(g), HH[hh]], Z[HH[hh], padded(g)]).then_inc(s["xbd"], 1)

            def z_scaled(n, g):
                dve.wait_ge(s["z"], n * 12 + 10 + g + 1)
                dve.wait_ge(s["umm"], n * 1)
                for hh in range(2):
                    nc.vector.tensor_tensor(Z_bd[HH[hh], grp(g), HH[hh]], Z[HH[hh], padded(g)], per_row(d2, g)[HH[hh]],
                                            ALU.mult).then_inc(s["zbd"], 1)

            def rest_in(n):
                dve.wait_ge(s["ks_mm"], n * 1 + 1)
                dve.wait_ge(s["vp"], n * 1 + 1)
                dve.wait_ge(s["umm"], n * 1)
                nc.vector.tensor_tensor(rest, vp, units(bank[4][:, :]), ALU.subtract).then_inc(s["rest"], 1)

            def o_scaled(n):
                dve.wait_ge(s["omm"], n * 1 + 1)
                dve.wait_ge(s["norms"], n * 2 + 2)
                dve.wait_ge(s["o2"], n * 1)
                nc.vector.tensor_tensor(o1, units(bank[5][:, :]), per_row(qs), ALU.mult).then_inc(s["o1"], 1)

            def o_summed(n):
                dve.wait_ge(s["o1"], n * 1 + 1)
                dve.wait_ge(s["ov"], n * 2 + 2)
                dve.wait_ge(s["obd"], n * 2)
                nc.vector.tensor_tensor(o2, o1, ov, ALU.add).then_inc(s["o2"], 1)

            def o_meansq(n):
                dve.wait_ge(s["osq"], n * 1 + 1)
                nc.vector.tensor_reduce(oms[:, 0], osq, AX, ALU.add).then_inc(s["oms"], 1)
                dve.wait_ge(s["oms"], n * 2 + 1)
                nc.vector.tensor_scalar(oms[:, 0], oms[:, 0], 1.0 / DK, EPS, ALU.mult, ALU.add).then_inc(s["oms"], 1)

            def o_normed(n):
                dve.wait_ge(s["ro"], n * 1 + 1)
                for hh in range(2):
                    nc.vector.tensor_tensor(o_bd[HH[hh], :, HH[hh]], o2[HH[hh]], per_row(ro)[HH[hh]], ALU.mult).then_inc(s["obd"], 1)

            def row_stats(n, i, name, src, eps, normed):
                dve.wait_ge(s[normed], n * 1)
                dve.wait_ge(s[name], n * 3)
                for j in range(2):
                    last = nc.vector.bn_stats(bn[:, i, j, :], src[:, j, :])
                last.then_inc(s[name], 1)
                dve.wait_ge(s[name], n * 3 + 1)
                alone(dve)
                for j in range(2):
                    last = nc.vector.bn_aggr(mv[:, i, j, :], bn[:, i, j, :])
                last.then_inc(s[name], 1)
                dve.wait_ge(s[name], n * 3 + 2)
                nc.vector.tensor_scalar(ve[:, i].rearrange("p (j o) -> p j o", o=1), mv[:, i, :, 1:2], eps, None,
                                        ALU.add).then_inc(s[name], 1)

            def row_norm(n, i, dst, src, name):
                for j in range(2):
                    last = nc.vector.tensor_scalar(dst[:, j, :], src[:, j, :], mv[:, i, j, 0:1], rs[:, i, j:j + 1],
                                                   ALU.subtract, ALU.mult)
                last.then_inc(s[name], 1)

            def y_stats(n):
                dve.wait_ge(s["ymm"], n * 1 + 1)
                row_stats(n, 0, "st1", bank[5][:, :].rearrange("p (j c) -> p j c", j=2), EPS, "t1")

            def residual(n):
                dve.wait_ge(s["r1"], n * 1 + 1)
                dve.wait_ge(s["x1"], n * 1)
                row_norm(n, 0, t1, bank[5][:, :].rearrange("p (j c) -> p j c", j=2), "t1")
                dve.wait_ge(s["t1"], n * 1 + 1)
                dve.wait_ge(s["x_in"], n * 64 + 64)
                dve.wait_ge(s["y_out"], n * 1)
                nc.vector.tensor_tensor(x1, t1, x_in, ALU.add).then_inc(s["x1"], 1)

            def x_stats(n):
                dve.wait_ge(s["x1"], n * 1 + 1)
                row_stats(n, 1, "st2", x1, EPS, "xn2")

            def x_normed(n):
                dve.wait_ge(s["r2"], n * 1 + 1)
                row_norm(n, 1, xn2, x1, "xn2")

            def shifted(n):
                dve.wait_ge(s["xf"], n * 2 + 2)
                dve.wait_ge(s["mix"], n * 4)
                for hf in range(HALVES):
                    nc.vector.tensor_tensor(dx[:, hf].rearrange("p (b t) -> p b t", b=B), xf[:, hf, :, 1:],
                                            xf[:, hf, :, 0:C], ALU.subtract).then_inc(s["dx"], 1)

            def mix(n, i, dst):
                dve.wait_ge(s["dx"], n * 2 + 2)
                dve.wait_ge(s["kmm"], n * 1)
                dve.wait_ge(s["rmm"], n * 1)
                for hf in range(HALVES):
                    nc.vector.scalar_tensor_tensor(dst[:, hf].rearrange("p (b t) -> p b t", b=B),
                                                   dx[:, hf].rearrange("p (b t) -> p b t", b=B), mu[:, i, hf:hf + 1],
                                                   xf[:, hf, :, 0:C], ALU.mult, ALU.add).then_inc(s["mix"], 1)

            def ffn_out(n):
                dve.wait_ge(s["vmm"], n * 1 + 1)
                dve.wait_ge(s["th"], n * 1 + 1)
                dve.wait_ge(s["t3"], n * 1)
                nc.vector.scalar_tensor_tensor(f2, th, 1.0, bank[6][:, :].rearrange("p (j c) -> p j c", j=2),
                                               ALU.add, ALU.mult).then_inc(s["f2"], 1)

            def f_stats(n):
                dve.wait_ge(s["f2"], n * 1 + 1)
                row_stats(n, 2, "st3", f2, 4 * EPS, "t3")

            def f_normed(n):
                dve.wait_ge(s["r3"], n * 1 + 1)
                dve.wait_ge(s["y_out"], n * 1)
                row_norm(n, 2, t3, f2, "t3")

            conv(0, 0)
            conv(0, 1)
            conv(0, 2)
            conv(0, 3)
            at_parts(0, 0)
            sumsq_out(0)
            m_lower(0, 0)
            norms_in(0)
            k_rate(0)
            m_scaled(0, 0)
            x_first(0, 0)
            at_parts(0, 1)
            m_lower(0, 1)
            m_scaled(0, 1)
            p_masked(0, 0, 0)
            x_first(0, 1)
            z_next(0, 0, 0)
            p_masked(0, 0, 1)
            x_next(0, 0, 0)
            p_masked(0, 1, 0)
            z_next(0, 0, 1)
            z_next(0, 1, 0)
            x_next(0, 0, 1)
            p_masked(0, 1, 1)
            z_next(0, 1, 1)
            x_next(0, 1, 0)
            p_masked(0, 2, 0)
            x_next(0, 1, 1)
            z_next(0, 2, 0)
            p_masked(0, 2, 1)
            x_next(0, 2, 0)
            p_masked(0, 3, 0)
            z_next(0, 2, 1)
            x_next(0, 2, 1)
            p_masked(0, 3, 1)
            z_next(0, 3, 0)
            x_next(0, 3, 0)
            p_masked(0, 4, 0)
            z_next(0, 3, 1)
            x_next(0, 3, 1)
            z_next(0, 4, 0)
            p_masked(0, 4, 1)
            z_scaled(0, 0)
            z_next(0, 4, 1)
            z_scaled(0, 1)

            def chunk_step(n):
                rest_in(n)
                conv(n + 1, 0)
                conv(n + 1, 1)
                conv(n + 1, 2)
                conv(n + 1, 3)
                o_scaled(n)
                o_summed(n)
                o_meansq(n)
                at_parts(n + 1, 0)
                sumsq_out(n + 1)
                m_lower(n + 1, 0)
                norms_in(n + 1)
                k_rate(n + 1)
                o_normed(n)
                m_scaled(n + 1, 0)
                x_first(n + 1, 0)
                at_parts(n + 1, 1)
                m_lower(n + 1, 1)
                m_scaled(n + 1, 1)
                p_masked(n + 1, 0, 0)
                x_first(n + 1, 1)
                y_stats(n)
                z_next(n + 1, 0, 0)
                p_masked(n + 1, 0, 1)
                x_next(n + 1, 0, 0)
                p_masked(n + 1, 1, 0)
                residual(n)
                z_next(n + 1, 0, 1)
                z_next(n + 1, 1, 0)
                x_next(n + 1, 0, 1)
                p_masked(n + 1, 1, 1)
                x_stats(n)
                z_next(n + 1, 1, 1)
                x_next(n + 1, 1, 0)
                p_masked(n + 1, 2, 0)
                x_normed(n)
                x_next(n + 1, 1, 1)
                z_next(n + 1, 2, 0)
                p_masked(n + 1, 2, 1)
                x_next(n + 1, 2, 0)
                p_masked(n + 1, 3, 0)
                shifted(n)
                z_next(n + 1, 2, 1)
                mix(n, 1, xk)
                x_next(n + 1, 2, 1)
                p_masked(n + 1, 3, 1)
                z_next(n + 1, 3, 0)
                mix(n, 0, xr)
                x_next(n + 1, 3, 0)
                p_masked(n + 1, 4, 0)
                z_next(n + 1, 3, 1)
                x_next(n + 1, 3, 1)
                ffn_out(n)
                z_next(n + 1, 4, 0)
                p_masked(n + 1, 4, 1)
                f_stats(n)
                z_scaled(n + 1, 0)
                z_next(n + 1, 4, 1)
                f_normed(n)
                z_scaled(n + 1, 1)

            chunk_step(0)
            with dve.Fori(1, N - 1) as n:
                chunk_step(n)
            n = N - 1
            rest_in(n)
            o_scaled(n)
            o_summed(n)
            o_meansq(n)
            o_normed(n)
            y_stats(n)
            residual(n)
            x_stats(n)
            x_normed(n)
            shifted(n)
            mix(n, 1, xk)
            mix(n, 0, xr)
            ffn_out(n)
            f_stats(n)
            f_normed(n)

        @block.tensor
        def _(pe):
            mm = nc.tensor.matmul
            pe.wait_ge(s["consts_in"], 16)
            pe.wait_ge(s["weights_in"], 16 * N_W)

            def a_xT(b, q):
                pe.wait_ge(s["a_normed"], b * 8 + 2 * q + 2)
                pe.wait_ge(s["a_xT_out"], b * 4 + (q - 1 if q >= 1 else 0))
                for hf in range(HALVES):
                    for k in range(2):
                        last = nc.tensor.transpose(bank[q % 2][:, 256 * hf + P * k:256 * hf + P * k + P],
                                                   xna[:, 2 * q + k, P * hf:P * hf + P], ident)
                last.then_inc(s["a_xT"], 1)

            def a_proj(b, q):
                pe.wait_ge(s["a_xT_out"], b * 4 + q + 1)
                for oh in range(2):
                    i = 2 * q + oh
                    pe.wait_ge(s["a_conv"], b * 24 + (6 * (q - 1) + 5 + oh if i >= 2 else 0))
                    for kh in range(HALVES):
                        last = mm(bank[2 + oh][:, 0:PAD + 256], w["v"][:, kh, P * oh:P * oh + P],
                                  xnT[:, kh, 256 * q:256 * q + 256 + PAD], start=(kh == 0), stop=(kh == 1))
                    last.then_inc(s["a_proj"], 1)

            def a_win(b, i):
                q, pr = i // 2, i % 2
                pe.wait_ge(s["a_vT"], b * 8 + i + 1)
                pe.wait_ge(s["a_win_out"], b * 8 + (i - 1 if i >= 2 else 0))
                pe.wait_ge(s["a_vb"], b * 16 + (2 * (i - 1) if i >= 2 else 0))
                for k in range(4):
                    at_ = C * (4 * q + k)
                    last = nc.tensor.transpose(bank[4 + pr][:, P * k:P * k + P], vT[:, pr, at_:at_ + P], ident)
                last.then_inc(s["a_win"], 1)

            def a_gate(b):
                pe.wait_ge(s["a_gate_out"], b * 8)
                for m in range(M_TILES):
                    for kh in range(HALVES):
                        last = mm(bank[6][:, H * NG * m:H * NG * (m + 1)], xnT[:, kh, PAD + P * m:PAD + P * m + P],
                                  w_gate[:, kh, :], start=(kh == 0), stop=(kh == 1))
                last.then_inc(s["a_gate"], 1)

            def sequence(b):
                a_xT(b, 0)
                a_xT(b, 1)
                a_proj(b, 0)
                a_xT(b, 2)
                a_proj(b, 1)
                a_win(b, 0)
                a_win(b, 1)
                a_xT(b, 3)
                a_proj(b, 2)
                a_win(b, 2)
                a_win(b, 3)
                a_proj(b, 3)
                a_win(b, 4)
                a_win(b, 5)
                a_gate(b)
                a_win(b, 6)
                a_win(b, 7)

            sequence(0)
            with pe.Fori(1, B) as b:
                sequence(b)

            pe.wait_ge(s["a_win_out"], 8 * B)
            pe.wait_ge(s["a_gate_out"], 8 * B)
            pe.wait_ge(s["a_conv"], 24 * B)
            pe.wait_ge(s["a_vb"], 16 * B)
            for g in range(FG):
                for f in range(3):
                    if f == 0:
                        pe.wait_ge(s["toep_l_in"], 16 * (g + 1))
                    elif f == 1:
                        pe.wait_ge(s["toep_ms_in"], 32 * (g + 1))
                    toep = toep_l if f == 0 else toep_ms[:, f - 1]
                    for j in range(4):
                        k = 12 * g + 4 * f + j
                        if k >= 8:
                            pe.wait_ge(s["fir_prod"], k - 7)
                        for hh in range(2):
                            for d in range(8):
                                c = P * (g // 2) + 64 * hh + 32 * (g % 2) + 8 * j + d
                                last = mm(bank[k % 8][HH[hh], BLK * d:BLK * d + BLK],
                                          toep[:, :, 32 * hh + 8 * j + d], vwin[:, c, :], start=True, stop=True)
                        last.then_inc(s["fir_mm"], 1)

            pe.wait_ge(s["fir_prod"], 12 * FG)
            pe.wait_ge(s["state_zero"], 1)
            for hf in range(HALVES):
                mm(bank[7][:, 256 * hf:256 * hf + 256], ident, xf[:, 0, 0:B, 0:C], start=True, stop=True)

            def proj(n, kind, g):
                if kind == 0:
                    pe.wait_ge(s["window_in"], n * 32 + 32)
                    pe.wait_ge(s["kbd"], n * 2)
                else:
                    pe.wait_ge(s["conv"], n * 12 + 3 * g + 3)
                for kh in range(HALVES):
                    last = mm(bank[g][:, 0:B * (C + PAD)], w["kq"[kind]][:, kh, P * g:P * g + P],
                              xwin[:, kh], start=(kh == 0), stop=(kh == 1))
                last.then_inc(s["proj"], 1)

            def sumsq(n):
                pe.wait_ge(s["square"], n * 4 + 4)
                pe.wait_ge(s["conv"], n * 12 + 12)
                for a in range(2 * U):
                    last = mm(bank[1][0:C, 32 * a:32 * a + 32], sq[:, a], headsel, start=True, stop=True)
                last.then_inc(s["sumsq"], 1)

            def sums_twice(n):
                pe.wait_ge(s["ss64"], n * 1 + 1)
                mm(bank[1][:, 0:4 * U], twice[0:C, :], ss64, start=True, stop=True).then_inc(s["both_mm"], 1)

            def k_turn(n, g):
                pe.wait_ge(s["bd"], n * 8 + 2 * g + 2)
                pe.wait_ge(s["conv"], n * 12 + 3 * (2 + g) + 3)
                pe.wait_ge(s["ssel"], n * 2 + 2)
                for u in range(G4):
                    last = nc.tensor.transpose(bank[g][:, P * u:P * u + P], kT_bd[:, G4 * g + u, :], ident)
                last.then_inc(s["ktr"], 1)

            def gram(n, g):
                pe.wait_ge(s["silu"], n * 4 + 4)
                pe.wait_ge(s["z"], n * 12)
                for u in range(G4):
                    last = mm(bank[2 + g][:, P * u:P * u + P], kT_bd[:, G4 * g + u, :], kq[:, G4 * g + u],
                              start=True, stop=True)
                last.then_inc(s["gram"], 1)

            def mz(n, l, g):
                pe.wait_ge(s["z"], n * 12 + 2 * l + g + 1)
                if l == 0:
                    pe.wait_ge(s["mbd"], n * 4 + 2 * g + 2)
                    pe.wait_ge(s["mt"], n * 2 + g + 1)
                    pe.wait_ge(s["at"], n * 4 + 2 * g + 2)
                for u in range(G4):
                    if l == NL - 1:
                        for q in UPPER:
                            last = mm(bank[2 + g][q, P * u + 32:P * u + C], M_bd[:, G4 * g + u, q],
                                      Z[:, G5 * g + u, 32:C], start=True, stop=True)
                    else:
                        last = mm(bank[2 + g][:, P * u:P * u + P], M_bd[:, G4 * g + u, :],
                                  Z[:, G5 * g + u:G5 * g + u + 2, :], start=True, stop=True)
                last.then_inc(s["mm1"], 1)

            def zp(n, l, g):
                pe.wait_ge(s["pm"], n * 2 * NL + 2 * l + g + 1)
                if l == 0:
                    pe.wait_ge(s["xbd0"], n * 4 + 2 * g + 2)
                else:
                    pe.wait_ge(s["xbd"], n * 4 * (NL - 1) + 4 * (l - 1) + 2 * g + 2)
                for u in range(G4):
                    if l == NL - 1:
                        for q in UPPER:
                            last = mm(bank[2 + g][q, P * u + 32:P * u + C], X_bd[:, G4 * g + u, q],
                                      Pm[:, G5 * g + u, 32:C], start=True, stop=True)
                    else:
                        last = mm(bank[2 + g][:, P * u:P * u + P], X_bd[:, G4 * g + u, :],
                                  Pm[:, G5 * g + u:G5 * g + u + 2, :], start=True, stop=True)
                last.then_inc(s["mm2"], 1)

            def scan_k(n):
                pe.wait_ge(s["S"], n * 1 + 1)
                pe.wait_ge(s["bd"], n * 8 + 4)
                pe.wait_ge(s["xf"], n * 2)
                for u in range(U):
                    last = mm(bank[4][:, C * u:C * u + C], kT_bd[:, u, :], S[:, u, :], start=True, stop=True)
                last.then_inc(s["ks_mm"], 1)

            def scan_u(n):
                pe.wait_ge(s["zbd"], n * 4 + 4)
                pe.wait_ge(s["rest"], n * 1 + 1)
                for u in range(U):
                    last = mm(bank[4][:, C * u:C * u + C], Z_bd[:, u, :], rest[:, u, :], start=True, stop=True)
                last.then_inc(s["umm"], 1)

            def scan_state(n):
                pe.wait_ge(s["ut"], n * 1 + 1)
                pe.wait_ge(s["kbd"], n * 2 + 2)
                for u in range(U):
                    last = mm(bank[7][:, C * u:C * u + C], k_bd[:, u, :], ut[:, u, :], start=False, stop=False,
                              skip_group_check=True)
                last.then_inc(s["state"], 1)

            def scan_o(n):
                pe.wait_ge(s["bd"], n * 8 + 8)
                pe.wait_ge(s["at"], n * 4 + 4)
                pe.wait_ge(s["ut"], n * 1 + 1)
                pe.wait_ge(s["S"], n * 1 + 1)
                pe.wait_ge(s["rl"], n * 1)
                for u in range(U):
                    mm(bank[5][:, C * u:C * u + C], qT_bd[:, u, :], S[:, u, :], start=True, stop=False)
                    last = mm(bank[5][:, C * u:C * u + C], atT_bd[:, u, :], ut[:, u, :], start=False, stop=True)
                last.then_inc(s["omm"], 1)

            def o_turn(n):
                pe.wait_ge(s["obd"], n * 2 + 2)
                for u in range(U):
                    last = mm(bank[4][:, C * u:C * u + C], o_bd[:, u, :], rstack, start=True, stop=True)
                last.then_inc(s["oT_mm"], 1)

            def tokens(lhs, wt, dst, k_first=0):
                for j in range(2):
                    for kh in range(HALVES):
                        last = mm(dst[:, 256 * j:256 * j + 256], lhs[:, kh, P * j:P * j + P], wt[:, kh, :],
                                  start=(kh == 0), stop=(kh == 1))
                return last

            def y_rows(n):
                pe.wait_ge(s["oT"], n * 1 + 1)
                pe.wait_ge(s["o1"], n * 1 + 1)
                tokens(oT.rearrange("p (r b) t -> p r (b t)", r=PAIRS), w["o"], bank[5]).then_inc(s["ymm"], 1)

            def x_turn(n):
                pe.wait_ge(s["xn2"], n * 1 + 1)
                pe.wait_ge(s["oT"], n * 1 + 1)
                for hf in range(HALVES):
                    for j in range(2):
                        last = nc.tensor.transpose(bank[4][:, 256 * hf + P * j:256 * hf + P * j + P],
                                                   xn2[:, j, P * hf:P * hf + P], ident)
                last.then_inc(s["xT"], 1)

            def ffn_k(n):
                pe.wait_ge(s["mix"], n * 4 + 2)
                pe.wait_ge(s["t1"], n * 1 + 1)
                for oh in range(2):
                    for kh in range(HALVES):
                        last = mm(bank[5][:, 256 * oh:256 * oh + 256], w["fk"][:, kh, P * oh:P * oh + P], xk[:, kh, :],
                                  start=(kh == 0), stop=(kh == 1))
                last.then_inc(s["kmm"], 1)

            def ffn_r(n):
                pe.wait_ge(s["mix"], n * 4 + 4)
                pe.wait_ge(s["f2"], n * 1)
                tokens(xr, w["r"], bank[6]).then_inc(s["rmm"], 1)

            def ffn_v(n):
                pe.wait_ge(s["ka"], n * 1 + 1)
                pe.wait_ge(s["th"], n * 1 + 1)
                tokens(ka, w["fv"], bank[6]).then_inc(s["vmm"], 1)

            proj(0, 0, 0)
            proj(0, 0, 1)
            proj(0, 1, 0)
            proj(0, 1, 1)
            gram(0, 0)
            sumsq(0)
            sums_twice(0)
            k_turn(0, 0)
            gram(0, 1)
            mz(0, 0, 0)
            zp(0, 0, 0)
            mz(0, 0, 1)
            mz(0, 1, 0)
            zp(0, 0, 1)
            zp(0, 1, 0)
            mz(0, 1, 1)
            k_turn(0, 1)
            zp(0, 1, 1)
            mz(0, 2, 0)
            mz(0, 2, 1)
            zp(0, 2, 0)
            mz(0, 3, 0)
            zp(0, 2, 1)
            zp(0, 3, 0)
            mz(0, 3, 1)
            zp(0, 3, 1)
            mz(0, 4, 0)
            zp(0, 4, 0)
            mz(0, 4, 1)
            zp(0, 4, 1)

            def chunk_step(n):
                proj(n + 1, 0, 0)
                scan_k(n)
                proj(n + 1, 0, 1)
                scan_u(n)
                proj(n + 1, 1, 0)
                proj(n + 1, 1, 1)
                scan_o(n)
                scan_state(n)
                gram(n + 1, 0)
                sumsq(n + 1)
                sums_twice(n + 1)
                k_turn(n + 1, 0)
                gram(n + 1, 1)
                o_turn(n)
                mz(n + 1, 0, 0)
                y_rows(n)
                zp(n + 1, 0, 0)
                mz(n + 1, 0, 1)
                mz(n + 1, 1, 0)
                zp(n + 1, 0, 1)
                zp(n + 1, 1, 0)
                mz(n + 1, 1, 1)
                k_turn(n + 1, 1)
                zp(n + 1, 1, 1)
                mz(n + 1, 2, 0)
                mz(n + 1, 2, 1)
                zp(n + 1, 2, 0)
                x_turn(n)
                mz(n + 1, 3, 0)
                zp(n + 1, 2, 1)
                zp(n + 1, 3, 0)
                mz(n + 1, 3, 1)
                ffn_k(n)
                ffn_r(n)
                zp(n + 1, 3, 1)
                mz(n + 1, 4, 0)
                ffn_v(n)
                zp(n + 1, 4, 0)
                mz(n + 1, 4, 1)
                zp(n + 1, 4, 1)

            chunk_step(0)
            with pe.Fori(1, N - 1) as n:
                chunk_step(n)
            n = N - 1
            scan_k(n)
            scan_u(n)
            scan_o(n)
            scan_state(n)
            o_turn(n)
            y_rows(n)
            x_turn(n)
            ffn_k(n)
            ffn_r(n)
            ffn_v(n)


def constants():
    import numpy as np

    c = np.zeros((P, NCONST), np.float32)
    i = np.arange(P) % C
    j = np.arange(C)
    c[:, C_ID:C_ID + P] = np.eye(P)
    c[:, C_R:C_R + C] = i[:, None] == j[None, :]
    c[:, C_LOW:C_LOW + C] = i[:, None] > j[None, :]
    c[:, C_UP:C_UP + C] = i[:, None] <= j[None, :]
    c[:, C_NM1:C_NM1 + C] = -1.0 * ((i[:, None] // 2 == j[None, :] // 2) & (i[:, None] > j[None, :]))
    for l, size in enumerate(LEVELS):
        same = i[:, None] // (2 * size) == j[None, :] // (2 * size)
        c[:, C_LV + C * l:C_LV + C * (l + 1)] = same & (i[:, None] // size % 2 == 0) & (j[None, :] // size % 2 == 1)
    c[:, C_HS] = np.arange(P) < C
    c[:, C_HS + 1] = np.arange(P) >= C
    return c


def kernel(**inputs):
    import numpy as np
    import concourse.bacc as bacc
    from concourse.bass_utils import run_bass_kernel_spmd

    g = {k[3:]: np.asarray(v) for k, v in inputs.items()}
    order = np.arange(D).reshape(PAIRS, 2, 2, 32).transpose(0, 2, 1, 3).reshape(D)

    def padded(f):
        taps = f.reshape(D, -1)[order].T
        rows = np.zeros((ROWS, D), f.dtype)
        rows[P - taps.shape[0]:P] = taps
        return rows.reshape(ROWS, FG, GC).transpose(1, 0, 2)

    def per_head(v):
        return np.repeat(v.reshape(PAIRS, 2, -1).transpose(1, 0, 2).reshape(2, -1), C, axis=0)

    arrays = {
        "x": g["attn_hidden_states"],
        "wgate": np.concatenate([g["attn_gate_w"], g["attn_Wb"][:, None, :]], axis=1).reshape(H * NG, D).T,
        "consts": constants(),
        "wq": g["attn_Wq"].T, "wk": g["attn_Wk"].T, "wv": g["attn_Wv"].T, "wo": g["attn_Wo"].T,
        "wr": g["ffn_W_r"].T, "wfk": g["ffn_W_k"].T, "wfv": g["ffn_W_v"].T,
        "smalls": np.concatenate([
            *(g[k].reshape(HALVES, P, TAPS).transpose(1, 0, 2).reshape(P, -1) for k in ("attn_conv_q", "attn_conv_k", "attn_conv_v")),
            *(g[k].reshape(HALVES, P).T for k in ("ffn_mu_r", "ffn_mu_k")),
            np.tile(g["attn_norm_w"], 2)[:, None],
            *(per_head(g[k]) for k in ("attn_gate_b", "attn_log_temp", "attn_eps_param"))], axis=1),
        "fl": padded(g["attn_fir_l"]),
        "fms": np.stack([padded(g["attn_fir_m"]), padded(g["attn_fir_s"])]),
    }
    arrays = {k: np.ascontiguousarray(v) for k, v in arrays.items()}
    nc = bacc.Bacc("TRN2", target_bir_lowering=False, num_devices=1)
    a = {k: nc.dram_tensor(k, v.shape, F32, kind="ExternalInput").ap() for k, v in arrays.items()}
    out = nc.dram_tensor("out", (B, L, D), F32, kind="ExternalOutput").ap()
    build(nc, a["x"], out, *(a[k] for k in (
        "wgate", "consts", "smalls", "wq", "wk", "wv", "wo", "wr", "wfk", "wfv", "fl", "fms")))
    r = run_bass_kernel_spmd(nc, [arrays], core_ids=[0])
    return r.results[0]["out"]
```
